# Optimizing a Trainium2 kernel written in Bass

```python
import numpy as np
import jax
import jax.numpy as jnp

def _softmax(x, axis=-1):
    return jax.nn.softmax(x, axis=axis)

def _gelu(x):
    return jax.nn.gelu(x, approximate=True)

def _silu(x):
    return jax.nn.silu(x)

def _sigmoid(x):
    return jax.nn.sigmoid(x)

def _layernorm(x, axis=-1, eps=1e-05):
    m = jnp.mean(x, axis=axis, keepdims=True)
    v = jnp.var(x, axis=axis, keepdims=True)
    return (x - m) / jnp.sqrt(v + eps)

def _scatter_add(tgt, idx, src, axis=0):
    return tgt.at[idx].add(src)

def _segment_sum(src, seg, n):
    return jax.ops.segment_sum(src, seg, n)
kernel_name = 'mk_macaron_d1_jaxref_r8_427e64'

def setup_inputs(seed: int=0):
    np.random.seed(seed)
    _w = jnp.asarray

    def _L0_attn_setup():
        import jax, jax.numpy as jnp
        import numpy as np
        import math
        B, S, D = (4, 256, 128)
        H, DEG, DH, BUS, SLOTS = (8, 4, 32, 128, 64)
        EPS = 1.1920929e-07

        def _rms(x, w):
            return x * jax.lax.rsqrt(jnp.mean(x * x, axis=-1, keepdims=True) + EPS) * w
        key = jax.random.key(seed)
        ks = jax.random.split(key, 20)
        g = lambda k, shape, s=0.02: jax.random.normal(k, shape, jnp.float32) * s
        return {'x': jax.random.normal(ks[0], (B, S, D), jnp.float32), 'w_norm_in': jnp.ones((D,), jnp.float32), 'w_norm_out': jnp.ones((D,), jnp.float32), 'router_w1': g(ks[1], (D, D // 2)), 'router_w2': g(ks[2], (D // 2, 3)), 'router_b2': jnp.full((3,), 0.5, jnp.float32), 'ttt_w1': g(ks[3], (D, D // 4)), 'ttt_b1': jnp.zeros((D // 4,), jnp.float32), 'ttt_w2': g(ks[4], (D // 4, H * DEG)), 'ttt_b2': jnp.zeros((H * DEG,), jnp.float32), 'lambdas': jnp.array([0.9995, 0.9995, 0.997, 0.997, 0.995, 0.995, 0.97, 0.95], jnp.float32), 'slr_wq1': g(ks[5], (D, DH)), 'slr_wq2': g(ks[6], (D, DH)), 'slr_wk1': g(ks[7], (D, DH)), 'slr_wk2': g(ks[8], (D, DH)), 'slr_wv': g(ks[9], (D, DH)), 'slr_wo': g(ks[10], (DH, D)), 'slr_lam': jnp.array(0.5, jnp.float32), 'landmarks': g(ks[11], (SLOTS, D), 0.5), 'mix_w': g(ks[12], (2 * D, D)), 'bus_compress': g(ks[13], (D, BUS)), 'bus_expand': g(ks[14], (BUS, D)), 'bus_publish': g(ks[15], (BUS, BUS))}
    _L0_attn_in = _L0_attn_setup()

    def _L0_ffn_setup():
        import jax, jax.numpy as jnp
        import numpy as np
        B, L, D, E, K, DFF = (2, 256, 128, 8, 2, 512)
        key = jax.random.key(seed)
        kx, kr, kg, ku, kd = jax.random.split(key, 5)
        scale = 0.02
        return {'x': jax.random.normal(kx, (B, L, D), dtype=jnp.float32), 'Wr': jax.random.normal(kr, (E, D), dtype=jnp.float32) * scale, 'Wg': jax.random.normal(kg, (E, DFF, D), dtype=jnp.float32) * scale, 'Wu': jax.random.normal(ku, (E, DFF, D), dtype=jnp.float32) * scale, 'Wd': jax.random.normal(kd, (E, D, DFF), dtype=jnp.float32) * scale}
    _L0_ffn_in = _L0_ffn_setup()
    _d = {'L0_attn_x': _L0_attn_in['x'], 'L0_attn_w_norm_in': _L0_attn_in['w_norm_in'], 'L0_attn_w_norm_out': _L0_attn_in['w_norm_out'], 'L0_attn_router_w1': _L0_attn_in['router_w1'], 'L0_attn_router_w2': _L0_attn_in['router_w2'], 'L0_attn_router_b2': _L0_attn_in['router_b2'], 'L0_attn_ttt_w1': _L0_attn_in['ttt_w1'], 'L0_attn_ttt_b1': _L0_attn_in['ttt_b1'], 'L0_attn_ttt_w2': _L0_attn_in['ttt_w2'], 'L0_attn_ttt_b2': _L0_attn_in['ttt_b2'], 'L0_attn_lambdas': _L0_attn_in['lambdas'], 'L0_attn_slr_wq1': _L0_attn_in['slr_wq1'], 'L0_attn_slr_wq2': _L0_attn_in['slr_wq2'], 'L0_attn_slr_wk1': _L0_attn_in['slr_wk1'], 'L0_attn_slr_wk2': _L0_attn_in['slr_wk2'], 'L0_attn_slr_wv': _L0_attn_in['slr_wv'], 'L0_attn_slr_wo': _L0_attn_in['slr_wo'], 'L0_attn_slr_lam': _L0_attn_in['slr_lam'], 'L0_attn_landmarks': _L0_attn_in['landmarks'], 'L0_attn_mix_w': _L0_attn_in['mix_w'], 'L0_attn_bus_compress': _L0_attn_in['bus_compress'], 'L0_attn_bus_expand': _L0_attn_in['bus_expand'], 'L0_attn_bus_publish': _L0_attn_in['bus_publish'], 'L0_ffn_Wr': _L0_ffn_in['Wr'], 'L0_ffn_Wg': _L0_ffn_in['Wg'], 'L0_ffn_Wu': _L0_ffn_in['Wu'], 'L0_ffn_Wd': _L0_ffn_in['Wd']}
    _x0 = _d['L0_attn_x']
    _d['L0_attn_x'] = jax.random.normal(jax.random.fold_in(jax.random.key(seed), 1), (8, 1024, 128), dtype=_x0.dtype)
    del _x0
    return _d

def reference(L0_attn_x, L0_attn_w_norm_in, L0_attn_w_norm_out, L0_attn_router_w1, L0_attn_router_w2, L0_attn_router_b2, L0_attn_ttt_w1, L0_attn_ttt_b1, L0_attn_ttt_w2, L0_attn_ttt_b2, L0_attn_lambdas, L0_attn_slr_wq1, L0_attn_slr_wq2, L0_attn_slr_wk1, L0_attn_slr_wk2, L0_attn_slr_wv, L0_attn_slr_wo, L0_attn_slr_lam, L0_attn_landmarks, L0_attn_mix_w, L0_attn_bus_compress, L0_attn_bus_expand, L0_attn_bus_publish, L0_ffn_Wr, L0_ffn_Wg, L0_ffn_Wu, L0_ffn_Wd):

    def _L0_attn_ref(x, w_norm_in, w_norm_out, router_w1, router_w2, router_b2, ttt_w1, ttt_b1, ttt_w2, ttt_b2, lambdas, slr_wq1, slr_wq2, slr_wk1, slr_wk2, slr_wv, slr_wo, slr_lam, landmarks, mix_w, bus_compress, bus_expand, bus_publish):
        import jax, jax.numpy as jnp
        import numpy as np
        import math
        B, S, D = (4, 256, 128)
        H, DEG, DH, BUS, SLOTS = (8, 4, 32, 128, 64)
        EPS = 1.1920929e-07

        def _rms(x, w):
            return x * jax.lax.rsqrt(jnp.mean(x * x, axis=-1, keepdims=True) + EPS) * w
        b, s, d = x.shape
        hd = d // H
        residual = x
        xn = _rms(x, w_norm_in)
        route_in = xn.mean(axis=1)
        logits = jax.nn.silu(route_in @ router_w1) @ router_w2 + router_b2
        probs = jax.nn.softmax(logits, axis=-1)
        p_medium, p_full = (probs[:, 1], probs[:, 2])
        ttt = (jax.nn.silu(route_in @ ttt_w1 + ttt_b1) @ ttt_w2 + ttt_b2).reshape(b, H, DEG)
        ttt_scale = 0.1 * jnp.tanh(ttt)
        xh = xn.reshape(b, s, H, hd).transpose(1, 0, 2, 3)
        lam = lambdas[None, :, None]

        def ema_step(state, xt):
            state = lam * state + (1.0 - lam) * xt
            return (state, state)
        _, ys = jax.lax.scan(ema_step, jnp.zeros((b, H, hd), x.dtype), xh)
        ssm_out = ys.transpose(1, 0, 2, 3).reshape(b, s, d)
        q1, q2 = (xn @ slr_wq1, xn @ slr_wq2)
        k1, k2 = (xn @ slr_wk1, xn @ slr_wk2)
        v = xn @ slr_wv
        sc = 1.0 / math.sqrt(DH)
        a1 = jax.nn.softmax(jnp.einsum('bqd,bkd->bqk', q1, k1) * sc, axis=-1)
        a2 = jax.nn.softmax(jnp.einsum('bqd,bkd->bqk', q2, k2) * sc, axis=-1)
        ctx = jnp.einsum('bqk,bkd->bqd', a1 - slr_lam * a2, v)
        slr_out = ctx @ slr_wo
        mixed = ssm_out + (p_medium + p_full)[:, None, None] * slr_out
        qy = xn[:, -1:, :]
        kk = jnp.broadcast_to(landmarks[None], (b, SLOTS, d))
        attn = jax.nn.softmax(jnp.einsum('bqd,bkd->bqk', qy, kk) / math.sqrt(d), axis=-1)
        arc_ctx = jnp.einsum('bqk,bkd->bqd', attn, kk)
        mixed = mixed.at[:, -1:, :].add(p_full[:, None, None] * arc_ctx)
        out = jnp.concatenate([mixed, xn], axis=-1) @ mix_w
        out = residual + _rms(out, w_norm_out)
        summary = out.mean(axis=1, keepdims=True) @ bus_compress
        published = summary @ bus_publish
        aw = jax.nn.softmax(jnp.einsum('bqd,bkd->bqk', summary, published) / math.sqrt(BUS), axis=-1)
        context = jnp.einsum('bqk,bkd->bqd', aw, published)
        out = out + 0.1 * (context @ bus_expand)
        return out

    def _L0_ffn_ref(x, Wr, Wg, Wu, Wd):
        import jax, jax.numpy as jnp
        import numpy as np
        B, L, D, E, K, DFF = (2, 256, 128, 8, 2, 512)
        Bb, Ll, Dd = x.shape
        T = Bb * Ll
        xt = x.reshape(T, Dd)
        logits = jnp.einsum('td,ed->te', xt, Wr)
        scores = jax.nn.softmax(logits, axis=-1)
        k_scores, k_ids = jax.lax.top_k(scores, K)
        eps = jnp.finfo(x.dtype).eps
        k_w = k_scores / (k_scores.sum(axis=-1, keepdims=True) + eps)
        combine = jnp.sum(jax.nn.one_hot(k_ids, E, dtype=x.dtype) * k_w[..., None], axis=1)
        g = jnp.einsum('td,efd->etf', xt, Wg)
        u = jnp.einsum('td,efd->etf', xt, Wu)
        h = jax.nn.relu(g) * u
        out_e = jnp.einsum('etf,edf->etd', h, Wd)
        out = jnp.einsum('te,etd->td', combine, out_e)
        return out.reshape(Bb, Ll, Dd)
    x = L0_attn_x
    x = x + 0.5 * _L0_ffn_ref(_layernorm(x, axis=-1), L0_ffn_Wr, L0_ffn_Wg, L0_ffn_Wu, L0_ffn_Wd)
    x = x + _L0_attn_ref(_layernorm(x, axis=-1), L0_attn_w_norm_in, L0_attn_w_norm_out, L0_attn_router_w1, L0_attn_router_w2, L0_attn_router_b2, L0_attn_ttt_w1, L0_attn_ttt_b1, L0_attn_ttt_w2, L0_attn_ttt_b2, L0_attn_lambdas, L0_attn_slr_wq1, L0_attn_slr_wq2, L0_attn_slr_wk1, L0_attn_slr_wk2, L0_attn_slr_wv, L0_attn_slr_wo, L0_attn_slr_lam, L0_attn_landmarks, L0_attn_mix_w, L0_attn_bus_compress, L0_attn_bus_expand, L0_attn_bus_publish)
    x = x + 0.5 * _L0_ffn_ref(_layernorm(x, axis=-1), L0_ffn_Wr, L0_ffn_Wg, L0_ffn_Wu, L0_ffn_Wd)
    return x

_drawn_inputs = setup_inputs


def setup_inputs(seed=0):
    import zlib

    import numpy as np

    out = dict(_drawn_inputs(seed))
    spreads = {'L0_attn_w_norm_in': (1.0, 0.2),
     'L0_attn_w_norm_out': (1.0, 0.2),
     'L0_attn_router_b2': (0.5, 0.6),
     'L0_attn_ttt_b1': (0.0, 0.1),
     'L0_attn_ttt_b2': (0.0, 0.1)}
    factors = {'L0_attn_router_w1': 38.379,
     'L0_attn_router_w2': 34.046,
     'L0_attn_slr_wq1': 8.0,
     'L0_attn_slr_wq2': 8.0,
     'L0_attn_slr_wk1': 8.0,
     'L0_attn_slr_wk2': 8.0,
     'L0_attn_slr_wv': 8.0,
     'L0_attn_slr_wo': 8.0,
     'L0_attn_landmarks': 64.0,
     'L0_attn_bus_compress': 8.0,
     'L0_attn_bus_expand': 8.0,
     'L0_attn_bus_publish': 8.0,
     'L0_ffn_Wr': 8.0,
     'L0_ffn_Wg': 8.0,
     'L0_ffn_Wu': 7.477,
     'L0_ffn_Wd': 7.481}
    for name, (base, spread) in spreads.items():
        noise = np.random.default_rng([zlib.crc32(name.encode()), seed]).standard_normal(out[name].shape)
        drawn = base * np.exp(spread * noise) if base else spread * noise
        out[name] = jnp.asarray(drawn.astype(out[name].dtype))
    for name, factor in factors.items():
        out[name] = (out[name] * factor).astype(out[name].dtype)
    return out
```

```python
from contextlib import ExitStack

import concourse.bass as bass
from concourse import mybir

ALU = mybir.AluOpType
ACT = mybir.ActivationFunctionType
AX = mybir.AxisListType
F32 = mybir.dt.float32
F32R = mybir.dt.float32r

P = 128
LN_EPS = 1e-5
FP32_EPS = 1.1920929e-07


def over(ap, axis, shape):
    return ap.unsqueeze(axis).broadcast_to(shape)


def ffn_phase(nc, tag, persist, T, D, E, F, finish):
    X, rstd, stats = persist["X"], persist["rstd"], persist["stats"]
    ident, sel = persist["ident"], persist["sel"]
    WrH, WrL, later = persist["WrH"], persist["WrL"], persist["later"]
    WgH, WgL, WuH, WuL, WdH, WdL = (persist[n] for n in ("WgH", "WgL", "WuH", "WuL", "WdH", "WdL"))
    C = 512
    TC = C // P
    CHUNKS = T // C
    FS = F // P
    S = E * FS
    LAG = 2
    NB = 4

    with ExitStack() as ctx:
        def sb(name, shape, dt=F32):
            return ctx.enter_context(nc.sbuf_tensor(tag + name, shape, dt))

        def sem(name):
            return ctx.enter_context(nc.semaphore(tag + name))

        xn = sb("xn", [P, TC, D])
        xTh = sb("xTh", [P, 2, C], F32R)
        xTl = sb("xTl", [P, 2, C], F32R)
        lg = sb("lg", [P, TC, E])
        ex = sb("ex", [P, TC, E])
        mx = sb("mx", [P, 4, TC])
        beats = sb("beats", [P, TC * E, E])
        ties = sb("ties", [P, TC * E, E])
        rank = sb("rank", [P, TC, E])
        comb = sb("comb", [P, TC, E])
        cpart = sb("cpart", [P, TC, 2 * E], F32R)
        cT = sb("cT", [2 * E, 2, C], F32R)
        cb = sb("cb", [P, 2, C])
        rg = sb("rg", [P, 2, C])
        h = sb("h", [P, NB, C])
        hh = sb("hh", [P, NB, C], F32R)
        hl = sb("hl", [P, NB, C], F32R)
        yc = sb("yc", [P, 2, C])
        acc = sb("acc", [P, 2, C])
        xnew = sb("xnew", [P, TC, D])
        bst = sb("bst", [P, TC, 6])
        mv = sb("mv", [P, TC, 2])
        psG = ctx.enter_context(nc.psum_tensor(tag + "psG", [P, 2, C], F32))
        psU = ctx.enter_context(nc.psum_tensor(tag + "psU", [P, 2, C], F32))
        psY = ctx.enter_context(nc.psum_tensor(tag + "psY", [P, 2, C], F32))
        psM = ctx.enter_context(nc.psum_tensor(tag + "psM", [P, 2, C], F32))

        gate_ready = sem("gate_ready")
        up_ready = sem("up_ready")
        down_done = sem("down_done")
        relu_done = sem("relu_done")
        hid_done = sem("hid_done")
        hidh_done = sem("hidh_done")
        hidl_done = sem("hidl_done")
        scaled = sem("scaled")
        added = sem("added")
        norm_done = sem("norm_done")
        normT = sem("normT")
        xTh_done = sem("xTh_done")
        xTl_done = sem("xTl_done")
        logits_ready = sem("logits_ready")
        chain = sem("chain")
        shifted = sem("shifted")
        exp_done = sem("exp_done")
        comb_done = sem("comb_done")
        combT = sem("combT")
        cT_done = sem("cT_done")
        spread = sem("spread")
        cb_done = sem("cb_done")
        accT = sem("accT")
        x_done = sem("x_done")
        bst_done = sem("bst_done")
        mv_done = sem("mv_done")
        stored = sem("stored")
        CHAIN = 13

        AT_ACCT, AT_X = 6, 7
        AT_NORM, AT_NORMT, AT_XH, AT_XL = 7, 9, 10, 10
        AT_LOGITS, AT_SHIFT, AT_EXP, AT_ROUTE = 12, 12, 13, 14
        AT_COMBT, AT_CT = 18, 19
        AT_SPREAD = 2

        def tiles(c):
            return bass.ds(c * TC, TC) if not isinstance(c, int) else slice(c * TC, c * TC + TC)

        def one_tile(c, t):
            return bass.ds(c * TC + t, 1) if not isinstance(c, int) else slice(c * TC + t, c * TC + t + 1)

        def pe_three(out, ah, al, bh, bl, first=True, last=True):
            nc.tensor.matmul(out, ah, bh, start=first, stop=False)
            nc.tensor.matmul(out, al, bh, start=False, stop=False)
            return nc.tensor.matmul(out, ah, bl, start=False, stop=last)

        def pe_up(pe, c, p, s, first):
            n = c * S + s
            w = slice(s * P, s * P + P)
            if s == 0:
                pe.wait_ge(xTl_done, c + 1)
            if not (first and s < 2):
                pe.wait_ge(relu_done, n - 1)
            pe_three(psG[:, s % 2, :], WgH[:, w], WgL[:, w], xTh[:, p, :], xTl[:, p, :]).then_inc(gate_ready, 1)
            if not (first and s < 2):
                pe.wait_ge(hid_done, n - 1)
            pe_three(psU[:, s % 2, :], WuH[:, w], WuL[:, w], xTh[:, p, :], xTl[:, p, :]).then_inc(up_ready, 1)

        def pe_down(pe, c, s, first):
            n = c * S + s
            w = slice(s * P, s * P + P)
            e, f = s // FS, s % FS
            if f == 0 and not (first and e < 2):
                pe.wait_ge(scaled, c * E + e - 1)
            pe.wait_ge(hidl_done, n + 1)
            pe_three(psY[:, e % 2, :], WdH[:, w], WdL[:, w], hh[:, s % NB, :], hl[:, s % NB, :],
                     f == 0, f == FS - 1).then_inc(down_done, 1)

        def pe_accT(pe, c, p):
            pe.wait_ge(added, (c + 1) * (E - 1))
            for t in range(TC):
                m = nc.tensor.transpose(psM[:, 0, t * P:t * P + P], acc[:, p, t * P:t * P + P], ident[:, :])
            m.then_inc(accT, 1)

        def pe_normT(pe, c, start):
            pe.wait_ge(norm_done, c + 1)
            if not start:
                pe.wait_ge(x_done, c - 1)
            for t in range(TC):
                m = nc.tensor.transpose(psM[:, 0, t * P:t * P + P], xn[:, t, :], ident[:, :])
            m.then_inc(normT, 1)

        def pe_logits(pe, c, p, start):
            pe.wait_ge(xTl_done, c + 1)
            if not start:
                pe.wait_ge(cb_done, (c - 1) * E + (AT_LOGITS - AT_SPREAD - 1) // FS + 1)
            for t in range(TC):
                k = slice(t * P, t * P + P)
                nc.tensor.matmul(psM[:, 1, t * E:t * E + E], xTh[:, p, k], WrH[:, :], start=True, stop=False)
                nc.tensor.matmul(psM[:, 1, t * E:t * E + E], xTl[:, p, k], WrH[:, :], start=False, stop=False)
                m = nc.tensor.matmul(psM[:, 1, t * E:t * E + E], xTh[:, p, k], WrL[:, :], start=False, stop=True)
            m.then_inc(logits_ready, 1)

        def pe_combT(pe, c):
            pe.wait_ge(comb_done, c + 1)
            for t in range(TC):
                m = nc.tensor.transpose(psM[0:2 * E, 0, t * P:t * P + P], cpart[:, t, :].bitcast(F32), ident[:, :])
            m.then_inc(combT, 1)

        def pe_spread(pe, c, p, e, first, last):
            if e == 0:
                pe.wait_ge(cT_done, c + 1)
            if not (first and e == 0):
                pe.wait_ge(cb_done, c * E + e)
            if e == (AT_LOGITS - AT_SPREAD - 1) // FS + 1 and not last:
                pe.wait_ge(shifted, c + 2)
            nc.tensor.matmul(psM[:, 1, :], sel[:, e, :], cT[:, p, :], start=True, stop=True).then_inc(spread, 1)

        def act_relu(act, c, s, first):
            n = c * S + s
            act.wait_ge(gate_ready, n + 1)
            if not (first and s < 2):
                act.wait_ge(hid_done, n - 1)
            nc.scalar.activation(rg[:, s % 2, :], psG[:, s % 2, :], ACT.Relu).then_inc(relu_done, 1)

        def act_hid_high(act, c, s, first):
            n = c * S + s
            act.wait_ge(hid_done, n + 1)
            if not (first and s < NB):
                act.wait_ge(down_done, n + 1 - NB)
            nc.scalar.activation(hh[:, s % NB, :], h[:, s % NB, :], ACT.Copy).then_inc(hidh_done, 1)

        def act_xTh(act, c, p):
            act.wait_ge(normT, c + 1)
            nc.scalar.activation(xTh[:, p, :], psM[:, 0, :], ACT.Copy).then_inc(xTh_done, 1)

        def act_exp(act, c):
            act.wait_ge(shifted, c + 1)
            nc.scalar.activation(ex[:, :, :], lg[:, :, :], ACT.Exp).then_inc(exp_done, 1)

        def act_cT(act, c, p):
            act.wait_ge(combT, c + 1)
            nc.scalar.activation(cT[:, p, :], psM[0:2 * E, 0, :], ACT.Copy).then_inc(cT_done, 1)

        def act_cb(act, c, e, first):
            act.wait_ge(spread, c * E + e + 1)
            if not (first and e < 2):
                act.wait_ge(scaled, c * E + e - 1)
            nc.scalar.activation(cb[:, e % 2, :], psM[:, 1, :], ACT.Copy).then_inc(cb_done, 1)

        def dve_hid(dve, c, s, first):
            n = c * S + s
            dve.wait_ge(relu_done, n + 1)
            dve.wait_ge(up_ready, n + 1)
            if not (first and s < NB):
                dve.wait_ge(hidh_done, n + 1 - NB)
                dve.wait_ge(hidl_done, n + 1 - NB)
            nc.vector.tensor_tensor(h[:, s % NB, :], rg[:, s % 2, :], psU[:, s % 2, :], ALU.mult).then_inc(hid_done, 1)

        def dve_hid_low(dve, c, s, first):
            n = c * S + s
            dve.wait_ge(hidh_done, n + 1)
            if not (first and s < NB):
                dve.wait_ge(down_done, n + 1 - NB)
            nc.vector.tensor_tensor(hl[:, s % NB, :], h[:, s % NB, :], hh[:, s % NB, :].bitcast(F32),
                                    ALU.subtract).then_inc(hidl_done, 1)

        def dve_scale(dve, c, e, first):
            dve.wait_ge(down_done, c * S + (e + 1) * FS)
            dve.wait_ge(cb_done, c * E + e + 1)
            if not (first and e < 2):
                dve.wait_ge(added, c * (E - 1) + (max(e - 2, 1) if e >= 2 else e - 1))
            nc.vector.tensor_tensor(yc[:, e % 2, :], cb[:, e % 2, :], psY[:, e % 2, :], ALU.mult).then_inc(scaled, 1)

        def dve_norm(dve, c, start):
            if not start:
                dve.wait_ge(normT, c)
            for t in range(TC):
                k = one_tile(c, t)
                i = nc.vector.tensor_scalar(xn[:, t:t + 1, :], X[:, k, :], stats[:, k, 0:1], rstd[:, k],
                                            ALU.subtract, ALU.mult)
            i.then_inc(norm_done, 1)

        def dve_xTl(dve, c, p):
            dve.wait_ge(xTh_done, c + 1)
            nc.vector.tensor_tensor(xTl[:, p, :], psM[:, 0, :], xTh[:, p, :].bitcast(F32),
                                    ALU.subtract).then_inc(xTl_done, 1)

        def dve_shift(dve, c):
            base = c * CHAIN
            L = psM[:, 1, 0:TC * E].rearrange("p (t e) -> p t e", e=E)
            dve.wait_ge(logits_ready, c + 1)
            nc.vector.tensor_reduce(mx[:, 0, :], L, AX.X, ALU.max).then_inc(chain, 1)
            dve.wait_ge(chain, base + 1)
            nc.vector.tensor_tensor(lg[:, :, :], L, over(mx[:, 0, :], 2, (P, TC, E)),
                                    ALU.subtract).then_inc(shifted, 1)

        def dve_route(dve, c, start):
            base = c * CHAIN + 1
            n = [0]

            def link(ins):
                n[0] += 1
                ins.then_inc(chain, 1)
                dve.wait_ge(chain, base + n[0])

            dve.wait_ge(exp_done, c + 1)
            link(nc.vector.tensor_reduce(mx[:, 1, :], ex[:, :, :], AX.X, ALU.add))
            link(nc.vector.reciprocal(mx[:, 2, :], mx[:, 1, :]))
            link(nc.vector.tensor_tensor(lg[:, :, :], ex[:, :, :], over(mx[:, 2, :], 2, (P, TC, E)), ALU.mult))
            mine = over(lg[:, :, :].rearrange("p t e -> p (t e)"), 2, (P, TC * E, E))
            flat = lg[:, :, :]
            for t in range(TC):
                other = flat[:, t:t + 1, :].broadcast_to((P, E, E))
                k = slice(t * E, t * E + E)
                nc.vector.tensor_tensor(beats[:, k, :], other, mine[:, k, :], ALU.is_gt)
                i = nc.vector.tensor_tensor(ties[:, k, :], other, mine[:, k, :], ALU.is_equal)
            link(i)
            link(nc.vector.tensor_tensor(ties[:, :, :], ties[:, :, :], later[:, :, :], ALU.mult))
            link(nc.vector.tensor_tensor(beats[:, :, :], beats[:, :, :], ties[:, :, :], ALU.add))
            link(nc.vector.tensor_reduce(rank[:, :, :].rearrange("p t e -> p (t e)"), beats[:, :, :], AX.X, ALU.add))
            link(nc.vector.scalar_tensor_tensor(out=rank[:, :, :], in0=rank[:, :, :], scalar=1.5, in1=lg[:, :, :],
                                                op0=ALU.is_lt, op1=ALU.mult))
            link(nc.vector.tensor_reduce(mx[:, 1, :], rank[:, :, :], AX.X, ALU.add))
            link(nc.vector.tensor_scalar(mx[:, 2, :], mx[:, 1, :], FP32_EPS, None, ALU.add))
            link(nc.vector.reciprocal(mx[:, 3, :], mx[:, 2, :]))
            link(nc.vector.tensor_tensor(comb[:, :, :], rank[:, :, :], over(mx[:, 3, :], 2, (P, TC, E)), ALU.mult))
            assert n[0] == CHAIN - 1
            if not start:
                dve.wait_ge(combT, c)
            nc.vector.tensor_copy(cpart[:, :, 0:E], comb[:, :, :]).then_inc(comb_high, 1)
            dve.wait_ge(comb_high, c + 1)
            nc.vector.tensor_tensor(cpart[:, :, E:2 * E], comb[:, :, :], cpart[:, :, 0:E].bitcast(F32),
                                    ALU.subtract).then_inc(comb_done, 1)

        comb_high = sem("comb_high")

        def dve_update(dve, c):
            dve.wait_ge(accT, c + 1)
            old = X[:, tiles(c), :].rearrange("p t d -> p (t d)")
            if finish:
                nc.vector.scalar_tensor_tensor(out=old, in0=psM[:, 0, :], scalar=0.5, in1=old,
                                               op0=ALU.mult, op1=ALU.add).then_inc(x_done, 1)
                return
            nc.vector.scalar_tensor_tensor(out=xnew[:, :, :].rearrange("p t d -> p (t d)"), in0=psM[:, 0, :], scalar=0.5,
                                           in1=old, op0=ALU.mult, op1=ALU.add).then_inc(x_done, 1)
            dve.wait_ge(x_done, c + 1)
            for t in range(TC):
                i = nc.vector.bn_stats(bst[:, t, :], xnew[:, t, :])
            i.then_inc(bst_done, 1)
            dve.wait_ge(bst_done, c + 1)
            nc.vector.tensor_scalar(X[:, tiles(c), :], xnew[:, :, :], 1.0, None, ALU.mult)
            for t in range(TC):
                i = nc.vector.bn_aggr(mv[:, t, :], bst[:, t, :])
            i.then_inc(mv_done, 1)
            dve.wait_ge(mv_done, c + 1)
            nc.vector.tensor_scalar(stats[:, tiles(c), :], mv[:, :, :], 1.0, None, ALU.mult)

        def pe_chunk(pe, c, p, first, last):
            for s in range(S):
                pe_up(pe, c, p, s, first)
                if s >= LAG:
                    pe_down(pe, c, s - LAG, first)
                elif not first:
                    pe_down(pe, c - 1, S + s - LAG, False)
                if s == AT_ACCT and not first:
                    pe_accT(pe, c - 1, 1 - p)
                if not last:
                    if s == AT_NORMT:
                        pe_normT(pe, c + 1, first)
                    if s == AT_LOGITS:
                        pe_logits(pe, c + 1, 1 - p, False)
                    if s == AT_COMBT:
                        pe_combT(pe, c + 1)
                if s % FS == AT_SPREAD:
                    pe_spread(pe, c, p, s // FS, first, last)

        def act_chunk(act, c, p, first, last):
            for s in range(S):
                act_relu(act, c, s, first)
                if s >= 1:
                    act_hid_high(act, c, s - 1, first)
                elif not first:
                    act_hid_high(act, c - 1, S - 1, False)
                if not last:
                    if s == AT_XH:
                        act_xTh(act, c + 1, 1 - p)
                    if s == AT_EXP:
                        act_exp(act, c + 1)
                    if s == AT_CT:
                        act_cT(act, c + 1, 1 - p)
                if s % FS == AT_SPREAD + 1:
                    act_cb(act, c, s // FS, first)

        def dve_chunk(dve, c, p, first, last):
            for s in range(S):
                dve_hid(dve, c, s, first)
                if s >= 1:
                    dve_hid_low(dve, c, s - 1, first)
                elif not first:
                    dve_hid_low(dve, c - 1, S - 1, False)
                if s >= LAG + FS and (s - LAG) % FS == 0:
                    dve_scale(dve, c, (s - LAG) // FS - 1, first)
                elif s == LAG and not first:
                    dve_scale(dve, c - 1, E - 1, False)
                if s == AT_X and not first:
                    dve_update(dve, c - 1)
                if not last:
                    if s == AT_NORM:
                        dve_norm(dve, c + 1, False)
                    if s == AT_XL:
                        dve_xTl(dve, c + 1, 1 - p)
                    if s == AT_SHIFT:
                        dve_shift(dve, c + 1)
                    if s == AT_ROUTE:
                        dve_route(dve, c + 1, False)

        def pool_chunk(pool, c, p, first):
            for e in range(1, E):
                pool.wait_ge(scaled, c * E + e + 1)
                if e == 1:
                    if not first:
                        pool.wait_ge(accT, c - 1)
                    nc.gpsimd.tensor_tensor(acc[:, p, :], yc[:, 0, :], yc[:, 1, :], ALU.add).then_inc(added, 1)
                else:
                    pool.wait_ge(added, c * (E - 1) + e - 1)
                    nc.gpsimd.tensor_tensor(acc[:, p, :], acc[:, p, :], yc[:, e % 2, :], ALU.add).then_inc(added, 1)

        def over_chunks(eng, body):
            body(eng, 0, 0, True, False)
            body(eng, 1, 1, False, False)
            with eng.Fori(2, CHUNKS - 2, 2) as c:
                body(eng, c, 0, False, False)
                body(eng, c + 1, 1, False, False)
            body(eng, CHUNKS - 2, 0, False, False)
            body(eng, CHUNKS - 1, 1, False, True)

        end = CHUNKS - 1
        block = ctx.enter_context(nc.Block(tag + "block"))

        @block.tensor
        def _(pe):
            pe_normT(pe, 0, True)
            pe_logits(pe, 0, 0, True)
            pe_combT(pe, 0)
            over_chunks(pe, pe_chunk)
            for s in range(S - LAG, S):
                pe_down(pe, end, s, False)
            pe_accT(pe, end, end % 2)

        @block.scalar
        def _(act):
            act_xTh(act, 0, 0)
            act_exp(act, 0)
            act_cT(act, 0, 0)
            over_chunks(act, act_chunk)
            act_hid_high(act, end, S - 1, False)

        @block.vector
        def _(dve):
            dve_norm(dve, 0, True)
            dve_xTl(dve, 0, 0)
            dve_shift(dve, 0)
            dve_route(dve, 0, True)
            over_chunks(dve, dve_chunk)
            dve_hid_low(dve, end, S - 1, False)
            dve_scale(dve, end, E - 1, False)
            dve_update(dve, end)

        @block.gpsimd
        def _(pool):
            over_chunks(pool, lambda eng, c, p, first, last: pool_chunk(
                eng, c, p, first or (isinstance(c, int) and c == 1)))

        if finish:
            @block.sync
            def _(sp):
                with sp.Fori(0, CHUNKS) as c:
                    sp.wait_ge(x_done, c + 1)
                    sp.dma_start(persist["out"][:, bass.ds(c * TC, TC), :], X[:, bass.ds(c * TC, TC), :]).then_inc(stored, 16)
                sp.wait_ge(stored, 16 * CHUNKS)


def moe_constants(nc, tag, persist, ins, T, D, E, F, first):
    X, stats = persist["X"], persist["stats"]
    W = E * F
    TILES = T // P
    with ExitStack() as ctx:
        raw = [ctx.enter_context(nc.sbuf_tensor(tag + f"raw{k}", [P, W], F32)) for k in range(3)]
        wr = ctx.enter_context(nc.sbuf_tensor(tag + "wr", [P, E], F32))
        bst = ctx.enter_context(nc.sbuf_tensor(tag + "bst0", [P, TILES, 6], F32))
        in_w = [ctx.enter_context(nc.semaphore(tag + f"in_w{k}")) for k in range(3)]
        in_x = [ctx.enter_context(nc.semaphore(tag + f"in_x{k}")) for k in range(4)]
        in_wr = ctx.enter_context(nc.semaphore(tag + "in_wr"))
        high = ctx.enter_context(nc.semaphore(tag + "high"))
        bst_ready = ctx.enter_context(nc.semaphore(tag + "bst_ready"))
        made = ctx.enter_context(nc.semaphore(tag + "made"))
        sel0 = ctx.enter_context(nc.sbuf_tensor(tag + "sel0", [2 * E, E, P], F32))
        pairs = [("WgH", "WgL", "WgT"), ("WuH", "WuL", "WuT"), ("WdH", "WdL", "WdT")]
        Q = TILES // 4
        block = ctx.enter_context(nc.Block(tag + "setup"))

        @block.sync
        def _(sp):
            sp.dma_start(wr[:, :], ins["WrT"]).then_inc(in_wr, 16)
            for k in range(4 if first else 0):
                sp.dma_start(X[:, k * Q:k * Q + Q, :], persist["x"][:, k * Q:k * Q + Q, :]).then_inc(in_x[k], 16)
            for k in range(3):
                sp.dma_start(raw[k][:, :], ins[pairs[k][2]]).then_inc(in_w[k], 16)

        @block.gpsimd
        def _(pool):
            ident, later = persist["ident"], persist["later"]
            nc.gpsimd.memset(ident[:, :], 0.0).then_inc(made, 1)
            nc.gpsimd.memset(later[:, :, :], 1.0).then_inc(made, 1)
            nc.gpsimd.memset(sel0[:, :, :], 0.0).then_inc(made, 1)
            pool.wait_ge(made, 3)
            nc.gpsimd.affine_select(out=ident[:, :], in_=ident[:, :], compare_op=ALU.not_equal, fill=1.0,
                                    base=0, pattern=[[-1, P]], channel_multiplier=1)
            nc.gpsimd.affine_select(out=later[:, :, :].rearrange("p (t e) j -> p t e j", e=E),
                                    in_=later[:, :, :].rearrange("p (t e) j -> p t e j", e=E),
                                    compare_op=ALU.is_gt, fill=0.0, base=0,
                                    pattern=[[0, 4], [1, E], [-1, E]], channel_multiplier=0)
            nc.gpsimd.affine_select(out=sel0[:, :, :], in_=sel0[:, :, :], compare_op=ALU.not_equal, fill=1.0,
                                    base=0, pattern=[[-1, E], [0, P]], channel_multiplier=1).then_inc(made, 1)
            pool.wait_ge(made, 4)
            nc.gpsimd.affine_select(out=sel0[:, :, :], in_=sel0[:, :, :], compare_op=ALU.not_equal, fill=1.0,
                                    base=-E, pattern=[[-1, E], [0, P]], channel_multiplier=1).then_inc(made, 1)

        @block.scalar
        def _(act):
            act.wait_ge(in_wr, 16)
            nc.scalar.activation(persist["WrH"][:, :], wr[:, :], ACT.Copy).then_inc(high, 1)
            for k in range(3):
                act.wait_ge(in_w[k], 16)
                nc.scalar.activation(persist[pairs[k][0]][:, :], raw[k][:, :], ACT.Copy).then_inc(high, 1)
            act.wait_ge(made, 5)
            nc.scalar.activation(persist["sel"][:, :, :], sel0[:, :, :], ACT.Copy)

        @block.vector
        def _(dve):
            dve.wait_ge(high, 1)
            nc.vector.tensor_tensor(persist["WrL"][:, :], wr[:, :], persist["WrH"][:, :].bitcast(F32), ALU.subtract)
            for k in range(4 if first else 0):
                dve.wait_ge(in_x[k], 16)
                for t in range(k * Q, k * Q + Q):
                    i = nc.vector.bn_stats(bst[:, t, :], X[:, t, :])
                i.then_inc(bst_ready, 1)
                dve.wait_ge(bst_ready, k + 1)
                for t in range(k * Q, k * Q + Q):
                    nc.vector.bn_aggr(stats[:, t, :], bst[:, t, :])
            for k in range(3):
                dve.wait_ge(high, k + 2)
                nc.vector.tensor_tensor(persist[pairs[k][1]][:, :], raw[k][:, :],
                                        persist[pairs[k][0]][:, :].bitcast(F32), ALU.subtract)


def norm_phase(nc, tag, persist, T, inner):
    stats, rstd = persist["stats"], persist["rstd"]
    TILES = T // P
    with ExitStack() as ctx:
        v = ctx.enter_context(nc.sbuf_tensor(tag + "v", [P, TILES], F32))
        r = ctx.enter_context(nc.sbuf_tensor(tag + "r", [P, TILES], F32))
        q = ctx.enter_context(nc.sbuf_tensor(tag + "q", [P, TILES], F32))
        link = ctx.enter_context(nc.semaphore(tag + "link"))
        block = ctx.enter_context(nc.Block(tag + "norm"))
        LINKS = 6

        @block.scalar
        def _(act):
            for n in range(2 if inner else 1):
                act.wait_ge(link, n * LINKS + 1)
                nc.scalar.activation(r[:, :], v[:, :], ACT.Sqrt).then_inc(link, 1)

        @block.vector
        def _(dve):
            def root(n, out):
                dve.wait_ge(link, n * LINKS + 2)
                nc.vector.reciprocal(q[:, :], r[:, :]).then_inc(link, 1)
                dve.wait_ge(link, n * LINKS + 3)
                nc.vector.tensor_tensor(r[:, :], q[:, :], q[:, :], ALU.mult).then_inc(link, 1)
                dve.wait_ge(link, n * LINKS + 4)
                nc.vector.scalar_tensor_tensor(out=v[:, :], in0=v[:, :], scalar=-0.5, in1=r[:, :],
                                               op0=ALU.mult, op1=ALU.mult).then_inc(link, 1)
                dve.wait_ge(link, n * LINKS + 5)
                nc.vector.scalar_tensor_tensor(out=out, in0=v[:, :], scalar=1.5, in1=q[:, :],
                                               op0=ALU.add, op1=ALU.mult).then_inc(link, 1)
                dve.wait_ge(link, n * LINKS + 6)

            nc.vector.tensor_scalar(v[:, :], stats[:, :, 1], LN_EPS, None, ALU.add).then_inc(link, 1)
            root(0, rstd[:, :])
            if inner:
                squared = ctx.enter_context(nc.semaphore(tag + "squared"))
                nc.vector.tensor_tensor(q[:, :], rstd[:, :], rstd[:, :], ALU.mult).then_inc(squared, 1)
                dve.wait_ge(squared, 1)
                nc.vector.tensor_tensor(r[:, :], q[:, :], stats[:, :, 1], ALU.mult).then_inc(squared, 1)
                dve.wait_ge(squared, 2)
                nc.vector.tensor_scalar(v[:, :], r[:, :], FP32_EPS, None, ALU.add).then_inc(link, 1)
                root(1, persist["rmsin"][:, :])


def attention_constants(nc, persist, ins):
    A = persist["attn"]
    D = ins["mixA"].shape[0]
    with ExitStack() as ctx:
        raw = ctx.enter_context(nc.sbuf_tensor("aw_raw", [P, 4 * P], F32))
        woT = ctx.enter_context(nc.sbuf_tensor("aw_woT", [P, A["DH"]], F32))
        kone = ctx.enter_context(nc.sbuf_tensor("aw_kone", [P, A["K"].shape[-1]], F32))
        ps = ctx.enter_context(nc.psum_tensor("aw_ps", [P, 512], F32))
        loaded = ctx.enter_context(nc.semaphore("aw_loaded"))
        raw_in = ctx.enter_context(nc.semaphore("aw_raw_in"))
        cleared = ctx.enter_context(nc.semaphore("aw_cleared"))
        high = ctx.enter_context(nc.semaphore("aw_high"))
        folded = ctx.enter_context(nc.semaphore("aw_folded"))
        lam_in = ctx.enter_context(nc.semaphore("aw_lam_in"))
        DH = A["DH"]
        block = ctx.enter_context(nc.Block("aw"))

        @block.sync
        def _(sp):
            sp.dma_start(raw[:, :], ins["wproj"]).then_inc(raw_in, 16)
            sp.dma_start(woT[:, :], ins["woT"]).then_inc(loaded, 16)
            sp.dma_start(A["mixA"][:, :], ins["mixA"]).then_inc(loaded, 16)
            sp.dma_start(A["lam"][:, :], ins["lambdas"]).then_inc(lam_in, 16)
            for n in ("mixB", "wv", "w1", "w2", "b2", "w_in", "w_out", "slam", "lm", "lmT", "compress", "publish", "expand"):
                sp.dma_start(A[n][:, :], ins[n]).then_inc(loaded, 16)
            sp.wait_ge(loaded, 16 * 15)

        @block.scalar
        def _(act):
            act.wait_ge(raw_in, 16)
            nc.scalar.activation(A["wpH"][:, :], raw[:, :], ACT.Copy).then_inc(high, 1)

        @block.gpsimd
        def _(pool):
            nc.gpsimd.memset(A["mpad"][:, :, :], 0.0)
            nc.gpsimd.memset(A["V1"][:, :, :, :], 1.0)
            nc.gpsimd.memset(A["half"][:, :], -0.5)
            nc.gpsimd.memset(A["ones"][:, :], 1.0)

        @block.vector
        def _(dve):
            nc.vector.memset(A["Wc"][:, :], 0.0)
            nc.vector.memset(kone[:, :], 1.0)
            nc.vector.memset(A["sgnQ"][:, :], 0.0)
            nc.vector.memset(A["sgnK"][:, :], 0.0).then_inc(cleared, 1)
            dve.wait_ge(cleared, 1)
            nc.vector.memset(A["sgnQ"][DH:2 * DH, :], -1.0)
            nc.vector.memset(A["sgnK"][2 * DH:3 * DH, :], -1.0)
            for m in (0, 1):
                c = m * (D + 1) + D
                nc.vector.memset(A["Wc"][64 * m + DH:64 * m + DH + 1, c:c + 1], 1.0)
            for q in (0, 1):
                for m in (0, 1):
                    nc.vector.tensor_copy(A["K"][96:97, q, m, :], kone[96:97, :])
            dve.wait_ge(high, 1)
            nc.vector.tensor_tensor(A["wpL"][:, :], raw[:, :], A["wpH"][:, :].bitcast(F32), ALU.subtract)
            dve.wait_ge(lam_in, 16)
            nc.vector.tensor_scalar(A["oml"][:, :], A["lam"][:, :], -1.0, 1.0, ALU.mult, ALU.add)
            dve.wait_ge(folded, 1)
            for m in (0, 1):
                nc.vector.tensor_copy(A["Wc"][64 * m:64 * m + DH, m * (D + 1):m * (D + 1) + D], ps[64 * m:64 * m + DH, 0:D])

        @block.tensor
        def _(pe):
            pe.wait_ge(loaded, 16 * 15)
            for m in (0, 1):
                i = nc.tensor.matmul(ps[64 * m:64 * m + DH, 0:D], woT[:, :], A["mixA"][:, :], start=True, stop=True)
            i.then_inc(folded, 1)


def attention_phase(nc, persist, T, BATCH):
    A = persist["attn"]
    X, stats, rstd, ident = persist["X"], persist["stats"], persist["rstd"], persist["ident"]
    rmsin = persist["rmsin"]
    D, DH = 128, A["DH"]
    R = 3 * DH
    SEQ = T // BATCH
    TT = SEQ // P
    H = 512
    SC = float(DH) ** -0.5
    ARC = float(D) ** -0.5
    NL = A["lm"].shape[0]
    with ExitStack() as ctx:
        def sb(name, shape, dt=F32):
            return ctx.enter_context(nc.sbuf_tensor("at_" + name, shape, dt))

        def sem(name):
            return ctx.enter_context(nc.semaphore("at_" + name))

        Y = sb("Y", [P, TT, D])
        ysum = sb("ysum", [P, 2])
        ybus = sb("ybus", [P, 1])
        xn = sb("xn", [P, TT, D])
        xnT = sb("xnT", [P, SEQ])
        xnTh = sb("xnTh", [P, SEQ], F32R)
        xnTl = sb("xnTl", [P, SEQ], F32R)
        projh = sb("projh", [P, 2, H], F32R)
        rsum = sb("rsum", [P, 2])
        ema_in = sb("ema_in", [P, SEQ])
        ssmT = sb("ssmT", [P, SEQ])
        base = sb("base", [P, 2, TT, D])
        Ex = sb("Ex", [P, 2, 2 * H])
        CT = sb("CT", [P, 2, SEQ])
        O = sb("O", [P, TT, D])
        sq = sb("sq", [P, TT, D])
        col = sb("col", [P, 16])
        p3 = sb("p3", [P, 8])
        pl = sb("pl", [P, 2, 2])
        silb = sb("silb", [64, P])
        arow = sb("arow", [1, NL])
        arcn = sb("arcn", [1, 4])
        acol = sb("acol", [NL, 1])
        rec = sb("rec", [P, 2])
        coef = sb("coef", [P, TT, 2])
        ss = sb("ss", [P, TT])
        ms = sb("ms", [P, TT])
        rr = sb("rr", [P, TT])
        busc = sb("busc", [P, 4])
        pubb = sb("pubb", [P, P])
        bst = sb("bst", [P, TT, 6])
        mv = sb("mv", [P, TT, 2])
        psE = ctx.enter_context(nc.psum_tensor("at_psE", [P, 2, 2 * H], F32))
        psS = ctx.enter_context(nc.psum_tensor("at_psS", [P, 2, H], F32))
        psC = ctx.enter_context(nc.psum_tensor("at_psC", [P, H], F32))
        psM = ctx.enter_context(nc.psum_tensor("at_psM", [P, H], F32))

        y_done, xn_done = sem("y_done"), sem("xn_done")
        xT_ready, xT_done, xTh_done = sem("xT_ready"), sem("xT_done"), sem("xTh_done")
        xTl_done = sem("xTl_done")
        proj_ready, projh_done, proj_done = sem("proj_ready"), sem("projh_done"), sem("proj_done")
        v_ready, v_done = sem("v_ready"), sem("v_done")
        r1_ready, r1_exp, r1_done = sem("r1_ready"), sem("r1_exp"), sem("r1_done")
        r1_copied = sem("r1_copied")
        arc_max, arc_exp = sem("arc_max"), sem("arc_exp")
        r2_ready, r2_shift, r2_exp, r2_done = sem("r2_ready"), sem("r2_shift"), sem("r2_exp"), sem("r2_done")
        r3_ready, r3_done = sem("r3_ready"), sem("r3_done")
        rchain = sem("rchain")
        ema_scaled, ema_done = sem("ema_scaled"), sem("ema_done")
        p1_ready, p1_done = sem("p1_ready"), sem("p1_done")
        row_ready, row_done = sem("row_ready"), sem("row_done")
        st_ready, ex_done, pv_done = sem("st_ready"), sem("ex_done"), sem("pv_done")
        ct_done = sem("ct_done")
        mix_ready = sem("mix_ready")
        base_ready, base_done = sem("base_ready"), sem("base_done")
        xr_done = sem("xr_done")
        mchain = sem("mchain")
        o_done, sq_done = sem("o_done"), sem("sq_done")
        ms_done, rr_done, o2_done = sem("ms_done"), sem("rr_done"), sem("o2_done")
        bus_ready, bus_done = sem("bus_ready"), sem("bus_done")
        xa_done, bst_done, mv_done = sem("xa_done"), sem("bst_done"), sem("mv_done")

        UNITS = 16
        KP = SEQ // P // 2
        CR = 64 + DH + 1
        RCH, MCH = 10, 3

        def group(g):
            return g % 2, g // 2

        def half(h):
            return slice(h * H, h * H + H)

        def tile_cols(t):
            return slice(t * P, t * P + P)

        def xtiles(b):
            return slice(b * TT, b * TT + TT) if isinstance(b, int) else bass.ds(b * TT, TT)

        def xtile(b, t):
            return slice(b * TT + t, b * TT + t + 1) if isinstance(b, int) else bass.ds(b * TT + t, 1)

        def pe_xT(pe, b, q, h, start):
            pe.wait_ge(xn_done, 2 * b + h + 1)
            if h == 0 and not start:
                pe.wait_ge(p1_done, UNITS * b)
            for t in range(4):
                i = nc.tensor.transpose(psS[:, h, tile_cols(t)], xn[:, 4 * h + t, :], ident[:, :])
            i.then_inc(xT_ready, 1)

        def pe_proj(pe, b, k):
            w, h = k // 2, k % 2
            if k == 0:
                pe.wait_ge(xTl_done, 2 * b + 2)
            if k >= 2:
                pe.wait_ge(proj_done, 8 * b + k - 1)
            lo, hi = A["wpL"][:, w * P:w * P + P], A["wpH"][:, w * P:w * P + P]
            out = psS[:, h, :]
            nc.tensor.matmul(out, hi, xnTh[:, half(h)], start=True, stop=False)
            nc.tensor.matmul(out, lo, xnTh[:, half(h)], start=False, stop=False)
            nc.tensor.matmul(out, hi, xnTl[:, half(h)], start=False, stop=True).then_inc(proj_ready, 1)

        def pe_v_r1(pe, b, q):
            pe.wait_ge(proj_done, 8 * b + 8)
            for t in range(TT):
                i = nc.tensor.matmul(psS[:, 0, t * DH:t * DH + DH], xnT[:, tile_cols(t)], A["wv"][:, :],
                                     start=True, stop=True)
            i.then_inc(v_ready, 1)
            for h in (0, 1):
                nc.tensor.matmul(psS[0:64, 1, 0:1], A["w1"][:, :], rsum[:, h:h + 1], start=(h == 0), stop=(h == 1))
            for t in range(TT):
                nc.tensor.matmul(psS[:, 1, 32:33], Y[:, t, :], A["ones"][:, 0:1], start=(t == 0), stop=(t == TT - 1))
            nc.tensor.matmul(psS[0:1, 1, 64:64 + NL], xnT[:, SEQ - 1:SEQ], A["lmT"][:, :],
                             start=True, stop=True).then_inc(r1_ready, 1)

        def pe_r2(pe, b):
            pe.wait_ge(r1_done, b + 1)
            nc.tensor.matmul(psS[:, 1, 0:3], silb[:, :], A["w2"][:, :], start=True, stop=True)
            nc.tensor.matmul(psS[0:NL, 1, 8:9], arow[:, :], A["ones"][0:1, 0:1], start=True, stop=True).then_inc(r2_ready, 1)

        def pe_base(pe, b, h, after_bus):
            if h == 0:
                pe.wait_ge(r3_done, b + 1)
                if after_bus:
                    pe.wait_ge(xa_done, 2 * b - 2)
            else:
                pe.wait_ge(base_done, 2 * b + 1)
            for t in range(4):
                k = tile_cols(4 * h + t)
                nc.tensor.matmul(psM[:, tile_cols(t)], ssmT[:, k], A["mixA"][:, :], start=True, stop=False)
                i = nc.tensor.matmul(psM[:, tile_cols(t)], xnT[:, k], A["mixB"][:, :], start=False, stop=True)
            i.then_inc(base_ready, 1)

        def act_base(act, b, q, h):
            act.wait_ge(base_ready, 2 * b + h + 1)
            nc.scalar.activation(base[:, q, 4 * h:4 * h + 4, :].rearrange("p t d -> p (t d)"), psM[:, :],
                                 ACT.Copy).then_inc(base_done, 1)

        def pe_r3(pe, b):
            pe.wait_ge(r2_done, b + 1)
            nc.tensor.matmul(psS[:, 1, 16:17], A["lm"][:, :], acol[:, :], start=True, stop=True).then_inc(r3_ready, 1)

        def pe_p1(pe, b, q, v):
            m, t = v // TT, v % TT
            if v == 0:
                pe.wait_ge(v_done, b + 1)
                pe.wait_ge(r3_done, b + 1)
            else:
                pe.wait_ge(p1_done, UNITS * b + v)
            for h in (0, 1):
                i = nc.tensor.matmul(psS[:, h, :], A["Q"][0:R, q, m, tile_cols(t)], A["K"][0:R, q, m, half(h)],
                                     start=True, stop=True)
            i.then_inc(p1_ready, 1)

        def pe_row(pe, b, g):
            m, h = group(g)
            pe.wait_ge(p1_done, UNITS * b + TT * m + 4 * h + 4)
            if g >= 1:
                pe.wait_ge(row_done, 4 * b + g)
            else:
                pe.wait_ge(base_done, 2 * b + 2)
            for t in range(4):
                i = nc.tensor.transpose(psM[0:R + 1, tile_cols(t)], A["mpad"][:, TT * m + 4 * h + t, :], ident[:, :])
            i.then_inc(row_ready, 1)

        def act_xT(act, b, q, h, start):
            act.wait_ge(xT_ready, 2 * b + h + 1)
            if h == 0 and not start:
                act.wait_ge(r1_ready, b)
                act.wait_ge(base_ready, 2 * b)
            nc.scalar.activation(xnT[:, half(h)], psS[:, h, :], ACT.Copy, accum_out=rsum[:, h:h + 1]).then_inc(xT_done, 1)
            if h == 0 and not start:
                act.wait_ge(proj_ready, 8 * b)
            nc.scalar.activation(xnTh[:, half(h)], psS[:, h, :], ACT.Copy).then_inc(xTh_done, 1)

        def act_proj(act, b, k, start):
            act.wait_ge(proj_ready, 8 * b + k + 1)
            if not (start and k < 2):
                act.wait_ge(proj_done, 8 * b + k - 1)
            nc.scalar.activation(projh[0:R, k % 2, :], psS[0:R, k % 2, :], ACT.Copy).then_inc(projh_done, 1)

        def act_r1(act, b):
            act.wait_ge(r1_copied, b + 1)
            nc.scalar.activation(col[0:64, 0:1], col[0:64, 4:5], ACT.Exp, scale=-1.0 / SEQ).then_inc(r1_exp, 1)
            act.wait_ge(arc_max, b + 1)
            nc.scalar.activation(arow[:, :], arow[:, :], ACT.Exp, bias=arcn[:, 0:1], scale=ARC,
                                 accum_out=arcn[:, 1:2]).then_inc(arc_exp, 1)

        def act_r2(act, b):
            act.wait_ge(r2_shift, b + 1)
            nc.scalar.activation(p3[:, 0:3], p3[:, 0:3], ACT.Exp, accum_out=p3[:, 3:4]).then_inc(r2_exp, 1)

        def act_row(act, b, q, g):
            m, h = group(g)
            act.wait_ge(row_ready, 4 * b + g + 1)
            nc.scalar.activation(A["Q"][R:R + 1, q, m, half(h)], psM[R:R + 1, :], ACT.Copy).then_inc(row_done, 1)

        def dve_y(dve, b, q, start):
            if not start:
                dve.wait_ge(r1_ready, b)
            for t in range(TT):
                k = xtile(b, t)
                i = nc.vector.tensor_scalar(Y[:, t:t + 1, :], X[:, k, :], stats[:, k, 0:1], rstd[:, k],
                                            ALU.subtract, ALU.mult)
            i.then_inc(y_done, 1)
            dve.wait_ge(y_done, b + 1)
            nc.vector.tensor_tensor(X[:, xtiles(b), :], X[:, xtiles(b), :], Y[:, :, :], ALU.add).then_inc(xr_done, 1)
            for t in range(TT):
                i = nc.vector.scalar_tensor_tensor(out=xn[:, t, :], in0=Y[:, t, :], scalar=rmsin[:, xtile(b, t)],
                                                   in1=A["w_in"][:, :], op0=ALU.mult, op1=ALU.mult)
                if t % 4 == 3:
                    i.then_inc(xn_done, 1)

        def pool_xTl(pool, b, q, h):
            pool.wait_ge(xTh_done, 2 * b + h + 1)
            nc.gpsimd.tensor_tensor(xnTl[:, half(h)], xnT[:, half(h)], xnTh[:, half(h)].bitcast(F32),
                                    ALU.subtract).then_inc(xTl_done, 1)

        def dve_proj(dve, b, q, k):
            w, h = k // 2, k % 2
            m, side = w // 2, ("Q", "K")[w % 2]
            dve.wait_ge(projh_done, 8 * b + k + 1)
            nc.vector.scalar_tensor_tensor(out=A[side][0:R, q, m, half(h)], in0=projh[0:R, k % 2, :].bitcast(F32),
                                           scalar=A["sgn" + side][0:R, :], in1=psS[0:R, h, :],
                                           op0=ALU.mult, op1=ALU.add).then_inc(proj_done, 1)

        def dve_v(dve, b, q):
            dve.wait_ge(v_ready, b + 1)
            nc.vector.tensor_copy(A["V1"][:, q, :, 0:DH],
                                  psS[:, 0, 0:TT * DH].rearrange("p (t c) -> p t c", c=DH)).then_inc(v_done, 1)

        def dve_ema(dve, b, start):
            dve.wait_ge(xT_done, 2 * b + 2)
            if not start:
                dve.wait_ge(base_ready, 2 * b)
            nc.vector.tensor_scalar(ema_in[:, :], xnT[:, :], A["oml"][:, :], None, ALU.mult).then_inc(ema_scaled, 1)
            dve.wait_ge(ema_scaled, b + 1)
            nc.vector.tensor_tensor_scan(out=ssmT[:, :], data0=A["lam"][:, 0:1].broadcast_to((P, SEQ)),
                                         data1=ema_in[:, :], initial=0.0, op0=ALU.mult, op1=ALU.add).then_inc(ema_done, 1)

        def dve_r1(dve, b, q):
            n = [RCH * b]

            def link(ins):
                n[0] = n[0] + 1
                ins.then_inc(rchain, 1)
                dve.wait_ge(rchain, n[0])

            dve.wait_ge(r1_ready, b + 1)
            nc.vector.tensor_copy(ysum[:, q:q + 1], psS[:, 1, 32:33])
            nc.vector.tensor_copy(col[0:64, 4:5], psS[0:64, 1, 0:1])
            nc.vector.tensor_copy(arow[:, :], psS[0:1, 1, 64:64 + NL]).then_inc(r1_copied, 1)
            dve.wait_ge(r1_copied, b + 1)
            link(nc.vector.tensor_reduce(arcn[:, 2:3], arow[:, :], AX.X, ALU.max))
            nc.vector.tensor_scalar(arcn[:, 0:1], arcn[:, 2:3], -ARC, None, ALU.mult).then_inc(arc_max, 1)
            dve.wait_ge(r1_exp, b + 1)
            link(nc.vector.tensor_scalar(col[0:64, 1:2], col[0:64, 0:1], 1.0, None, ALU.add))
            link(nc.vector.reciprocal(col[0:64, 2:3], col[0:64, 1:2]))
            link(nc.vector.scalar_tensor_tensor(out=col[0:64, 3:4], in0=col[0:64, 4:5], scalar=1.0 / SEQ,
                                                in1=col[0:64, 2:3], op0=ALU.mult, op1=ALU.mult))
            nc.vector.tensor_scalar(silb[:, :], A["ones"][0:64, :], col[0:64, 3:4], None, ALU.mult)
            dve.wait_ge(arc_exp, b + 1)
            link(nc.vector.reciprocal(arcn[:, 3:4], arcn[:, 1:2]))
            nc.vector.tensor_scalar(arow[:, :], arow[:, :], arcn[:, 3:4], None, ALU.mult).then_inc(r1_done, 1)

        def dve_r2(dve, b, q):
            n = [RCH * b + 5]

            def link(ins):
                n[0] = n[0] + 1
                ins.then_inc(rchain, 1)
                dve.wait_ge(rchain, n[0])

            dve.wait_ge(r2_ready, b + 1)
            nc.vector.tensor_copy(acol[:, :], psS[0:NL, 1, 8:9])
            link(nc.vector.tensor_tensor(p3[:, 0:3], psS[:, 1, 0:3], A["b2"][:, :], ALU.add))
            link(nc.vector.tensor_reduce(p3[:, 4:5], p3[:, 0:3], AX.X, ALU.max))
            nc.vector.tensor_scalar(p3[:, 0:3], p3[:, 0:3], p3[:, 4:5], None, ALU.subtract).then_inc(r2_shift, 1)
            dve.wait_ge(r2_exp, b + 1)
            link(nc.vector.reciprocal(p3[:, 5:6], p3[:, 3:4]))
            link(nc.vector.tensor_scalar(p3[:, 0:3], p3[:, 0:3], p3[:, 5:6], None, ALU.mult))
            link(nc.vector.tensor_tensor(pl[:, q, 0:1], p3[:, 1:2], p3[:, 2:3], ALU.add))
            nc.vector.scalar_tensor_tensor(out=pl[:, q, 1:2], in0=pl[:, q, 0:1], scalar=-1.0, in1=A["slam"][:, :],
                                           op0=ALU.mult, op1=ALU.mult).then_inc(r2_done, 1)

        def dve_r3(dve, b, q):
            dve.wait_ge(r3_ready, b + 1)
            dve.wait_ge(ema_done, b + 1)
            nc.vector.scalar_tensor_tensor(out=ssmT[:, SEQ - 1:SEQ], in0=psS[:, 1, 16:17], scalar=p3[:, 2:3],
                                           in1=ssmT[:, SEQ - 1:SEQ], op0=ALU.mult, op1=ALU.add).then_inc(r3_done, 1)

        def dve_p1(dve, b, v):
            dve.wait_ge(p1_ready, UNITS * b + v + 1)
            nc.vector.tensor_reduce(A["mpad"][:, v, R:R + 1], psS[:, :, :], AX.XY, ALU.max,
                                    negate=True).then_inc(p1_done, 1)

        def pe_st(pe, b, q, u, start):
            m, h = group(u // KP)
            if u == 0:
                pe.wait_ge(row_done, 4 * b + 4)
            if not (start and u < 2):
                pe.wait_ge(ex_done, UNITS * b + u - 1)
            for j in (0, 1):
                i = nc.tensor.matmul(psE[:, u % 2, j * H:j * H + H], A["K"][0:R + 1, q, m, tile_cols(2 * (u % KP) + j)],
                                     A["Q"][0:R + 1, q, m, half(h)], start=True, stop=True)
            i.then_inc(st_ready, 1)

        def act_ex(act, b, u, start):
            act.wait_ge(st_ready, UNITS * b + u + 1)
            if not (start and u < 2):
                act.wait_ge(pv_done, UNITS * b + u - 1)
            nc.scalar.activation(Ex[:, u % 2, :], psE[:, u % 2, :], ACT.Exp, scale=SC).then_inc(ex_done, 1)

        def pe_pv(pe, b, q, u, start):
            g, kp = u // KP, u % KP
            m, h = group(g)
            pe.wait_ge(ex_done, UNITS * b + u + 1)
            if kp == 0 and not (start and g < 2):
                pe.wait_ge(ct_done, 4 * b + g - 1)
            for j in (0, 1):
                i = nc.tensor.matmul(psC[64 * m:64 * m + DH + 1, :], A["V1"][:, q, 2 * kp + j, :], Ex[:, u % 2, j * H:j * H + H],
                                     start=(kp == 0 and j == 0), stop=(kp == KP - 1 and j == 1))
            i.then_inc(pv_done, 1)

        def dve_ct(dve, b, q, g):
            m, h = group(g)
            dve.wait_ge(pv_done, UNITS * b + KP * (g + 1))
            nc.vector.tensor_copy(CT[64 * m:64 * m + DH + 1, q, half(h)],
                                  psC[64 * m:64 * m + DH + 1, :]).then_inc(ct_done, 1)

        def pe_mix(pe, b, q, t):
            if t == 0:
                pe.wait_ge(ct_done, 4 * b + 4)
            else:
                pe.wait_ge(o_done, TT * b + t)
            nc.tensor.matmul(psM[:, 0:2 * (D + 1)], CT[0:CR, q, tile_cols(t)], A["Wc"][0:CR, :],
                             start=True, stop=True).then_inc(mix_ready, 1)

        def act_sq(act, b, t):
            act.wait_ge(o_done, TT * b + t + 1)
            nc.scalar.activation(sq[:, t, :], O[:, t, :], ACT.Square, accum_out=ss[:, t:t + 1]).then_inc(sq_done, 1)

        def dve_mix(dve, b, q, t):
            n = (b * TT + t) * MCH
            dve.wait_ge(mix_ready, TT * b + t + 1)
            if t == 0:
                dve.wait_ge(base_done, 2 * b + 2)
                nc.vector.tensor_copy(ybus[:, :], ysum[:, q:q + 1])
            nc.vector.reciprocal(rec[:, :], psM[:, D:2 * D + 2:D + 1]).then_inc(mchain, 1)
            dve.wait_ge(mchain, n + 1)
            nc.vector.tensor_tensor(coef[:, t, :], rec[:, :], pl[:, q, :], ALU.mult).then_inc(mchain, 1)
            dve.wait_ge(mchain, n + 2)
            nc.vector.scalar_tensor_tensor(out=O[:, t, :], in0=psM[:, 0:D], scalar=coef[:, t, 0:1],
                                           in1=base[:, q, t, :], op0=ALU.mult, op1=ALU.add).then_inc(mchain, 1)
            dve.wait_ge(mchain, n + 3)
            nc.vector.scalar_tensor_tensor(out=O[:, t, :], in0=psM[:, D + 1:2 * D + 1], scalar=coef[:, t, 1:2],
                                           in1=O[:, t, :], op0=ALU.mult, op1=ALU.add).then_inc(o_done, 1)

        def dve_ms(dve, b):
            dve.wait_ge(sq_done, TT * b + TT)
            nc.vector.tensor_scalar(ms[:, :], ss[:, :], 1.0 / D, FP32_EPS, ALU.mult, ALU.add).then_inc(ms_done, 1)

        def pool_rr(pool, b):
            pool.wait_ge(ms_done, b + 1)
            nc.gpsimd.tensor_tensor(rr[:, :], ms[:, :], A["half"][:, :], ALU.pow).then_inc(rr_done, 1)

        def dve_o2(dve, b):
            dve.wait_ge(rr_done, b + 1)
            for t in range(TT):
                i = nc.vector.scalar_tensor_tensor(out=O[:, t, :], in0=O[:, t, :], scalar=rr[:, t:t + 1],
                                                   in1=A["w_out"][:, :], op0=ALU.mult, op1=ALU.mult)
            i.then_inc(o2_done, 1)

        def pe_bus(pe, b, k):
            if k == 0:
                pe.wait_ge(o2_done, b + 1)
                for t in range(TT):
                    i = nc.tensor.matmul(psM[:, 0:1], O[:, t, :], A["ones"][:, 0:1], start=(t == 0), stop=(t == TT - 1))
            else:
                pe.wait_ge(bus_done, 3 * b + k)
                if k == 1:
                    i = nc.tensor.matmul(psM[:, 0:1], A["compress"][:, :], busc[:, 0:1], start=True, stop=True)
                elif k == 2:
                    i = nc.tensor.matmul(psM[:, 0:1], A["publish"][:, :], busc[:, 1:2], start=True, stop=True)
                else:
                    i = nc.tensor.matmul(psM[:, 0:D], pubb[:, :], A["expand"][:, :], start=True, stop=True)
            i.then_inc(bus_ready, 1)

        def dve_bus(dve, b, k):
            dve.wait_ge(bus_ready, 4 * b + k + 1)
            if k == 0:
                i = nc.vector.tensor_scalar(busc[:, 0:1], psM[:, 0:1], ybus[:, :], 1.0 / SEQ, ALU.add, ALU.mult)
            elif k == 1:
                i = nc.vector.tensor_copy(busc[:, 1:2], psM[:, 0:1])
            else:
                i = nc.vector.tensor_scalar(pubb[:, :], A["ones"][:, :], psM[:, 0:1], 0.1, ALU.mult, ALU.mult)
            i.then_inc(bus_done, 1)

        def dve_x(dve, b):
            k = xtiles(b)
            dve.wait_ge(xr_done, b + 1)
            dve.wait_ge(o2_done, b + 1)
            nc.vector.tensor_tensor(O[:, :, :], X[:, k, :], O[:, :, :], ALU.add).then_inc(xa_done, 1)
            dve.wait_ge(xa_done, 2 * b + 1)
            dve.wait_ge(bus_ready, 4 * b + 4)
            nc.vector.tensor_tensor(O[:, :, :], O[:, :, :], psM[:, 0:D].unsqueeze(1).broadcast_to((P, TT, D)),
                                    ALU.add).then_inc(xa_done, 1)
            dve.wait_ge(xa_done, 2 * b + 2)
            for t in range(TT):
                i = nc.vector.bn_stats(bst[:, t, :], O[:, t, :])
            i.then_inc(bst_done, 1)
            dve.wait_ge(bst_done, b + 1)
            nc.vector.tensor_scalar(X[:, k, :], O[:, :, :], 1.0, None, ALU.mult)
            for t in range(TT):
                i = nc.vector.bn_aggr(mv[:, t, :], bst[:, t, :])
            i.then_inc(mv_done, 1)
            dve.wait_ge(mv_done, b + 1)
            nc.vector.tensor_scalar(stats[:, k, :], mv[:, :, :], 1.0, None, ALU.mult)

        def pe_turn(pe, b, q, first, last):
            for u in range(UNITS):
                pe_st(pe, b, q, u, first)
                if u >= 1:
                    pe_pv(pe, b, q, u - 1, first)
                if not first:
                    if u < TT:
                        pe_mix(pe, b - 1, 1 - q, u)
                    if 9 <= u < 13:
                        pe_bus(pe, b - 1, u - 9)
                if not last:
                    if u in (0, 1):
                        pe_xT(pe, b + 1, 1 - q, u, False)
                    if u in (2, 3, 4, 5):
                        pe_proj(pe, b + 1, 2 * u - 4)
                        pe_proj(pe, b + 1, 2 * u - 3)
                    if u == 6:
                        pe_v_r1(pe, b + 1, 1 - q)
                    if u == 7:
                        pe_r2(pe, b + 1)
                    if u == 8:
                        pe_r3(pe, b + 1)
                    if u in (14, 15):
                        pe_base(pe, b + 1, u - 14, not first)
                    if u >= 8:
                        pe_p1(pe, b + 1, 1 - q, 2 * u - 16)
                        pe_p1(pe, b + 1, 1 - q, 2 * u - 15)
            pe_pv(pe, b, q, UNITS - 1, first)
            if not last:
                for g in range(4):
                    pe_row(pe, b + 1, g)

        def act_turn(act, b, q, first, last):
            for u in range(UNITS):
                act_ex(act, b, u, first)
                if not first and 1 <= u <= TT:
                    act_sq(act, b - 1, u - 1)
                if not last:
                    if u in (0, 1):
                        act_xT(act, b + 1, 1 - q, u, False)
                    if u in (2, 3, 4, 5):
                        act_proj(act, b + 1, 2 * u - 4, False)
                        act_proj(act, b + 1, 2 * u - 3, False)
                    if u == 6:
                        act_r1(act, b + 1)
                    if u == 7:
                        act_r2(act, b + 1)
                    if u in (14, 15):
                        act_base(act, b + 1, 1 - q, u - 14)
            if not last:
                for g in range(4):
                    act_row(act, b + 1, 1 - q, g)

        def dve_turn(dve, b, q, first, last):
            for u in range(UNITS):
                if u >= KP and u % KP == 1:
                    dve_ct(dve, b, q, u // KP - 1)
                if not first and u < TT:
                    dve_mix(dve, b - 1, 1 - q, u)
                if not last:
                    if u == 0:
                        dve_y(dve, b + 1, 1 - q, False)
                    if u in (2, 3, 4, 5):
                        dve_proj(dve, b + 1, 1 - q, 2 * u - 4)
                        dve_proj(dve, b + 1, 1 - q, 2 * u - 3)
                    if u == 5:
                        dve_ema(dve, b + 1, False)
                    if u == 6:
                        dve_v(dve, b + 1, 1 - q)
                        dve_r1(dve, b + 1, 1 - q)
                    if u == 7:
                        dve_r2(dve, b + 1, 1 - q)
                    if u == 8:
                        dve_r3(dve, b + 1, 1 - q)
                if not first:
                    if u == 8:
                        dve_ms(dve, b - 1)
                        dve_o2(dve, b - 1)
                    if 9 <= u < 12:
                        dve_bus(dve, b - 1, u - 9)
                    if u == 13:
                        dve_x(dve, b - 1)
                if not last and u >= 8:
                    dve_p1(dve, b + 1, 2 * u - 16)
                    dve_p1(dve, b + 1, 2 * u - 15)
            dve_ct(dve, b, q, 3)

        def pool_turn(pool, b, q, first, last):
            if not last:
                for h in (0, 1):
                    pool_xTl(pool, b + 1, 1 - q, h)
            if not first:
                pool_rr(pool, b - 1)

        def over_batches(eng, turn):
            turn(eng, 0, 0, True, False)
            turn(eng, 1, 1, False, False)
            with eng.Fori(2, BATCH - 2, 2) as b:
                turn(eng, b, 0, False, False)
                turn(eng, b + 1, 1, False, False)
            turn(eng, BATCH - 2, 0, False, False)
            turn(eng, BATCH - 1, 1, False, True)

        end, eq = BATCH - 1, (BATCH - 1) % 2
        block = ctx.enter_context(nc.Block("at_block"))

        @block.tensor
        def _(pe):
            for h in (0, 1):
                pe_xT(pe, 0, 0, h, True)
            for k in range(8):
                pe_proj(pe, 0, k)
            pe_v_r1(pe, 0, 0)
            pe_r2(pe, 0)
            pe_r3(pe, 0)
            for v in range(UNITS):
                pe_p1(pe, 0, 0, v)
            for h in (0, 1):
                pe_base(pe, 0, h, False)
            for g in range(4):
                pe_row(pe, 0, g)
            over_batches(pe, pe_turn)
            for t in range(TT):
                pe_mix(pe, end, eq, t)
            for k in range(4):
                pe_bus(pe, end, k)

        @block.scalar
        def _(act):
            for h in (0, 1):
                act_xT(act, 0, 0, h, True)
            for k in range(8):
                act_proj(act, 0, k, True)
            act_r1(act, 0)
            act_r2(act, 0)
            for h in (0, 1):
                act_base(act, 0, 0, h)
            for g in range(4):
                act_row(act, 0, 0, g)
            over_batches(act, act_turn)
            for t in range(TT):
                act_sq(act, end, t)

        @block.vector
        def _(dve):
            nc.vector.memset(CT[:, :, :].bitcast(mybir.dt.uint32), 0)
            dve_y(dve, 0, 0, True)
            for k in range(8):
                dve_proj(dve, 0, 0, k)
            dve_ema(dve, 0, True)
            dve_v(dve, 0, 0)
            dve_r1(dve, 0, 0)
            dve_r2(dve, 0, 0)
            dve_r3(dve, 0, 0)
            for v in range(UNITS):
                dve_p1(dve, 0, v)
            over_batches(dve, dve_turn)
            for t in range(TT):
                dve_mix(dve, end, eq, t)
            dve_ms(dve, end)
            dve_o2(dve, end)
            for k in range(3):
                dve_bus(dve, end, k)
            dve_x(dve, end)

        @block.gpsimd
        def _(pool):
            for h in (0, 1):
                pool_xTl(pool, 0, 0, h)
            over_batches(pool, pool_turn)
            pool_rr(pool, end)


def program(nc, ins, out):
    T, D = ins["x"].shape
    E = ins["WrT"].shape[1]
    F = ins["WgT"].shape[1] // E
    BATCH = ins["batches"]
    DH = ins["wv"].shape[1]
    TILES = T // P
    SEQ = T // BATCH
    with ExitStack() as ctx:
        def sb(name, shape, dt=F32, where=None):
            return (where or ctx).enter_context(nc.sbuf_tensor(name, shape, dt))

        persist = {
            "X": sb("X", [P, TILES, D]),
            "stats": sb("stats", [P, TILES, 2]),
            "rstd": sb("rstd", [P, TILES]),
            "rmsin": sb("rmsin", [P, TILES]),
            "ident": sb("ident", [P, P]),
            "x": ins["x"].rearrange("(t p) d -> p t d", p=P),
            "out": out.rearrange("(t p) d -> p t d", p=P),
        }

        def moe(tag, first):
            with ExitStack() as here:
                for n in ("WgH", "WgL", "WuH", "WuL", "WdH", "WdL"):
                    persist[n] = sb(tag + n, [P, E * F], F32R, here)
                persist["WrH"], persist["WrL"] = (sb(tag + n, [P, E], F32R, here) for n in ("WrH", "WrL"))
                persist["sel"] = sb(tag + "sel", [2 * E, E, P], F32R, here)
                persist["later"] = sb(tag + "later", [P, 4 * E, E], F32, here)
                moe_constants(nc, tag, persist, ins, T, D, E, F, first)
                norm_phase(nc, tag, persist, T, False)
                ffn_phase(nc, tag, persist, T, D, E, F, not first)

        moe("ffn1_", True)
        with ExitStack() as here:
            A = {"DH": DH}
            for n in ("mixA", "mixB", "wv", "w1", "w2", "b2", "w_in", "w_out", "slam", "lm", "lmT", "compress",
                      "publish", "expand", "lambdas"):
                A["lam" if n == "lambdas" else n] = sb("a_" + n, list(ins[n].shape), F32, here)
            A["wpH"], A["wpL"] = (sb("a_" + n, [P, 4 * P], F32R, here) for n in ("wpH", "wpL"))
            A["mpad"] = sb("a_mpad", [P, 2 * SEQ // P, 3 * DH + 1], F32, here)
            A["V1"] = sb("a_V1", [P, 2, SEQ // P, DH + 1], F32, here)
            A["half"] = sb("a_half", [P, SEQ // P], F32, here)
            A["ones"] = sb("a_ones", [P, P], F32, here)
            A["Wc"] = sb("a_Wc", [P, 2 * (D + 1)], F32, here)
            A["sgnQ"], A["sgnK"], A["oml"] = (sb("a_" + n, [P, 1], F32, here) for n in ("sgnQ", "sgnK", "oml"))
            A["Q"], A["K"] = (sb("a_" + n, [P, 2, 2, SEQ], F32R, here) for n in ("Q", "K"))
            persist["attn"] = A
            attention_constants(nc, persist, ins)
            norm_phase(nc, "at_", persist, T, True)
            attention_phase(nc, persist, T, BATCH)
        moe("ffn2_", False)


def kernel(**inputs):
    import numpy as np
    import concourse.bacc as bacc
    from concourse import mybir as mb
    from concourse.bass_utils import run_bass_kernel_spmd as run

    nc = bacc.Bacc("TRN2", target_bir_lowering=False, num_devices=1)
    g = {k: np.asarray(v) for k, v in inputs.items()}
    E, F, D = g["L0_ffn_Wg"].shape
    B, S, _ = g["L0_attn_x"].shape

    def rows(a):
        return np.broadcast_to(a, (128, a.size))

    arrays = {
        "x": g["L0_attn_x"].reshape(B * S, D),
        "WrT": g["L0_ffn_Wr"].T,
        "WgT": g["L0_ffn_Wg"].transpose(2, 0, 1).reshape(D, E * F),
        "WuT": g["L0_ffn_Wu"].transpose(2, 0, 1).reshape(D, E * F),
        "WdT": g["L0_ffn_Wd"].reshape(E, D, F // 128, 128).transpose(3, 0, 2, 1).reshape(128, E * F // 128 * D),
        "wproj": np.concatenate([np.tile(g["L0_attn_slr_" + n], (1, 4)) for n in ("wq1", "wk1", "wq2", "wk2")], axis=1),
        "woT": g["L0_attn_slr_wo"].T,
        "mixA": g["L0_attn_mix_w"][:D],
        "mixB": g["L0_attn_mix_w"][D:],
        "wv": g["L0_attn_slr_wv"],
        "w1": g["L0_attn_router_w1"],
        "w2": g["L0_attn_router_w2"],
        "b2": rows(g["L0_attn_router_b2"]),
        "w_in": rows(g["L0_attn_w_norm_in"]),
        "w_out": rows(g["L0_attn_w_norm_out"]),
        "slam": rows(g["L0_attn_slr_lam"].reshape(1)),
        "lambdas": np.repeat(g["L0_attn_lambdas"], D // g["L0_attn_lambdas"].size).reshape(D, 1),
        "lm": g["L0_attn_landmarks"],
        "lmT": g["L0_attn_landmarks"].T,
        "compress": g["L0_attn_bus_compress"],
        "publish": g["L0_attn_bus_publish"],
        "expand": g["L0_attn_bus_expand"],
    }
    arrays = {k: np.ascontiguousarray(v) for k, v in arrays.items()}
    ins = {k: nc.dram_tensor("in_" + k, v.shape, mb.dt.from_np(v.dtype), kind="ExternalInput").ap() for k, v in arrays.items()}
    ins["batches"] = B
    out = nc.dram_tensor("out", (B * S, D), mb.dt.float32, kind="ExternalOutput").ap()
    program(nc, ins, out)
    r = run(nc, [{"in_" + k: v for k, v in arrays.items()}], core_ids=[0])
    return r.results[0]["out"].reshape(B, S, D)
```

```python
from contextlib import ExitStack

import concourse.bass as bass
from concourse import mybir

ALU = mybir.AluOpType
ACT = mybir.ActivationFunctionType
AX = mybir.AxisListType
F32 = mybir.dt.float32
F32R = mybir.dt.float32r
U32 = mybir.dt.uint32

P = 128
LN_EPS = 1e-5
FP32_EPS = 1.1920929e-07


def over(ap, axis, shape):
    return ap.unsqueeze(axis).broadcast_to(shape)


def ffn_phase(nc, tag, persist, T, D, E, F, finish):
    X, rstd, stats = persist["X"], persist["rstd"], persist["stats"]
    ident = persist["ident"]
    WrH, WrL, later = persist["WrH"], persist["WrL"], persist["later"]
    WgH, WgL, WuH, WuL, WdH, WdL = (persist[n] for n in ("WgH", "WgL", "WuH", "WuL", "WdH", "WdL"))
    before, ones_r, jt = persist["before"], persist["ones_r"], persist["jt"]
    xsort, ysort = persist["xsort"], persist["ysort"]
    GROUPS, GT, NT = persist["GROUPS"], persist["GT"], persist["NT"]
    FS = F // P
    PAIRS = NT // 2
    IN_FLIGHT = 2 * GT
    MAGIC = 1.5 * 2.0 ** 23

    with ExitStack() as ctx:
        def sb(name, shape, dt=F32):
            return ctx.enter_context(nc.sbuf_tensor(tag + name, shape, dt))

        def sem(name):
            return nc.alloc_semaphore(tag + name)

        xn = sb("xn", [P, GT, D])
        xTh, xTl = sb("xTh", [P, 4 * P], F32R), sb("xTl", [P, 4 * P], F32R)
        lg = sb("lg", [P, GT, E])
        ex = sb("ex", [P, GT, E])
        red = sb("red", [P, 8, GT])
        beats, ties = sb("beats", [P, GT * E, E]), sb("ties", [P, GT * E, E])
        rank = sb("rank", [P, GT, E])
        mask = sb("mask", [P, 2 * GT * E], F32R)
        pick1, pick2 = sb("pick1", [P, GT, E]), sb("pick2", [P, GT, E])
        slot = sb("slot", [P, GT, E])
        ends = sb("ends", [P, 5, E])
        posf = sb("posf", [P, 2 * GT])
        sidx = sb("sidx", [P, 2 * GT], U32)
        gidx = sb("gidx", [P, 2 * GT], U32)
        pos_all = sb("pos_all", [P, GROUPS * 2 * GT])
        comb_all = sb("comb_all", [P, GROUPS * 2 * GT])
        past = sb("past", [1, NT, E])
        pastn = sb("pastn", [1, NT])
        expert = sb("expert", [1, GROUPS * NT], U32)
        gbase = sb("gbase", [P, 1])
        xs = sb("xs", [P, 2, 2, D])
        xsh, xsl = sb("xsh", [P, 2, P], F32R), sb("xsl", [P, 2, P], F32R)
        rg, h = sb("rg", [P, 2, F]), sb("h", [P, 2, F])
        hh, hl = sb("hh", [P, 2, F], F32R), sb("hl", [P, 2, F], F32R)
        ysb = sb("ysb", [P, 2, 2, D])
        yg = sb("yg", [P, 2, GT, D])
        xw = sb("xw", [P, 2, D])
        settled = sb("settled", [P, 2])
        bst, mv = sb("bst", [P, GT, 6]), sb("mv", [P, GT, 2])

        def bank(name, n=1):
            return ctx.enter_context(nc.psum_tensor(tag + name, [P, n, 512], F32))

        psG, psU, psH, psT, psY, psR = bank("psG", 2), bank("psU"), bank("psH", 2), bank("psT"), bank("psY"), bank("psR")

        xs_in = [sem("xs_in0"), sem("xs_in1")]
        xsT, xsh_done, xsl_done = sem("xsT"), sem("xsh_done"), sem("xsl_done")
        gate_ready, up_ready = sem("gate_ready"), sem("up_ready")
        relu_done, hid_done = sem("relu_done"), sem("hid_done")
        hidT, hh_done, hl_done = sem("hidT"), sem("hh_done"), sem("hl_done")
        down_ready, y_copied = sem("down_ready"), sem("y_copied")
        y_stored = [sem("y_stored0"), sem("y_stored1")]
        norm_done = sem("norm_done")
        normT, xTh_done, xTl_done = sem("normT"), sem("xTh_done"), sem("xTl_done")
        logits_ready, logits_done = sem("logits_ready"), sem("logits_done")
        shifted, exp_done = sem("shifted"), sem("exp_done")
        mask_done, ranks_ready = sem("mask_done"), sem("ranks_ready")
        chain = sem("chain")
        slots_done, experts_done = sem("slots_done"), sem("experts_done")
        scattered = sem("scattered")
        io_go = sem("io_go")
        scatter_go, gather_go = sem("scatter_go"), sem("gather_go")
        gidx_done = sem("gidx_done")
        gathered = [sem(f"gathered{k}") for k in range(GT // 4)]
        half_added, x_done = sem("half_added"), sem("x_done")
        bst_done, mv_done = sem("bst_done"), sem("mv_done")
        out_done = sem("out_done")
        QC = GT // 4
        LINKS = 27

        def cut(start, size):
            return slice(start, start + size) if isinstance(start, int) else bass.ds(start, size)

        def pe_three(out, ah, al, bh, bl, first=True, last=True):
            nc.tensor.matmul(out, ah, bh, start=first, stop=False)
            nc.tensor.matmul(out, al, bh, start=False, stop=False)
            return nc.tensor.matmul(out, ah, bl, start=False, stop=last)

        def pe_xsT(pe, g, j):
            n, pair = g * NT + j, j // 2
            if j % 2 == 0:
                pe.wait_ge(xs_in[pair % 2], 16 * (g * (PAIRS // 2) + pair // 2 + 1))
            if not (isinstance(n, int) and n == 0):
                pe.wait_ge(xsl_done, n)
            nc.tensor.transpose(psT[:, 0, 0:P], xs[:, pair % 2, j % 2, :], ident[:, :]).then_inc(xsT, 1)

        def pe_expert(pe, g, j):
            return pe.value_load(expert[0:1, cut(g * NT + j, 1)], min_val=0, max_val=E - 1)

        def pe_up(pe, g, j, e, head):
            n = g * NT + j
            pe.wait_ge(xsl_done, n + 1)
            if not (head and j < 2):
                pe.wait_ge(relu_done, n - 1)
            ah, al, w = xsh[:, j % 2, :], xsl[:, j % 2, :], bass.ds(e * F, F)
            pe_three(psG[:, j % 2, :], ah, al, WgH[:, w], WgL[:, w]).then_inc(gate_ready, 1)
            if not (head and j < 1):
                pe.wait_ge(hid_done, n)
            pe_three(psU[:, 0, :], ah, al, WuH[:, w], WuL[:, w]).then_inc(up_ready, 1)

        def pe_hidT(pe, g, j, head):
            n = g * NT + j
            pe.wait_ge(hid_done, n + 1)
            if not (head and j < 2):
                pe.wait_ge(hl_done, n - 1)
            for f in range(FS):
                i = nc.tensor.transpose(psH[:, j % 2, f * P:f * P + P], h[:, j % 2, f * P:f * P + P], ident[:, :])
            i.then_inc(hidT, 1)

        def pe_down(pe, g, j, e, head):
            n = g * NT + j
            pe.wait_ge(hl_done, n + 1)
            if not (head and j < 1):
                pe.wait_ge(y_copied, n)
            for f in range(FS):
                k, w = slice(f * P, f * P + P), bass.ds(e * F + f * P, P)
                i = pe_three(psY[:, 0, 0:D], hh[:, j % 2, k], hl[:, j % 2, k], WdH[:, w], WdL[:, w],
                             f == 0, f == FS - 1)
            i.then_inc(down_ready, 1)

        def act_xsh(act, g, j):
            act.wait_ge(xsT, g * NT + j + 1)
            nc.scalar.activation(xsh[:, j % 2, :], psT[:, 0, 0:P], ACT.Copy).then_inc(xsh_done, 1)

        def act_relu(act, g, j, head):
            n = g * NT + j
            act.wait_ge(gate_ready, n + 1)
            if not (head and j < 2):
                act.wait_ge(hid_done, n - 1)
            nc.scalar.activation(rg[:, j % 2, :], psG[:, j % 2, :], ACT.Relu).then_inc(relu_done, 1)

        def act_hh(act, g, j, head):
            n = g * NT + j
            act.wait_ge(hidT, n + 1)
            if not (head and j < 2):
                act.wait_ge(down_ready, n - 1)
            nc.scalar.activation(hh[:, j % 2, :], psH[:, j % 2, :], ACT.Copy).then_inc(hh_done, 1)

        def act_y(act, g, j, head):
            pair = j // 2
            act.wait_ge(down_ready, g * NT + j + 1)
            if j % 2 == 0 and not (head and j < 4):
                act.wait_ge(y_stored[pair % 2], 16 * (g * (PAIRS // 2) + pair // 2))
            nc.scalar.activation(ysb[:, pair % 2, j % 2, :], psY[:, 0, 0:D], ACT.Copy).then_inc(y_copied, 1)

        def dve_xsl(dve, g, j):
            dve.wait_ge(xsh_done, g * NT + j + 1)
            nc.vector.tensor_tensor(xsl[:, j % 2, :], psT[:, 0, 0:P], xsh[:, j % 2, :].bitcast(F32),
                                    ALU.subtract).then_inc(xsl_done, 1)

        def dve_hid(dve, g, j, head):
            n = g * NT + j
            dve.wait_ge(relu_done, n + 1)
            dve.wait_ge(up_ready, n + 1)
            if not (head and j < 2):
                dve.wait_ge(hidT, n - 1)
            nc.vector.tensor_tensor(h[:, j % 2, :], rg[:, j % 2, :], psU[:, 0, :], ALU.mult).then_inc(hid_done, 1)

        def dve_hl(dve, g, j):
            dve.wait_ge(hh_done, g * NT + j + 1)
            nc.vector.tensor_tensor(hl[:, j % 2, :], psH[:, j % 2, :], hh[:, j % 2, :].bitcast(F32),
                                    ALU.subtract).then_inc(hl_done, 1)

        def sp_load(sp, g, pair, head):
            q = g * PAIRS + pair
            here = (g & 1) * PAIRS + pair
            rows = xsort.rearrange("(t p) d -> p t d", p=P)[:, cut(2 * here, 2), :]
            if pair == 0:
                sp.wait_ge(scattered, (g + 1) * 16 * IN_FLIGHT)
            if not (head and pair < 2):
                sp.wait_ge(xsT, 2 * q - 2)
            sp.sem_inc(io_go, 1)
            sp.dma_start(xs[:, pair % 2, :, :], rows)\
                .then_inc(xs_in[pair % 2], 16)

        def sp_store(sp, g, pair):
            q = g * PAIRS + pair
            here = (g & 1) * PAIRS + pair
            rows = ysort.rearrange("(t p) d -> p t d", p=P)[:, cut(2 * here, 2), :]
            if pair == 0 and not (isinstance(g, int) and g < 2):
                sp.wait_ge(gidx_done, g)
            sp.wait_ge(y_copied, 2 * q + 2)
            sp.sem_inc(io_go, 1)
            sp.dma_start(rows, ysb[:, pair % 2, :, :])\
                .then_inc(y_stored[pair % 2], 16)

        def dve_norm(dve, g, start):
            if not start:
                dve.wait_ge(scattered, g * 16 * IN_FLIGHT)
            for t in range(GT):
                k = cut(g * GT + t, 1)
                i = nc.vector.tensor_scalar(xn[:, t:t + 1, :], X[:, k, :], stats[:, k, 0:1], rstd[:, k],
                                            ALU.subtract, ALU.mult)
            i.then_inc(norm_done, 1)

        def pe_normT(pe, g, c, start):
            if c == 0:
                pe.wait_ge(norm_done, g + 1)
                if not start:
                    pe.wait_ge(slots_done, g)
                    pe.wait_ge(experts_done, g)
            else:
                pe.wait_ge(logits_done, QC * g + c)
            for t in range(4):
                i = nc.tensor.transpose(psR[:, 0, t * P:t * P + P], xn[:, 4 * c + t, :], ident[:, :])
            i.then_inc(normT, 1)

        def act_xTh(act, g, c):
            act.wait_ge(normT, QC * g + c + 1)
            nc.scalar.activation(xTh[:, :], psR[:, 0, :], ACT.Copy).then_inc(xTh_done, 1)

        def dve_xTl(dve, g, c):
            dve.wait_ge(xTh_done, QC * g + c + 1)
            nc.vector.tensor_tensor(xTl[:, :], psR[:, 0, :], xTh[:, :].bitcast(F32), ALU.subtract).then_inc(xTl_done, 1)

        def pe_logits(pe, g, c):
            pe.wait_ge(xTl_done, QC * g + c + 1)
            for t in range(4):
                k = slice(t * P, t * P + P)
                i = pe_three(psR[:, 0, t * E:t * E + E], xTh[:, k], xTl[:, k], WrH[:, :], WrL[:, :])
            i.then_inc(logits_ready, 1)

        def dve_logits(dve, g, c):
            dve.wait_ge(logits_ready, QC * g + c + 1)
            nc.vector.tensor_copy(lg[:, 4 * c:4 * c + 4, :].rearrange("p t e -> p (t e)"),
                                  psR[:, 0, 0:4 * E]).then_inc(logits_done, 1)

        def act_exp(act, g):
            act.wait_ge(shifted, g + 1)
            nc.scalar.activation(ex[:, :, :], lg[:, :, :], ACT.Exp).then_inc(exp_done, 1)

        def along(row):
            return over(red[:, row, :], 2, (P, GT, E))

        def flat(t):
            return t[:, :, :].rearrange("p t e -> p (t e)")

        def dve_route(dve, g, step):
            count = [(0, 1, 4, 9, 16, 19, 24, 25, LINKS)[step]]
            upto = (0, 1, 4, 9, 16, 19, 24, 25, LINKS)[step + 1]

            def link(ins):
                count[0] += 1
                ins.then_inc(chain, 1)
                dve.wait_ge(chain, g * LINKS + count[0])

            if step == 0:
                dve.wait_ge(logits_done, QC * g + QC)
                link(nc.vector.tensor_reduce(red[:, 0, :], lg[:, :, :], AX.X, ALU.max))
                nc.vector.tensor_tensor(lg[:, :, :], lg[:, :, :], along(0), ALU.subtract).then_inc(shifted, 1)
            elif step == 1:
                dve.wait_ge(exp_done, g + 1)
                link(nc.vector.tensor_reduce(red[:, 1, :], ex[:, :, :], AX.X, ALU.add))
                link(nc.vector.reciprocal(red[:, 2, :], red[:, 1, :]))
                link(nc.vector.tensor_tensor(lg[:, :, :], ex[:, :, :], along(2), ALU.mult))
            elif step == 2:
                mine = over(flat(lg), 2, (P, GT * E, E))
                for t in range(GT):
                    other, k = lg[:, t:t + 1, :].broadcast_to((P, E, E)), slice(t * E, t * E + E)
                    nc.vector.tensor_tensor(beats[:, k, :], other, mine[:, k, :], ALU.is_gt)
                    i = nc.vector.tensor_tensor(ties[:, k, :], other, mine[:, k, :], ALU.is_equal)
                link(i)
                link(nc.vector.tensor_tensor(ties[:, :, :], ties[:, :, :], later[:, :, :], ALU.mult))
                link(nc.vector.tensor_tensor(beats[:, :, :], beats[:, :, :], ties[:, :, :], ALU.add))
                link(nc.vector.tensor_reduce(flat(rank), beats[:, :, :], AX.X, ALU.add))
                nc.vector.tensor_scalar(mask[:, GT * E:], flat(rank), 1.5, None, ALU.is_lt).then_inc(mask_done, 1)
                count[0] += 1
                dve.wait_ge(mask_done, g + 1)
                dve.sem_inc(chain, 1)
            elif step == 3:
                for r, (pick, place) in enumerate(((pick1, 0.0), (pick2, 1.0))):
                    link(nc.vector.scalar_tensor_tensor(out=flat(pick), in0=flat(rank), scalar=place, in1=flat(lg),
                                                        op0=ALU.is_equal, op1=ALU.mult))
                    link(nc.vector.tensor_reduce(red[:, 3 + r, :], pick[:, :, :], AX.X, ALU.add))
                link(nc.vector.tensor_tensor(red[:, 5, :], red[:, 3, :], red[:, 4, :], ALU.add))
                link(nc.vector.tensor_scalar(red[:, 6, :], red[:, 5, :], FP32_EPS, None, ALU.add))
                link(nc.vector.reciprocal(red[:, 7, :], red[:, 6, :]))
                for r in (0, 1):
                    nc.vector.scalar_tensor_tensor(out=comb_all[:, cut(g * 2 * GT + r * GT, GT)], in0=red[:, 3 + r, :],
                                                   scalar=0.5, in1=red[:, 7, :], op0=ALU.mult, op1=ALU.mult)
            elif step == 4:
                dve.wait_ge(ranks_ready, g + 1)
                link(nc.vector.tensor_scalar(ends[:, 0, :], psR[:, 0, 256:256 + E], P / 2 - 0.5, 1.0 / P,
                                             ALU.add, ALU.mult))
                link(nc.vector.tensor_scalar(ends[:, 1, :], ends[:, 0, :], MAGIC, -MAGIC, ALU.add, ALU.add))
                link(nc.vector.tensor_tensor_scan(out=ends[:, 2, :], data0=persist["one8"][:, :], data1=ends[:, 1, :],
                                                  initial=0.0, op0=ALU.mult, op1=ALU.add))
            elif step == 5:
                link(nc.vector.tensor_tensor(ends[:, 3, :], ends[:, 2, :], ends[:, 1, :], ALU.subtract))
                link(nc.vector.tensor_scalar(ends[:, 4, :], ends[:, 3, :], float(P), gbase[:, 0:1], ALU.mult, ALU.add))
                link(nc.vector.tensor_tensor(slot[:, :, :], psR[:, 0, 0:GT * E].rearrange("p (t e) -> p t e", e=E),
                                             over(ends[:, 4, :], 1, (P, GT, E)), ALU.add))
                for r, (pick, place) in enumerate(((pick1, 0.0), (pick2, 1.0))):
                    i = nc.vector.scalar_tensor_tensor(out=flat(pick), in0=flat(rank), scalar=place, in1=flat(slot),
                                                       op0=ALU.is_equal, op1=ALU.mult)
                link(i)
                for r, pick in enumerate((pick1, pick2)):
                    i = nc.vector.tensor_reduce(posf[:, r * GT:r * GT + GT], pick[:, :, :], AX.X, ALU.add)
                link(i)
            elif step == 6:
                nc.vector.tensor_copy(sidx[:, :], posf[:, :]).then_inc(slots_done, 1)
                nc.vector.tensor_scalar(pos_all[:, cut(g * 2 * GT, 2 * GT)], posf[:, :], 1.0, None, ALU.mult)
                link(nc.vector.tensor_scalar(gbase[:, :], gbase[:, :], -1.0, float(NT * P), ALU.mult, ALU.add))
            else:
                link(nc.vector.tensor_tensor(past[:, :, :], jt[:, :, :], over(ends[0:1, 2, :], 1, (1, NT, E)), ALU.is_ge))
                link(nc.vector.tensor_reduce(pastn[:, :], past[:, :, :], AX.X, ALU.add))
                nc.vector.tensor_scalar(expert[:, cut(g * NT, NT)], pastn[:, :], float(E - 1), None,
                                        ALU.min).then_inc(experts_done, 1)
            assert count[0] == upto, (step, count[0], upto)

        def pe_ranks(pe, g):
            pe.wait_ge(mask_done, g + 1)
            nc.tensor.matmul(psR[:, 0, 0:GT * E], before[:, :], mask[:, GT * E:], start=True, stop=False)
            for d in range(1, GT):
                nc.tensor.matmul(psR[:, 0, 0:GT * E], ones_r[:, :], mask[:, (GT - d) * E:(2 * GT - d) * E],
                                 start=False, stop=d == GT - 1)
            for t in range(GT):
                i = nc.tensor.matmul(psR[:, 0, 256:256 + E], ones_r[:, :], mask[:, (GT + t) * E:(GT + t + 1) * E],
                                     start=t == 0, stop=t == GT - 1)
            i.then_inc(ranks_ready, 1)

        def pool_scatter(pool, g, start):
            pool.wait_ge(slots_done, g + 1)
            if not start:
                pool.wait_ge(scattered, g * 16 * IN_FLIGHT)
                pool.wait_ge(xsT, (g - 1) * NT + 1)
            pool.sem_inc(scatter_go, 1)
            for r in (0, 1):
                for t in range(GT):
                    k = r * GT + t
                    pool.indirect_dma_start(xsort, bass.IndirectOffsetOnAxis(ap=sidx[:, k:k + 1], axis=0),
                                            xn[:, t, :], None).then_inc(scattered, 16)

        def dve_gidx(dve, g):
            nc.vector.tensor_scalar(gidx[:, :], pos_all[:, cut(g * 2 * GT, 2 * GT)], 1.0, None,
                                    ALU.mult).then_inc(gidx_done, 1)

        def pool_gather(pool, g):
            pool.wait_ge(gidx_done, g + 1)
            for b in (0, 1):
                pool.wait_ge(y_stored[b], 16 * (PAIRS // 2) * (g + 1))
            pool.sem_inc(gather_go, 1)
            for t in range(GT):
                for r in (0, 1):
                    k = r * GT + t
                    pool.indirect_dma_start(yg[:, r, t, :], None, ysort,
                                            bass.IndirectOffsetOnAxis(ap=gidx[:, k:k + 1], axis=0))\
                        .then_inc(gathered[t // 4], 16)

        def dve_combine(dve, g, t):
            n, k, c = g * GT + t, cut(g * GT + t, 1), g * 2 * GT + t
            if t % 4 == 0:
                dve.wait_ge(gathered[t // 4], 16 * 8 * (g + 1))
            if t > 0:
                dve.wait_ge(x_done, n)
            nc.vector.scalar_tensor_tensor(out=xw[:, t % 2, :], in0=yg[:, 0, t, :], scalar=comb_all[:, cut(c, 1)],
                                           in1=X[:, k, :].rearrange("p t d -> p (t d)"),
                                           op0=ALU.mult, op1=ALU.add).then_inc(half_added, 1)
            if t > 0 and not finish:
                nc.vector.bn_stats(bst[:, t - 1, :], X[:, cut(n - 1, 1), :].rearrange("p t d -> p (t d)"))
            dve.wait_ge(half_added, n + 1)
            nc.vector.scalar_tensor_tensor(out=X[:, k, :].rearrange("p t d -> p (t d)"), in0=yg[:, 1, t, :],
                                           scalar=comb_all[:, cut(c + GT, 1)], in1=xw[:, t % 2, :],
                                           op0=ALU.mult, op1=ALU.add).then_inc(x_done, 1)

        def dve_stats(dve, g):
            dve.wait_ge(x_done, g * GT + GT)
            nc.vector.tensor_scalar(xw[:, 0:1, :], X[:, cut(g * GT + GT - 1, 1), :], 1.0, None, ALU.mult).then_inc(bst_done, 1)
            dve.wait_ge(bst_done, 2 * g + 1)
            nc.vector.bn_stats(bst[:, GT - 1, :], xw[:, 0, :]).then_inc(bst_done, 1)
            dve.wait_ge(bst_done, 2 * g + 2)
            nc.vector.tensor_copy(settled[:, :], bst[:, 0, 0:2])
            for t in range(GT):
                i = nc.vector.bn_aggr(mv[:, t, :], bst[:, t, :])
            i.then_inc(mv_done, 1)
            dve.wait_ge(mv_done, g + 1)
            nc.vector.tensor_scalar(stats[:, cut(g * GT, GT), :], mv[:, :, :], 1.0, None, ALU.mult)

        AT_CHUNK, AT_SOFTMAX, AT_RANKS = 2, 2 + 2 * QC, 2 + 2 * QC + 6
        AT_COMBINE = NT - GT - 2

        def pe_group(pe, g, first, last, held):
            for j in range(NT):
                if not (last and j == NT - 1):
                    if j < NT - 1:
                        pe_xsT(pe, g, j + 1)
                    else:
                        pe_xsT(pe, g + 1, 0)
                if j == 0:
                    pe.wait_ge(experts_done, g + 1)
                e = pe_expert(pe, g, j)
                pe_up(pe, g, j, e, first)
                if j >= 1:
                    pe_hidT(pe, g, j - 1, first)
                elif not first:
                    pe_hidT(pe, g - 1, NT - 1 + 0, False)
                if j >= 2:
                    pe_down(pe, g, j - 2, pe_expert(pe, g, j - 2), first)
                elif not first:
                    pe_down(pe, g - 1, NT - 2 + j, pe_expert(pe, g - 1, NT - 2 + j), False)
                if not last:
                    c = j - AT_CHUNK
                    if 0 <= c < 2 * QC:
                        (pe_normT(pe, g + 1, c // 2, False) if c % 2 == 0 else pe_logits(pe, g + 1, c // 2))
                    if j == AT_RANKS:
                        pe_ranks(pe, g + 1)

        def act_group(act, g, first, last, held):
            for j in range(NT):
                if j < NT - 1:
                    act_xsh(act, g, j + 1)
                elif not last:
                    act_xsh(act, g + 1, 0)
                act_relu(act, g, j, first)
                if j >= 1:
                    act_hh(act, g, j - 1, first)
                elif not first:
                    act_hh(act, g - 1, NT - 1, False)
                if j >= 2:
                    act_y(act, g, j - 2, first)
                elif not first:
                    act_y(act, g - 1, NT - 2 + j, False)
                if not last:
                    c = j - AT_CHUNK
                    if 0 <= c < 2 * QC and c % 2 == 0:
                        act_xTh(act, g + 1, c // 2)
                    if j == AT_SOFTMAX:
                        act_exp(act, g + 1)

        def dve_group(dve, g, first, last, held):
            for j in range(NT):
                if j < NT - 1:
                    dve_xsl(dve, g, j + 1)
                elif not last:
                    dve_xsl(dve, g + 1, 0)
                dve_hid(dve, g, j, first)
                if j >= 1:
                    dve_hl(dve, g, j - 1)
                elif not first:
                    dve_hl(dve, g - 1, NT - 1)
                if not last:
                    c = j - AT_CHUNK
                    if j == 0:
                        dve_norm(dve, g + 1, False)
                    if 0 <= c < 2 * QC:
                        (dve_xTl(dve, g + 1, c // 2) if c % 2 == 0 else dve_logits(dve, g + 1, c // 2))
                    if AT_SOFTMAX <= j < AT_SOFTMAX + 4:
                        dve_route(dve, g + 1, j - AT_SOFTMAX)
                    if AT_RANKS <= j < AT_RANKS + 4:
                        dve_route(dve, g + 1, j - AT_RANKS + 4)
                if not first:
                    if j == 0:
                        dve_gidx(dve, g - 1)
                    if 0 <= j - AT_COMBINE < GT:
                        dve_combine(dve, g - 1, j - AT_COMBINE)
                    if j == NT - 1 and not finish:
                        dve_stats(dve, g - 1)

        def pool_group(pool, g, first, last, held):
            if not first:
                pool_gather(pool, g - 1)
            if not last:
                pool_scatter(pool, g + 1, False)

        def sp_group(sp, g, first, last, held):
            for pair in range(PAIRS):
                if pair < PAIRS - 1:
                    sp_load(sp, g, pair + 1, first)
                elif not last:
                    sp_load(sp, g + 1, 0, False)
                if pair >= 1:
                    sp_store(sp, g, pair - 1)
                elif not first:
                    sp_store(sp, g - 1, PAIRS - 1)
            if finish and not first:
                sp_out(sp, g - 1)

        def sp_out(sp, g):
            sp.wait_ge(x_done, GT * (g + 1))
            sp.dma_start(persist["out"][:, cut(g * GT, GT), :], X[:, cut(g * GT, GT), :]).then_inc(out_done, 16)

        def over_groups(eng, body):
            held = {}
            body(eng, 0, True, False, held)
            with eng.Fori(1, GROUPS - 1) as g:
                body(eng, g, False, False, held)
            body(eng, GROUPS - 1, False, True, held)

        end = GROUPS - 1
        block = ctx.enter_context(nc.Block(tag + "block"))

        @block.sync
        def _(sp):
            sp_load(sp, 0, 0, True)
            over_groups(sp, sp_group)
            sp_store(sp, end, PAIRS - 1)
            for b in (0, 1):
                sp.wait_ge(y_stored[b], 16 * (PAIRS // 2) * GROUPS)
            if finish:
                sp_out(sp, end)
                sp.wait_ge(out_done, 16 * GROUPS)

        @block.tensor
        def _(pe):
            for c in range(QC):
                pe_normT(pe, 0, c, True)
                pe_logits(pe, 0, c)
            pe_ranks(pe, 0)
            pe_xsT(pe, 0, 0)
            over_groups(pe, pe_group)
            pe_hidT(pe, end, NT - 1, False)
            for j in (NT - 2, NT - 1):
                pe_down(pe, end, j, pe_expert(pe, end, j), False)

        @block.scalar
        def _(act):
            for c in range(QC):
                act_xTh(act, 0, c)
            act_exp(act, 0)
            act_xsh(act, 0, 0)
            over_groups(act, act_group)
            act_hh(act, end, NT - 1, False)
            for j in (NT - 2, NT - 1):
                act_y(act, end, j, False)

        @block.vector
        def _(dve):
            nc.vector.memset(gbase[:, :], 0.0)
            nc.vector.tensor_scalar(mask[:, 0:GT * E], persist["ident"][:, 0:GT * E], 0.0, None, ALU.mult)
            dve_norm(dve, 0, True)
            for c in range(QC):
                dve_xTl(dve, 0, c)
                dve_logits(dve, 0, c)
            for step in range(8):
                dve_route(dve, 0, step)
            dve_xsl(dve, 0, 0)
            over_groups(dve, dve_group)
            dve_hl(dve, end, NT - 1)
            dve_gidx(dve, end)
            for t in range(GT):
                dve_combine(dve, end, t)
            if not finish:
                dve_stats(dve, end)

        @block.gpsimd
        def _(pool):
            pool.wait_ge(persist["cleared"][0], 16 * persist["FILLS"])
            pool.wait_ge(persist["cleared"][1], 3 * 16 * persist["FILLS"])
            pool_scatter(pool, 0, True)
            over_groups(pool, pool_group)
            pool_gather(pool, end)


def moe_constants(nc, tag, persist, ins, T, D, E, F, first):
    X, stats = persist["X"], persist["stats"]
    W = E * F
    TILES = T // P
    with ExitStack() as ctx:
        raw = [ctx.enter_context(nc.sbuf_tensor(tag + f"raw{k}", [P, W], F32)) for k in range(3)]
        wr = ctx.enter_context(nc.sbuf_tensor(tag + "wr", [P, E], F32))
        bst = ctx.enter_context(nc.sbuf_tensor(tag + "bst0", [P, TILES, 6], F32))
        in_w = [ctx.enter_context(nc.semaphore(tag + f"in_w{k}")) for k in range(3)]
        in_x = [ctx.enter_context(nc.semaphore(tag + f"in_x{k}")) for k in range(4)]
        in_wr = ctx.enter_context(nc.semaphore(tag + "in_wr"))
        high = ctx.enter_context(nc.semaphore(tag + "high"))
        bst_ready = ctx.enter_context(nc.semaphore(tag + "bst_ready"))
        made = ctx.enter_context(nc.semaphore(tag + "made"))
        tri = ctx.enter_context(nc.sbuf_tensor(tag + "tri", [P, P], F32))
        ones0 = ctx.enter_context(nc.sbuf_tensor(tag + "ones0", [P, P], F32))
        GT, NT, ZC = persist["GT"], persist["NT"], persist["ZC"]
        zeroed = ctx.enter_context(nc.semaphore(tag + "zeroed"))
        pairs = [("WgH", "WgL", "WgT"), ("WuH", "WuL", "WuT"), ("WdH", "WdL", "WdT")]
        Q = TILES // 4
        block = ctx.enter_context(nc.Block(tag + "setup"))

        @block.sync
        def _(sp):
            sp.dma_start(wr[:, :], ins["WrT"]).then_inc(in_wr, 16)
            for k in range(4 if first else 0):
                sp.dma_start(X[:, k * Q:k * Q + Q, :], persist["x"][:, k * Q:k * Q + Q, :]).then_inc(in_x[k], 16)
            for k in range(3):
                sp.dma_start(raw[k][:, :], ins[pairs[k][2]]).then_inc(in_w[k], 16)

        @block.gpsimd
        def _(pool):
            ident, later, jti = persist["ident"], persist["later"], persist["jti"]
            nc.gpsimd.iota(jti[:, :, :], pattern=[[1, NT], [0, E]], base=0, channel_multiplier=0).then_inc(made, 1)
            nc.gpsimd.memset(ident[:, :], 0.0)
            nc.gpsimd.memset(tri[:, :], 1.0)
            nc.gpsimd.memset(persist["one8"][:, :], 1.0)
            nc.gpsimd.memset(later[:, :, :], 1.0).then_inc(made, 1)
            pool.wait_ge(made, 2)
            nc.gpsimd.affine_select(out=ident[:, :], in_=ident[:, :], compare_op=ALU.not_equal, fill=1.0,
                                    base=0, pattern=[[-1, P]], channel_multiplier=1)
            nc.gpsimd.affine_select(out=tri[:, :], in_=tri[:, :], compare_op=ALU.is_gt, fill=0.0,
                                    base=0, pattern=[[1, P]], channel_multiplier=-1)
            nc.gpsimd.affine_select(out=later[:, :, :].rearrange("p (t e) j -> p t e j", e=E),
                                    in_=later[:, :, :].rearrange("p (t e) j -> p t e j", e=E),
                                    compare_op=ALU.is_gt, fill=0.0, base=0,
                                    pattern=[[0, GT], [1, E], [-1, E]], channel_multiplier=0).then_inc(made, 1)

        @block.scalar
        def _(act):
            def clear(rows, half, signal):
                part = rows[half * NT * P:(half + 1) * NT * P, :].rearrange("(p r) d -> p (r d)", p=P)
                for k in range(persist["FILLS"]):
                    act.dma_start(part[:, k * ZC:k * ZC + ZC], persist["zero"][:, :]).then_inc(signal, 16)

            if first:
                act.wait_ge(zeroed, 1)
                clear(persist["xsort"], 0, persist["cleared"][0])
            act.wait_ge(in_wr, 16)
            nc.scalar.activation(persist["WrH"][:, :], wr[:, :], ACT.Copy).then_inc(high, 1)
            for k in range(3):
                act.wait_ge(in_w[k], 16)
                nc.scalar.activation(persist[pairs[k][0]][:, :], raw[k][:, :], ACT.Copy).then_inc(high, 1)
            if first:
                clear(persist["xsort"], 1, persist["cleared"][1])
                clear(persist["ysort"], 0, persist["cleared"][1])
                clear(persist["ysort"], 1, persist["cleared"][1])
            act.wait_ge(made, 3)
            nc.scalar.activation(persist["before"][:, :], tri[:, :], ACT.Copy)

        @block.vector
        def _(dve):
            if first:
                nc.vector.memset(persist["zero"][:, :].bitcast(U32), 0).then_inc(zeroed, 1)
            nc.vector.memset(ones0[:, :], 1.0).then_inc(zeroed, 1)
            dve.wait_ge(zeroed, 2 if first else 1)
            nc.vector.tensor_copy(persist["ones_r"][:, :], ones0[:, :])
            dve.wait_ge(made, 1)
            nc.vector.tensor_copy(persist["jt"][:, :, :], persist["jti"][:, :, :])
            dve.wait_ge(high, 1)
            nc.vector.tensor_tensor(persist["WrL"][:, :], wr[:, :], persist["WrH"][:, :].bitcast(F32), ALU.subtract)
            for k in range(4 if first else 0):
                dve.wait_ge(in_x[k], 16)
                for t in range(k * Q, k * Q + Q):
                    i = nc.vector.bn_stats(bst[:, t, :], X[:, t, :])
                i.then_inc(bst_ready, 1)
                dve.wait_ge(bst_ready, k + 1)
                for t in range(k * Q, k * Q + Q):
                    nc.vector.bn_aggr(stats[:, t, :], bst[:, t, :])
            for k in range(3):
                dve.wait_ge(high, k + 2)
                nc.vector.tensor_tensor(persist[pairs[k][1]][:, :], raw[k][:, :],
                                        persist[pairs[k][0]][:, :].bitcast(F32), ALU.subtract)


def norm_phase(nc, tag, persist, T, inner):
    stats, rstd = persist["stats"], persist["rstd"]
    TILES = T // P
    with ExitStack() as ctx:
        v = ctx.enter_context(nc.sbuf_tensor(tag + "v", [P, TILES], F32))
        r = ctx.enter_context(nc.sbuf_tensor(tag + "r", [P, TILES], F32))
        q = ctx.enter_context(nc.sbuf_tensor(tag + "q", [P, TILES], F32))
        link = ctx.enter_context(nc.semaphore(tag + "link"))
        block = ctx.enter_context(nc.Block(tag + "norm"))
        LINKS = 6

        @block.scalar
        def _(act):
            for n in range(2 if inner else 1):
                act.wait_ge(link, n * LINKS + 1)
                nc.scalar.activation(r[:, :], v[:, :], ACT.Sqrt).then_inc(link, 1)

        @block.vector
        def _(dve):
            def root(n, out):
                dve.wait_ge(link, n * LINKS + 2)
                nc.vector.reciprocal(q[:, :], r[:, :]).then_inc(link, 1)
                dve.wait_ge(link, n * LINKS + 3)
                nc.vector.tensor_tensor(r[:, :], q[:, :], q[:, :], ALU.mult).then_inc(link, 1)
                dve.wait_ge(link, n * LINKS + 4)
                nc.vector.scalar_tensor_tensor(out=v[:, :], in0=v[:, :], scalar=-0.5, in1=r[:, :],
                                               op0=ALU.mult, op1=ALU.mult).then_inc(link, 1)
                dve.wait_ge(link, n * LINKS + 5)
                nc.vector.scalar_tensor_tensor(out=out, in0=v[:, :], scalar=1.5, in1=q[:, :],
                                               op0=ALU.add, op1=ALU.mult).then_inc(link, 1)
                dve.wait_ge(link, n * LINKS + 6)

            nc.vector.tensor_scalar(v[:, :], stats[:, :, 1], LN_EPS, None, ALU.add).then_inc(link, 1)
            root(0, rstd[:, :])
            if inner:
                squared = ctx.enter_context(nc.semaphore(tag + "squared"))
                nc.vector.tensor_tensor(q[:, :], rstd[:, :], rstd[:, :], ALU.mult).then_inc(squared, 1)
                dve.wait_ge(squared, 1)
                nc.vector.tensor_tensor(r[:, :], q[:, :], stats[:, :, 1], ALU.mult).then_inc(squared, 1)
                dve.wait_ge(squared, 2)
                nc.vector.tensor_scalar(v[:, :], r[:, :], FP32_EPS, None, ALU.add).then_inc(link, 1)
                root(1, persist["rmsin"][:, :])


def attention_constants(nc, persist, ins):
    A = persist["attn"]
    D = ins["mixA"].shape[0]
    with ExitStack() as ctx:
        raw = ctx.enter_context(nc.sbuf_tensor("aw_raw", [P, 4 * P], F32))
        woT = ctx.enter_context(nc.sbuf_tensor("aw_woT", [P, A["DH"]], F32))
        kone = ctx.enter_context(nc.sbuf_tensor("aw_kone", [P, A["K"].shape[-1]], F32))
        ps = ctx.enter_context(nc.psum_tensor("aw_ps", [P, 512], F32))
        loaded = ctx.enter_context(nc.semaphore("aw_loaded"))
        raw_in = ctx.enter_context(nc.semaphore("aw_raw_in"))
        cleared = ctx.enter_context(nc.semaphore("aw_cleared"))
        high = ctx.enter_context(nc.semaphore("aw_high"))
        folded = ctx.enter_context(nc.semaphore("aw_folded"))
        lam_in = ctx.enter_context(nc.semaphore("aw_lam_in"))
        DH = A["DH"]
        block = ctx.enter_context(nc.Block("aw"))

        @block.sync
        def _(sp):
            sp.dma_start(raw[:, :], ins["wproj"]).then_inc(raw_in, 16)
            sp.dma_start(woT[:, :], ins["woT"]).then_inc(loaded, 16)
            sp.dma_start(A["mixA"][:, :], ins["mixA"]).then_inc(loaded, 16)
            sp.dma_start(A["lam"][:, :], ins["lambdas"]).then_inc(lam_in, 16)
            for n in ("mixB", "wv", "w1", "w2", "b2", "w_in", "w_out", "slam", "lm", "lmT", "compress", "publish", "expand"):
                sp.dma_start(A[n][:, :], ins[n]).then_inc(loaded, 16)
            sp.wait_ge(loaded, 16 * 15)

        @block.scalar
        def _(act):
            act.wait_ge(raw_in, 16)
            nc.scalar.activation(A["wpH"][:, :], raw[:, :], ACT.Copy).then_inc(high, 1)

        @block.gpsimd
        def _(pool):
            nc.gpsimd.memset(A["mpad"][:, :, :], 0.0)
            nc.gpsimd.memset(A["V1"][:, :, :, :], 1.0)
            nc.gpsimd.memset(A["half"][:, :], -0.5)
            nc.gpsimd.memset(A["ones"][:, :], 1.0)

        @block.vector
        def _(dve):
            nc.vector.memset(A["Wc"][:, :], 0.0)
            nc.vector.memset(kone[:, :], 1.0)
            nc.vector.memset(A["sgnQ"][:, :], 0.0)
            nc.vector.memset(A["sgnK"][:, :], 0.0).then_inc(cleared, 1)
            dve.wait_ge(cleared, 1)
            nc.vector.memset(A["sgnQ"][DH:2 * DH, :], -1.0)
            nc.vector.memset(A["sgnK"][2 * DH:3 * DH, :], -1.0)
            for m in (0, 1):
                c = m * (D + 1) + D
                nc.vector.memset(A["Wc"][64 * m + DH:64 * m + DH + 1, c:c + 1], 1.0)
            for q in (0, 1):
                for m in (0, 1):
                    nc.vector.tensor_copy(A["K"][96:97, q, m, :], kone[96:97, :])
            dve.wait_ge(high, 1)
            nc.vector.tensor_tensor(A["wpL"][:, :], raw[:, :], A["wpH"][:, :].bitcast(F32), ALU.subtract)
            dve.wait_ge(lam_in, 16)
            nc.vector.tensor_scalar(A["oml"][:, :], A["lam"][:, :], -1.0, 1.0, ALU.mult, ALU.add)
            dve.wait_ge(folded, 1)
            for m in (0, 1):
                nc.vector.tensor_copy(A["Wc"][64 * m:64 * m + DH, m * (D + 1):m * (D + 1) + D], ps[64 * m:64 * m + DH, 0:D])

        @block.tensor
        def _(pe):
            pe.wait_ge(loaded, 16 * 15)
            for m in (0, 1):
                i = nc.tensor.matmul(ps[64 * m:64 * m + DH, 0:D], woT[:, :], A["mixA"][:, :], start=True, stop=True)
            i.then_inc(folded, 1)


def attention_phase(nc, persist, T, BATCH):
    A = persist["attn"]
    X, stats, rstd, ident = persist["X"], persist["stats"], persist["rstd"], persist["ident"]
    rmsin = persist["rmsin"]
    D, DH = 128, A["DH"]
    R = 3 * DH
    SEQ = T // BATCH
    TT = SEQ // P
    H = 512
    SC = float(DH) ** -0.5
    ARC = float(D) ** -0.5
    NL = A["lm"].shape[0]
    with ExitStack() as ctx:
        def sb(name, shape, dt=F32):
            return ctx.enter_context(nc.sbuf_tensor("at_" + name, shape, dt))

        def sem(name):
            return ctx.enter_context(nc.semaphore("at_" + name))

        Y = sb("Y", [P, TT, D])
        ysum = sb("ysum", [P, 2])
        ybus = sb("ybus", [P, 1])
        xn = sb("xn", [P, TT, D])
        xnT = sb("xnT", [P, SEQ])
        xnTh = sb("xnTh", [P, SEQ], F32R)
        xnTl = sb("xnTl", [P, SEQ], F32R)
        projh = sb("projh", [P, 2, H], F32R)
        rsum = sb("rsum", [P, 2])
        ema_in = sb("ema_in", [P, SEQ])
        ssmT = sb("ssmT", [P, SEQ])
        base = sb("base", [P, 2, TT, D])
        Ex = sb("Ex", [P, 2, 2 * H])
        CT = sb("CT", [P, 2, SEQ])
        O = sb("O", [P, TT, D])
        sq = sb("sq", [P, TT, D])
        col = sb("col", [P, 16])
        p3 = sb("p3", [P, 8])
        pl = sb("pl", [P, 2, 2])
        silb = sb("silb", [64, P])
        arow = sb("arow", [1, NL])
        arcn = sb("arcn", [1, 4])
        acol = sb("acol", [NL, 1])
        rec = sb("rec", [P, 2])
        coef = sb("coef", [P, TT, 2])
        ss = sb("ss", [P, TT])
        ms = sb("ms", [P, TT])
        rr = sb("rr", [P, TT])
        busc = sb("busc", [P, 4])
        pubb = sb("pubb", [P, P])
        bst = sb("bst", [P, TT, 6])
        mv = sb("mv", [P, TT, 2])
        psE = ctx.enter_context(nc.psum_tensor("at_psE", [P, 2, 2 * H], F32))
        psS = ctx.enter_context(nc.psum_tensor("at_psS", [P, 2, H], F32))
        psC = ctx.enter_context(nc.psum_tensor("at_psC", [P, H], F32))
        psM = ctx.enter_context(nc.psum_tensor("at_psM", [P, H], F32))

        y_done, xn_done = sem("y_done"), sem("xn_done")
        xT_ready, xT_done, xTh_done = sem("xT_ready"), sem("xT_done"), sem("xTh_done")
        xTl_done = sem("xTl_done")
        proj_ready, projh_done, proj_done = sem("proj_ready"), sem("projh_done"), sem("proj_done")
        v_ready, v_done = sem("v_ready"), sem("v_done")
        r1_ready, r1_exp, r1_done = sem("r1_ready"), sem("r1_exp"), sem("r1_done")
        r1_copied = sem("r1_copied")
        arc_max, arc_exp = sem("arc_max"), sem("arc_exp")
        r2_ready, r2_shift, r2_exp, r2_done = sem("r2_ready"), sem("r2_shift"), sem("r2_exp"), sem("r2_done")
        r3_ready, r3_done = sem("r3_ready"), sem("r3_done")
        rchain = sem("rchain")
        ema_scaled, ema_done = sem("ema_scaled"), sem("ema_done")
        p1_ready, p1_done = sem("p1_ready"), sem("p1_done")
        row_ready, row_done = sem("row_ready"), sem("row_done")
        st_ready, ex_done, pv_done = sem("st_ready"), sem("ex_done"), sem("pv_done")
        ct_done = sem("ct_done")
        mix_ready = sem("mix_ready")
        base_ready, base_done = sem("base_ready"), sem("base_done")
        xr_done = sem("xr_done")
        mchain = sem("mchain")
        o_done, sq_done = sem("o_done"), sem("sq_done")
        ms_done, rr_done, o2_done = sem("ms_done"), sem("rr_done"), sem("o2_done")
        bus_ready, bus_done = sem("bus_ready"), sem("bus_done")
        xa_done, bst_done, mv_done = sem("xa_done"), sem("bst_done"), sem("mv_done")

        UNITS = 16
        KP = SEQ // P // 2
        CR = 64 + DH + 1
        RCH, MCH = 10, 3

        def group(g):
            return g % 2, g // 2

        def half(h):
            return slice(h * H, h * H + H)

        def tile_cols(t):
            return slice(t * P, t * P + P)

        def xtiles(b):
            return slice(b * TT, b * TT + TT) if isinstance(b, int) else bass.ds(b * TT, TT)

        def xtile(b, t):
            return slice(b * TT + t, b * TT + t + 1) if isinstance(b, int) else bass.ds(b * TT + t, 1)

        def pe_xT(pe, b, q, h, start):
            pe.wait_ge(xn_done, 2 * b + h + 1)
            if h == 0 and not start:
                pe.wait_ge(p1_done, UNITS * b)
            for t in range(4):
                i = nc.tensor.transpose(psS[:, h, tile_cols(t)], xn[:, 4 * h + t, :], ident[:, :])
            i.then_inc(xT_ready, 1)

        def pe_proj(pe, b, k):
            w, h = k // 2, k % 2
            if k == 0:
                pe.wait_ge(xTl_done, 2 * b + 2)
            if k >= 2:
                pe.wait_ge(proj_done, 8 * b + k - 1)
            lo, hi = A["wpL"][:, w * P:w * P + P], A["wpH"][:, w * P:w * P + P]
            out = psS[:, h, :]
            nc.tensor.matmul(out, hi, xnTh[:, half(h)], start=True, stop=False)
            nc.tensor.matmul(out, lo, xnTh[:, half(h)], start=False, stop=False)
            nc.tensor.matmul(out, hi, xnTl[:, half(h)], start=False, stop=True).then_inc(proj_ready, 1)

        def pe_v_r1(pe, b, q):
            pe.wait_ge(proj_done, 8 * b + 8)
            for t in range(TT):
                i = nc.tensor.matmul(psS[:, 0, t * DH:t * DH + DH], xnT[:, tile_cols(t)], A["wv"][:, :],
                                     start=True, stop=True)
            i.then_inc(v_ready, 1)
            for h in (0, 1):
                nc.tensor.matmul(psS[0:64, 1, 0:1], A["w1"][:, :], rsum[:, h:h + 1], start=(h == 0), stop=(h == 1))
            for t in range(TT):
                nc.tensor.matmul(psS[:, 1, 32:33], Y[:, t, :], A["ones"][:, 0:1], start=(t == 0), stop=(t == TT - 1))
            nc.tensor.matmul(psS[0:1, 1, 64:64 + NL], xnT[:, SEQ - 1:SEQ], A["lmT"][:, :],
                             start=True, stop=True).then_inc(r1_ready, 1)

        def pe_r2(pe, b):
            pe.wait_ge(r1_done, b + 1)
            nc.tensor.matmul(psS[:, 1, 0:3], silb[:, :], A["w2"][:, :], start=True, stop=True)
            nc.tensor.matmul(psS[0:NL, 1, 8:9], arow[:, :], A["ones"][0:1, 0:1], start=True, stop=True).then_inc(r2_ready, 1)

        def pe_base(pe, b, h, after_bus):
            if h == 0:
                pe.wait_ge(r3_done, b + 1)
                if after_bus:
                    pe.wait_ge(xa_done, 2 * b - 2)
            else:
                pe.wait_ge(base_done, 2 * b + 1)
            for t in range(4):
                k = tile_cols(4 * h + t)
                nc.tensor.matmul(psM[:, tile_cols(t)], ssmT[:, k], A["mixA"][:, :], start=True, stop=False)
                i = nc.tensor.matmul(psM[:, tile_cols(t)], xnT[:, k], A["mixB"][:, :], start=False, stop=True)
            i.then_inc(base_ready, 1)

        def act_base(act, b, q, h):
            act.wait_ge(base_ready, 2 * b + h + 1)
            nc.scalar.activation(base[:, q, 4 * h:4 * h + 4, :].rearrange("p t d -> p (t d)"), psM[:, :],
                                 ACT.Copy).then_inc(base_done, 1)

        def pe_r3(pe, b):
            pe.wait_ge(r2_done, b + 1)
            nc.tensor.matmul(psS[:, 1, 16:17], A["lm"][:, :], acol[:, :], start=True, stop=True).then_inc(r3_ready, 1)

        def pe_p1(pe, b, q, v):
            m, t = v // TT, v % TT
            if v == 0:
                pe.wait_ge(v_done, b + 1)
                pe.wait_ge(r3_done, b + 1)
            else:
                pe.wait_ge(p1_done, UNITS * b + v)
            for h in (0, 1):
                i = nc.tensor.matmul(psS[:, h, :], A["Q"][0:R, q, m, tile_cols(t)], A["K"][0:R, q, m, half(h)],
                                     start=True, stop=True)
            i.then_inc(p1_ready, 1)

        def pe_row(pe, b, g):
            m, h = group(g)
            pe.wait_ge(p1_done, UNITS * b + TT * m + 4 * h + 4)
            if g >= 1:
                pe.wait_ge(row_done, 4 * b + g)
            else:
                pe.wait_ge(base_done, 2 * b + 2)
            for t in range(4):
                i = nc.tensor.transpose(psM[0:R + 1, tile_cols(t)], A["mpad"][:, TT * m + 4 * h + t, :], ident[:, :])
            i.then_inc(row_ready, 1)

        def act_xT(act, b, q, h, start):
            act.wait_ge(xT_ready, 2 * b + h + 1)
            if h == 0 and not start:
                act.wait_ge(r1_ready, b)
                act.wait_ge(base_ready, 2 * b)
            nc.scalar.activation(xnT[:, half(h)], psS[:, h, :], ACT.Copy, accum_out=rsum[:, h:h + 1]).then_inc(xT_done, 1)
            if h == 0 and not start:
                act.wait_ge(proj_ready, 8 * b)
            nc.scalar.activation(xnTh[:, half(h)], psS[:, h, :], ACT.Copy).then_inc(xTh_done, 1)

        def act_proj(act, b, k, start):
            act.wait_ge(proj_ready, 8 * b + k + 1)
            if not (start and k < 2):
                act.wait_ge(proj_done, 8 * b + k - 1)
            nc.scalar.activation(projh[0:R, k % 2, :], psS[0:R, k % 2, :], ACT.Copy).then_inc(projh_done, 1)

        def act_r1(act, b):
            act.wait_ge(r1_copied, b + 1)
            nc.scalar.activation(col[0:64, 0:1], col[0:64, 4:5], ACT.Exp, scale=-1.0 / SEQ).then_inc(r1_exp, 1)
            act.wait_ge(arc_max, b + 1)
            nc.scalar.activation(arow[:, :], arow[:, :], ACT.Exp, bias=arcn[:, 0:1], scale=ARC,
                                 accum_out=arcn[:, 1:2]).then_inc(arc_exp, 1)

        def act_r2(act, b):
            act.wait_ge(r2_shift, b + 1)
            nc.scalar.activation(p3[:, 0:3], p3[:, 0:3], ACT.Exp, accum_out=p3[:, 3:4]).then_inc(r2_exp, 1)

        def act_row(act, b, q, g):
            m, h = group(g)
            act.wait_ge(row_ready, 4 * b + g + 1)
            nc.scalar.activation(A["Q"][R:R + 1, q, m, half(h)], psM[R:R + 1, :], ACT.Copy).then_inc(row_done, 1)

        def dve_y(dve, b, q, start):
            if not start:
                dve.wait_ge(r1_ready, b)
            for t in range(TT):
                k = xtile(b, t)
                i = nc.vector.tensor_scalar(Y[:, t:t + 1, :], X[:, k, :], stats[:, k, 0:1], rstd[:, k],
                                            ALU.subtract, ALU.mult)
            i.then_inc(y_done, 1)
            dve.wait_ge(y_done, b + 1)
            nc.vector.tensor_tensor(X[:, xtiles(b), :], X[:, xtiles(b), :], Y[:, :, :], ALU.add).then_inc(xr_done, 1)
            for t in range(TT):
                i = nc.vector.scalar_tensor_tensor(out=xn[:, t, :], in0=Y[:, t, :], scalar=rmsin[:, xtile(b, t)],
                                                   in1=A["w_in"][:, :], op0=ALU.mult, op1=ALU.mult)
                if t % 4 == 3:
                    i.then_inc(xn_done, 1)

        def pool_xTl(pool, b, q, h):
            pool.wait_ge(xTh_done, 2 * b + h + 1)
            nc.gpsimd.tensor_tensor(xnTl[:, half(h)], xnT[:, half(h)], xnTh[:, half(h)].bitcast(F32),
                                    ALU.subtract).then_inc(xTl_done, 1)

        def dve_proj(dve, b, q, k):
            w, h = k // 2, k % 2
            m, side = w // 2, ("Q", "K")[w % 2]
            dve.wait_ge(projh_done, 8 * b + k + 1)
            nc.vector.scalar_tensor_tensor(out=A[side][0:R, q, m, half(h)], in0=projh[0:R, k % 2, :].bitcast(F32),
                                           scalar=A["sgn" + side][0:R, :], in1=psS[0:R, h, :],
                                           op0=ALU.mult, op1=ALU.add).then_inc(proj_done, 1)

        def dve_v(dve, b, q):
            dve.wait_ge(v_ready, b + 1)
            nc.vector.tensor_copy(A["V1"][:, q, :, 0:DH],
                                  psS[:, 0, 0:TT * DH].rearrange("p (t c) -> p t c", c=DH)).then_inc(v_done, 1)

        def dve_ema(dve, b, start):
            dve.wait_ge(xT_done, 2 * b + 2)
            if not start:
                dve.wait_ge(base_ready, 2 * b)
            nc.vector.tensor_scalar(ema_in[:, :], xnT[:, :], A["oml"][:, :], None, ALU.mult).then_inc(ema_scaled, 1)
            dve.wait_ge(ema_scaled, b + 1)
            nc.vector.tensor_tensor_scan(out=ssmT[:, :], data0=A["lam"][:, 0:1].broadcast_to((P, SEQ)),
                                         data1=ema_in[:, :], initial=0.0, op0=ALU.mult, op1=ALU.add).then_inc(ema_done, 1)

        def dve_r1(dve, b, q):
            n = [RCH * b]

            def link(ins):
                n[0] = n[0] + 1
                ins.then_inc(rchain, 1)
                dve.wait_ge(rchain, n[0])

            dve.wait_ge(r1_ready, b + 1)
            nc.vector.tensor_copy(ysum[:, q:q + 1], psS[:, 1, 32:33])
            nc.vector.tensor_copy(col[0:64, 4:5], psS[0:64, 1, 0:1])
            nc.vector.tensor_copy(arow[:, :], psS[0:1, 1, 64:64 + NL]).then_inc(r1_copied, 1)
            dve.wait_ge(r1_copied, b + 1)
            link(nc.vector.tensor_reduce(arcn[:, 2:3], arow[:, :], AX.X, ALU.max))
            nc.vector.tensor_scalar(arcn[:, 0:1], arcn[:, 2:3], -ARC, None, ALU.mult).then_inc(arc_max, 1)
            dve.wait_ge(r1_exp, b + 1)
            link(nc.vector.tensor_scalar(col[0:64, 1:2], col[0:64, 0:1], 1.0, None, ALU.add))
            link(nc.vector.reciprocal(col[0:64, 2:3], col[0:64, 1:2]))
            link(nc.vector.scalar_tensor_tensor(out=col[0:64, 3:4], in0=col[0:64, 4:5], scalar=1.0 / SEQ,
                                                in1=col[0:64, 2:3], op0=ALU.mult, op1=ALU.mult))
            nc.vector.tensor_scalar(silb[:, :], A["ones"][0:64, :], col[0:64, 3:4], None, ALU.mult)
            dve.wait_ge(arc_exp, b + 1)
            link(nc.vector.reciprocal(arcn[:, 3:4], arcn[:, 1:2]))
            nc.vector.tensor_scalar(arow[:, :], arow[:, :], arcn[:, 3:4], None, ALU.mult).then_inc(r1_done, 1)

        def dve_r2(dve, b, q):
            n = [RCH * b + 5]

            def link(ins):
                n[0] = n[0] + 1
                ins.then_inc(rchain, 1)
                dve.wait_ge(rchain, n[0])

            dve.wait_ge(r2_ready, b + 1)
            nc.vector.tensor_copy(acol[:, :], psS[0:NL, 1, 8:9])
            link(nc.vector.tensor_tensor(p3[:, 0:3], psS[:, 1, 0:3], A["b2"][:, :], ALU.add))
            link(nc.vector.tensor_reduce(p3[:, 4:5], p3[:, 0:3], AX.X, ALU.max))
            nc.vector.tensor_scalar(p3[:, 0:3], p3[:, 0:3], p3[:, 4:5], None, ALU.subtract).then_inc(r2_shift, 1)
            dve.wait_ge(r2_exp, b + 1)
            link(nc.vector.reciprocal(p3[:, 5:6], p3[:, 3:4]))
            link(nc.vector.tensor_scalar(p3[:, 0:3], p3[:, 0:3], p3[:, 5:6], None, ALU.mult))
            link(nc.vector.tensor_tensor(pl[:, q, 0:1], p3[:, 1:2], p3[:, 2:3], ALU.add))
            nc.vector.scalar_tensor_tensor(out=pl[:, q, 1:2], in0=pl[:, q, 0:1], scalar=-1.0, in1=A["slam"][:, :],
                                           op0=ALU.mult, op1=ALU.mult).then_inc(r2_done, 1)

        def dve_r3(dve, b, q):
            dve.wait_ge(r3_ready, b + 1)
            dve.wait_ge(ema_done, b + 1)
            nc.vector.scalar_tensor_tensor(out=ssmT[:, SEQ - 1:SEQ], in0=psS[:, 1, 16:17], scalar=p3[:, 2:3],
                                           in1=ssmT[:, SEQ - 1:SEQ], op0=ALU.mult, op1=ALU.add).then_inc(r3_done, 1)

        def dve_p1(dve, b, v):
            dve.wait_ge(p1_ready, UNITS * b + v + 1)
            nc.vector.tensor_reduce(A["mpad"][:, v, R:R + 1], psS[:, :, :], AX.XY, ALU.max,
                                    negate=True).then_inc(p1_done, 1)

        def pe_st(pe, b, q, u, start):
            m, h = group(u // KP)
            if u == 0:
                pe.wait_ge(row_done, 4 * b + 4)
            if not (start and u < 2):
                pe.wait_ge(ex_done, UNITS * b + u - 1)
            for j in (0, 1):
                i = nc.tensor.matmul(psE[:, u % 2, j * H:j * H + H], A["K"][0:R + 1, q, m, tile_cols(2 * (u % KP) + j)],
                                     A["Q"][0:R + 1, q, m, half(h)], start=True, stop=True)
            i.then_inc(st_ready, 1)

        def act_ex(act, b, u, start):
            act.wait_ge(st_ready, UNITS * b + u + 1)
            if not (start and u < 2):
                act.wait_ge(pv_done, UNITS * b + u - 1)
            nc.scalar.activation(Ex[:, u % 2, :], psE[:, u % 2, :], ACT.Exp, scale=SC).then_inc(ex_done, 1)

        def pe_pv(pe, b, q, u, start):
            g, kp = u // KP, u % KP
            m, h = group(g)
            pe.wait_ge(ex_done, UNITS * b + u + 1)
            if kp == 0 and not (start and g < 2):
                pe.wait_ge(ct_done, 4 * b + g - 1)
            for j in (0, 1):
                i = nc.tensor.matmul(psC[64 * m:64 * m + DH + 1, :], A["V1"][:, q, 2 * kp + j, :], Ex[:, u % 2, j * H:j * H + H],
                                     start=(kp == 0 and j == 0), stop=(kp == KP - 1 and j == 1))
            i.then_inc(pv_done, 1)

        def dve_ct(dve, b, q, g):
            m, h = group(g)
            dve.wait_ge(pv_done, UNITS * b + KP * (g + 1))
            nc.vector.tensor_copy(CT[64 * m:64 * m + DH + 1, q, half(h)],
                                  psC[64 * m:64 * m + DH + 1, :]).then_inc(ct_done, 1)

        def pe_mix(pe, b, q, t):
            if t == 0:
                pe.wait_ge(ct_done, 4 * b + 4)
            else:
                pe.wait_ge(o_done, TT * b + t)
            nc.tensor.matmul(psM[:, 0:2 * (D + 1)], CT[0:CR, q, tile_cols(t)], A["Wc"][0:CR, :],
                             start=True, stop=True).then_inc(mix_ready, 1)

        def act_sq(act, b, t):
            act.wait_ge(o_done, TT * b + t + 1)
            nc.scalar.activation(sq[:, t, :], O[:, t, :], ACT.Square, accum_out=ss[:, t:t + 1]).then_inc(sq_done, 1)

        def dve_mix(dve, b, q, t):
            n = (b * TT + t) * MCH
            dve.wait_ge(mix_ready, TT * b + t + 1)
            if t == 0:
                dve.wait_ge(base_done, 2 * b + 2)
                nc.vector.tensor_copy(ybus[:, :], ysum[:, q:q + 1])
            nc.vector.reciprocal(rec[:, :], psM[:, D:2 * D + 2:D + 1]).then_inc(mchain, 1)
            dve.wait_ge(mchain, n + 1)
            nc.vector.tensor_tensor(coef[:, t, :], rec[:, :], pl[:, q, :], ALU.mult).then_inc(mchain, 1)
            dve.wait_ge(mchain, n + 2)
            nc.vector.scalar_tensor_tensor(out=O[:, t, :], in0=psM[:, 0:D], scalar=coef[:, t, 0:1],
                                           in1=base[:, q, t, :], op0=ALU.mult, op1=ALU.add).then_inc(mchain, 1)
            dve.wait_ge(mchain, n + 3)
            nc.vector.scalar_tensor_tensor(out=O[:, t, :], in0=psM[:, D + 1:2 * D + 1], scalar=coef[:, t, 1:2],
                                           in1=O[:, t, :], op0=ALU.mult, op1=ALU.add).then_inc(o_done, 1)

        def dve_ms(dve, b):
            dve.wait_ge(sq_done, TT * b + TT)
            nc.vector.tensor_scalar(ms[:, :], ss[:, :], 1.0 / D, FP32_EPS, ALU.mult, ALU.add).then_inc(ms_done, 1)

        def pool_rr(pool, b):
            pool.wait_ge(ms_done, b + 1)
            nc.gpsimd.tensor_tensor(rr[:, :], ms[:, :], A["half"][:, :], ALU.pow).then_inc(rr_done, 1)

        def dve_o2(dve, b):
            dve.wait_ge(rr_done, b + 1)
            for t in range(TT):
                i = nc.vector.scalar_tensor_tensor(out=O[:, t, :], in0=O[:, t, :], scalar=rr[:, t:t + 1],
                                                   in1=A["w_out"][:, :], op0=ALU.mult, op1=ALU.mult)
            i.then_inc(o2_done, 1)

        def pe_bus(pe, b, k):
            if k == 0:
                pe.wait_ge(o2_done, b + 1)
                for t in range(TT):
                    i = nc.tensor.matmul(psM[:, 0:1], O[:, t, :], A["ones"][:, 0:1], start=(t == 0), stop=(t == TT - 1))
            else:
                pe.wait_ge(bus_done, 3 * b + k)
                if k == 1:
                    i = nc.tensor.matmul(psM[:, 0:1], A["compress"][:, :], busc[:, 0:1], start=True, stop=True)
                elif k == 2:
                    i = nc.tensor.matmul(psM[:, 0:1], A["publish"][:, :], busc[:, 1:2], start=True, stop=True)
                else:
                    i = nc.tensor.matmul(psM[:, 0:D], pubb[:, :], A["expand"][:, :], start=True, stop=True)
            i.then_inc(bus_ready, 1)

        def dve_bus(dve, b, k):
            dve.wait_ge(bus_ready, 4 * b + k + 1)
            if k == 0:
                i = nc.vector.tensor_scalar(busc[:, 0:1], psM[:, 0:1], ybus[:, :], 1.0 / SEQ, ALU.add, ALU.mult)
            elif k == 1:
                i = nc.vector.tensor_copy(busc[:, 1:2], psM[:, 0:1])
            else:
                i = nc.vector.tensor_scalar(pubb[:, :], A["ones"][:, :], psM[:, 0:1], 0.1, ALU.mult, ALU.mult)
            i.then_inc(bus_done, 1)

        def dve_x(dve, b):
            k = xtiles(b)
            dve.wait_ge(xr_done, b + 1)
            dve.wait_ge(o2_done, b + 1)
            nc.vector.tensor_tensor(O[:, :, :], X[:, k, :], O[:, :, :], ALU.add).then_inc(xa_done, 1)
            dve.wait_ge(xa_done, 2 * b + 1)
            dve.wait_ge(bus_ready, 4 * b + 4)
            nc.vector.tensor_tensor(O[:, :, :], O[:, :, :], psM[:, 0:D].unsqueeze(1).broadcast_to((P, TT, D)),
                                    ALU.add).then_inc(xa_done, 1)
            dve.wait_ge(xa_done, 2 * b + 2)
            for t in range(TT):
                i = nc.vector.bn_stats(bst[:, t, :], O[:, t, :])
            i.then_inc(bst_done, 1)
            dve.wait_ge(bst_done, b + 1)
            nc.vector.tensor_scalar(X[:, k, :], O[:, :, :], 1.0, None, ALU.mult)
            for t in range(TT):
                i = nc.vector.bn_aggr(mv[:, t, :], bst[:, t, :])
            i.then_inc(mv_done, 1)
            dve.wait_ge(mv_done, b + 1)
            nc.vector.tensor_scalar(stats[:, k, :], mv[:, :, :], 1.0, None, ALU.mult)

        def pe_turn(pe, b, q, first, last):
            for u in range(UNITS):
                pe_st(pe, b, q, u, first)
                if u >= 1:
                    pe_pv(pe, b, q, u - 1, first)
                if not first:
                    if u < TT:
                        pe_mix(pe, b - 1, 1 - q, u)
                    if 9 <= u < 13:
                        pe_bus(pe, b - 1, u - 9)
                if not last:
                    if u in (0, 1):
                        pe_xT(pe, b + 1, 1 - q, u, False)
                    if u in (2, 3, 4, 5):
                        pe_proj(pe, b + 1, 2 * u - 4)
                        pe_proj(pe, b + 1, 2 * u - 3)
                    if u == 6:
                        pe_v_r1(pe, b + 1, 1 - q)
                    if u == 7:
                        pe_r2(pe, b + 1)
                    if u == 8:
                        pe_r3(pe, b + 1)
                    if u in (14, 15):
                        pe_base(pe, b + 1, u - 14, not first)
                    if u >= 8:
                        pe_p1(pe, b + 1, 1 - q, 2 * u - 16)
                        pe_p1(pe, b + 1, 1 - q, 2 * u - 15)
            pe_pv(pe, b, q, UNITS - 1, first)
            if not last:
                for g in range(4):
                    pe_row(pe, b + 1, g)

        def act_turn(act, b, q, first, last):
            for u in range(UNITS):
                act_ex(act, b, u, first)
                if not first and 1 <= u <= TT:
                    act_sq(act, b - 1, u - 1)
                if not last:
                    if u in (0, 1):
                        act_xT(act, b + 1, 1 - q, u, False)
                    if u in (2, 3, 4, 5):
                        act_proj(act, b + 1, 2 * u - 4, False)
                        act_proj(act, b + 1, 2 * u - 3, False)
                    if u == 6:
                        act_r1(act, b + 1)
                    if u == 7:
                        act_r2(act, b + 1)
                    if u in (14, 15):
                        act_base(act, b + 1, 1 - q, u - 14)
            if not last:
                for g in range(4):
                    act_row(act, b + 1, 1 - q, g)

        def dve_turn(dve, b, q, first, last):
            for u in range(UNITS):
                if u >= KP and u % KP == 1:
                    dve_ct(dve, b, q, u // KP - 1)
                if not first and u < TT:
                    dve_mix(dve, b - 1, 1 - q, u)
                if not last:
                    if u == 0:
                        dve_y(dve, b + 1, 1 - q, False)
                    if u in (2, 3, 4, 5):
                        dve_proj(dve, b + 1, 1 - q, 2 * u - 4)
                        dve_proj(dve, b + 1, 1 - q, 2 * u - 3)
                    if u == 5:
                        dve_ema(dve, b + 1, False)
                    if u == 6:
                        dve_v(dve, b + 1, 1 - q)
                        dve_r1(dve, b + 1, 1 - q)
                    if u == 7:
                        dve_r2(dve, b + 1, 1 - q)
                    if u == 8:
                        dve_r3(dve, b + 1, 1 - q)
                if not first:
                    if u == 8:
                        dve_ms(dve, b - 1)
                        dve_o2(dve, b - 1)
                    if 9 <= u < 12:
                        dve_bus(dve, b - 1, u - 9)
                    if u == 13:
                        dve_x(dve, b - 1)
                if not last and u >= 8:
                    dve_p1(dve, b + 1, 2 * u - 16)
                    dve_p1(dve, b + 1, 2 * u - 15)
            dve_ct(dve, b, q, 3)

        def pool_turn(pool, b, q, first, last):
            if not last:
                for h in (0, 1):
                    pool_xTl(pool, b + 1, 1 - q, h)
            if not first:
                pool_rr(pool, b - 1)

        def over_batches(eng, turn):
            turn(eng, 0, 0, True, False)
            turn(eng, 1, 1, False, False)
            with eng.Fori(2, BATCH - 2, 2) as b:
                turn(eng, b, 0, False, False)
                turn(eng, b + 1, 1, False, False)
            turn(eng, BATCH - 2, 0, False, False)
            turn(eng, BATCH - 1, 1, False, True)

        end, eq = BATCH - 1, (BATCH - 1) % 2
        block = ctx.enter_context(nc.Block("at_block"))

        @block.tensor
        def _(pe):
            for h in (0, 1):
                pe_xT(pe, 0, 0, h, True)
            for k in range(8):
                pe_proj(pe, 0, k)
            pe_v_r1(pe, 0, 0)
            pe_r2(pe, 0)
            pe_r3(pe, 0)
            for v in range(UNITS):
                pe_p1(pe, 0, 0, v)
            for h in (0, 1):
                pe_base(pe, 0, h, False)
            for g in range(4):
                pe_row(pe, 0, g)
            over_batches(pe, pe_turn)
            for t in range(TT):
                pe_mix(pe, end, eq, t)
            for k in range(4):
                pe_bus(pe, end, k)

        @block.scalar
        def _(act):
            for h in (0, 1):
                act_xT(act, 0, 0, h, True)
            for k in range(8):
                act_proj(act, 0, k, True)
            act_r1(act, 0)
            act_r2(act, 0)
            for h in (0, 1):
                act_base(act, 0, 0, h)
            for g in range(4):
                act_row(act, 0, 0, g)
            over_batches(act, act_turn)
            for t in range(TT):
                act_sq(act, end, t)

        @block.vector
        def _(dve):
            nc.vector.memset(CT[:, :, :].bitcast(mybir.dt.uint32), 0)
            dve_y(dve, 0, 0, True)
            for k in range(8):
                dve_proj(dve, 0, 0, k)
            dve_ema(dve, 0, True)
            dve_v(dve, 0, 0)
            dve_r1(dve, 0, 0)
            dve_r2(dve, 0, 0)
            dve_r3(dve, 0, 0)
            for v in range(UNITS):
                dve_p1(dve, 0, v)
            over_batches(dve, dve_turn)
            for t in range(TT):
                dve_mix(dve, end, eq, t)
            dve_ms(dve, end)
            dve_o2(dve, end)
            for k in range(3):
                dve_bus(dve, end, k)
            dve_x(dve, end)

        @block.gpsimd
        def _(pool):
            for h in (0, 1):
                pool_xTl(pool, 0, 0, h)
            over_batches(pool, pool_turn)
            pool_rr(pool, end)


def program(nc, ins, out):
    T, D = ins["x"].shape
    E = ins["WrT"].shape[1]
    F = ins["WgT"].shape[1] // E
    BATCH = ins["batches"]
    DH = ins["wv"].shape[1]
    TILES = T // P
    SEQ = T // BATCH
    with ExitStack() as ctx:
        def sb(name, shape, dt=F32, where=None):
            return (where or ctx).enter_context(nc.sbuf_tensor(name, shape, dt))

        persist = {
            "X": sb("X", [P, TILES, D]),
            "stats": sb("stats", [P, TILES, 2]),
            "rstd": sb("rstd", [P, TILES]),
            "rmsin": sb("rmsin", [P, TILES]),
            "ident": sb("ident", [P, P]),
            "x": ins["x"].rearrange("(t p) d -> p t d", p=P),
            "out": out.rearrange("(t p) d -> p t d", p=P),
        }

        GROUPS = 4
        GT = TILES // GROUPS
        NT = 2 * GT + E - 1
        NT += NT % 2
        NT += 2 * (NT // 2 % 2)
        slots = 2 * NT * P
        persist["GROUPS"], persist["GT"], persist["NT"], persist["ZC"] = GROUPS, GT, NT, 640
        persist["xsort"] = nc.dram_tensor("xsort", (slots, D), F32, kind="Internal").ap()
        persist["ysort"] = nc.dram_tensor("ysort", (slots, D), F32, kind="Internal").ap()
        persist["zero"] = sb("zero", [P, persist["ZC"]])
        persist["cleared"] = [ctx.enter_context(nc.semaphore(f"cleared{k}")) for k in (0, 1)]
        persist["FILLS"] = NT * D // persist["ZC"]

        def moe(tag, first):
            with ExitStack() as here:
                for n in ("WgH", "WgL", "WuH", "WuL", "WdH", "WdL"):
                    persist[n] = sb(tag + n, [P, E * F], F32R, here)
                persist["WrH"], persist["WrL"] = (sb(tag + n, [P, E], F32R, here) for n in ("WrH", "WrL"))
                persist["before"], persist["ones_r"] = (sb(tag + n, [P, P], F32R, here) for n in ("before", "ones_r"))
                persist["later"] = sb(tag + "later", [P, GT * E, E], F32, here)
                persist["one8"] = sb(tag + "one8", [P, E], F32, here)
                persist["jt"] = sb(tag + "jt", [1, NT, E], F32, here)
                persist["jti"] = sb(tag + "jti", [1, NT, E], mybir.dt.int32, here)
                moe_constants(nc, tag, persist, ins, T, D, E, F, first)
                norm_phase(nc, tag, persist, T, False)
                with nc.cleanup_on_exit():
                    ffn_phase(nc, tag, persist, T, D, E, F, not first)

        moe("ffn1_", True)
        with ExitStack() as here:
            A = {"DH": DH}
            for n in ("mixA", "mixB", "wv", "w1", "w2", "b2", "w_in", "w_out", "slam", "lm", "lmT", "compress",
                      "publish", "expand", "lambdas"):
                A["lam" if n == "lambdas" else n] = sb("a_" + n, list(ins[n].shape), F32, here)
            A["wpH"], A["wpL"] = (sb("a_" + n, [P, 4 * P], F32R, here) for n in ("wpH", "wpL"))
            A["mpad"] = sb("a_mpad", [P, 2 * SEQ // P, 3 * DH + 1], F32, here)
            A["V1"] = sb("a_V1", [P, 2, SEQ // P, DH + 1], F32, here)
            A["half"] = sb("a_half", [P, SEQ // P], F32, here)
            A["ones"] = sb("a_ones", [P, P], F32, here)
            A["Wc"] = sb("a_Wc", [P, 2 * (D + 1)], F32, here)
            A["sgnQ"], A["sgnK"], A["oml"] = (sb("a_" + n, [P, 1], F32, here) for n in ("sgnQ", "sgnK", "oml"))
            A["Q"], A["K"] = (sb("a_" + n, [P, 2, 2, SEQ], F32R, here) for n in ("Q", "K"))
            persist["attn"] = A
            attention_constants(nc, persist, ins)
            norm_phase(nc, "at_", persist, T, True)
            attention_phase(nc, persist, T, BATCH)
        moe("ffn2_", False)


def kernel(**inputs):
    import numpy as np
    import concourse.bacc as bacc
    from concourse import mybir as mb
    from concourse.bass_utils import run_bass_kernel_spmd as run

    nc = bacc.Bacc("TRN2", target_bir_lowering=False, num_devices=1)
    g = {k: np.asarray(v) for k, v in inputs.items()}
    E, F, D = g["L0_ffn_Wg"].shape
    B, S, _ = g["L0_attn_x"].shape

    def rows(a):
        return np.broadcast_to(a, (128, a.size))

    arrays = {
        "x": g["L0_attn_x"].reshape(B * S, D),
        "WrT": g["L0_ffn_Wr"].T,
        "WgT": g["L0_ffn_Wg"].transpose(2, 0, 1).reshape(D, E * F),
        "WuT": g["L0_ffn_Wu"].transpose(2, 0, 1).reshape(D, E * F),
        "WdT": g["L0_ffn_Wd"].reshape(E, D, F // 128, 128).transpose(3, 0, 2, 1).reshape(128, E * F // 128 * D),
        "wproj": np.concatenate([np.tile(g["L0_attn_slr_" + n], (1, 4)) for n in ("wq1", "wk1", "wq2", "wk2")], axis=1),
        "woT": g["L0_attn_slr_wo"].T,
        "mixA": g["L0_attn_mix_w"][:D],
        "mixB": g["L0_attn_mix_w"][D:],
        "wv": g["L0_attn_slr_wv"],
        "w1": g["L0_attn_router_w1"],
        "w2": g["L0_attn_router_w2"],
        "b2": rows(g["L0_attn_router_b2"]),
        "w_in": rows(g["L0_attn_w_norm_in"]),
        "w_out": rows(g["L0_attn_w_norm_out"]),
        "slam": rows(g["L0_attn_slr_lam"].reshape(1)),
        "lambdas": np.repeat(g["L0_attn_lambdas"], D // g["L0_attn_lambdas"].size).reshape(D, 1),
        "lm": g["L0_attn_landmarks"],
        "lmT": g["L0_attn_landmarks"].T,
        "compress": g["L0_attn_bus_compress"],
        "publish": g["L0_attn_bus_publish"],
        "expand": g["L0_attn_bus_expand"],
    }
    arrays = {k: np.ascontiguousarray(v) for k, v in arrays.items()}
    ins = {k: nc.dram_tensor("in_" + k, v.shape, mb.dt.from_np(v.dtype), kind="ExternalInput").ap() for k, v in arrays.items()}
    ins["batches"] = B
    out = nc.dram_tensor("out", (B * S, D), mb.dt.float32, kind="ExternalOutput").ap()
    program(nc, ins, out)
    r = run(nc, [{"in_" + k: v for k, v in arrays.items()}], core_ids=[0])
    return r.results[0]["out"].reshape(B, S, D)
```

```python
from contextlib import ExitStack

import concourse.bass as bass
from concourse import mybir

ALU = mybir.AluOpType
ACT = mybir.ActivationFunctionType
AX = mybir.AxisListType
F32 = mybir.dt.float32
F32R = mybir.dt.float32r
U32 = mybir.dt.uint32

P = 128
LN_EPS = 1e-5
FP32_EPS = 1.1920929e-07


def over(ap, axis, shape):
    return ap.unsqueeze(axis).broadcast_to(shape)


def ffn_phase(nc, tag, persist, T, D, E, F, finish):
    X, rstd, stats = persist["X"], persist["rstd"], persist["stats"]
    ident = persist["ident"]
    WrH, WrL, later = persist["WrH"], persist["WrL"], persist["later"]
    WgH, WgL, WuH, WuL, Wd = (persist[n] for n in ("WgH", "WgL", "WuH", "WuL", "Wd"))
    before, ones_r, jt = persist["before"], persist["ones_r"], persist["jt"]
    xsort, ysort = persist["xsort"], persist["ysort"]
    GROUPS, GT, NT = persist["GROUPS"], persist["GT"], persist["NT"]
    FS = F // P
    AHEAD = 4
    PAIRS = NT // 2
    IN_FLIGHT = 2 * GT
    MAGIC = 1.5 * 2.0 ** 23

    with ExitStack() as ctx:
        def sb(name, shape, dt=F32):
            return ctx.enter_context(nc.sbuf_tensor(tag + name, shape, dt))

        def sem(name):
            return nc.alloc_semaphore(tag + name)

        xn = sb("xn", [P, GT, D])
        xTh, xTl = sb("xTh", [P, 4 * P], F32R), sb("xTl", [P, 4 * P], F32R)
        lg = sb("lg", [P, GT, E])
        ex = sb("ex", [P, GT, E])
        red = sb("red", [P, 8, GT])
        beats, ties = sb("beats", [P, GT * E, E]), sb("ties", [P, GT * E, E])
        rank = sb("rank", [P, GT, E])
        mask = sb("mask", [P, E * GT], F32R)
        upto_tile, tiles_before = sb("upto_tile", [P, E * GT]), sb("tiles_before", [P, E * GT])
        pick1, pick2 = sb("pick1", [P, GT, E]), sb("pick2", [P, GT, E])
        slot = sb("slot", [P, GT, E])
        ends = sb("ends", [P, 5, E])
        posf = sb("posf", [P, 2 * GT])
        sidx = sb("sidx", [P, 2 * GT], U32)
        gidx = sb("gidx", [P, 2 * GT], U32)
        pos_all = sb("pos_all", [P, GROUPS * 2 * GT])
        comb_all = sb("comb_all", [P, GROUPS * 2 * GT])
        past = sb("past", [1, NT, E])
        pastn = sb("pastn", [1, NT])
        expert = sb("expert", [1, GROUPS * NT], U32)
        gbase = sb("gbase", [P, 1])
        xs = sb("xs", [P, AHEAD, 2, D])
        xsh, xsl = sb("xsh", [P, 2, P], F32R), sb("xsl", [P, 2, P], F32R)
        rg, h = sb("rg", [P, 2, F]), sb("h", [P, 2, F])
        hh, hl = sb("hh", [P, 2, F], F32R), sb("hl", [P, 2, F], F32R)
        ysb = sb("ysb", [P, 2, 2, D])
        yg = sb("yg", [P, 2, GT, D])
        xw = sb("xw", [P, 2, D])
        settled = sb("settled", [P, 2])
        bst, mv = sb("bst", [P, GT, 6]), sb("mv", [P, GT, 2])

        def bank(name, n=1):
            return ctx.enter_context(nc.psum_tensor(tag + name, [P, n, 512], F32))

        psG, psU, psH, psT, psY, psR = bank("psG", 2), bank("psU"), bank("psH", 2), bank("psT"), bank("psY"), bank("psR")

        xs_in = [sem(f"xs_in{k}") for k in range(AHEAD)]
        xsT, xsh_done, xsl_done = sem("xsT"), sem("xsh_done"), sem("xsl_done")
        gate_ready, up_ready = sem("gate_ready"), sem("up_ready")
        relu_done, hid_done = sem("relu_done"), sem("hid_done")
        hidT, hh_done, hl_done = sem("hidT"), sem("hh_done"), sem("hl_done")
        down_ready, y_copied, y_summed = sem("down_ready"), sem("y_copied"), sem("y_summed")
        y_stored = [sem("y_stored0"), sem("y_stored1")]
        norm_done = sem("norm_done")
        normT, xTh_done, xTl_done = sem("normT"), sem("xTh_done"), sem("xTl_done")
        logits_ready, logits_done = sem("logits_ready"), sem("logits_done")
        shifted, exp_done = sem("shifted"), sem("exp_done")
        mask_done, ranks_ready = sem("mask_done"), sem("ranks_ready")
        chain = sem("chain")
        slots_done, experts_done = sem("slots_done"), sem("experts_done")
        scattered = sem("scattered")
        io_go = sem("io_go")
        scatter_go, gather_go = sem("scatter_go"), sem("gather_go")
        gidx_done = sem("gidx_done")
        gathered = [sem(f"gathered{k}") for k in range(GT // 4)]
        half_added, x_done = sem("half_added"), sem("x_done")
        bst_done, mv_done = sem("bst_done"), sem("mv_done")
        out_done = sem("out_done")
        w_in = [sem(f"w_in{k}") for k in range(4)]
        w_high, w_low = sem("w_high"), sem("w_low")
        QC = GT // 4
        CH = 2 * GT * D // 4
        CE = E * F // CH
        WC = 3 * CE
        ring = yg[:, :, :, :].rearrange("p r t d -> p (r t d)")
        by_part = Wd[:, :].rearrange("p (k c d) -> p k c d", c=2, d=D)
        weights = [(WgH, WgL), (WuH, WuL)]
        LINKS_BEFORE = (0, 1, 4, 4, 5, 6, 7, 9, 16, 20, 26, 27, 29)
        STEPS, LINKS = len(LINKS_BEFORE) - 1, LINKS_BEFORE[-1]

        def cut(start, size):
            return slice(start, start + size) if isinstance(start, int) else bass.ds(start, size)

        def chunk(c):
            m, k, at = c // CE, c % CE, c % 4 * CH
            raw = ring[:, at:at + CH]
            if m < 2:
                return raw, weights[m][0][:, k * CH:k * CH + CH], weights[m][1][:, k * CH:k * CH + CH]
            kd = slice(k * (CH // D), (k + 1) * (CH // D))
            return raw.rearrange("p (k d) -> p k d", d=D), by_part[:, kd, 0, :], by_part[:, kd, 1, :]

        def sp_weights(sp):
            for c in range(WC):
                if c >= 4:
                    sp.wait_ge(w_low, c - 3)
                k, at = c % CE * CH, c % 4 * CH
                sp.dma_start(ring[:, at:at + CH], persist["weights"][c // CE][:, k:k + CH]).then_inc(w_in[c % 4], 16)

        def act_weights(act):
            for c in range(WC):
                raw, high, low = chunk(c)
                act.wait_ge(w_in[c % 4], 16 * (c // 4 + 1))
                nc.scalar.activation(high, raw, ACT.Copy).then_inc(w_high, 1)

        def dve_weights(dve):
            for c in range(WC):
                raw, high, low = chunk(c)
                dve.wait_ge(w_high, c + 1)
                nc.vector.tensor_tensor(low, raw, high.bitcast(F32), ALU.subtract).then_inc(w_low, 1)

        def pe_three(out, ah, al, bh, bl, first=True, last=True):
            nc.tensor.matmul(out, ah, bh, start=first, stop=False)
            nc.tensor.matmul(out, al, bh, start=False, stop=False)
            return nc.tensor.matmul(out, ah, bl, start=False, stop=last)

        def pe_xsT(pe, g, j):
            n, pair = g * NT + j, j // 2
            if j % 2 == 0:
                pe.wait_ge(xs_in[pair % AHEAD], 16 * (g * (PAIRS // AHEAD) + pair // AHEAD + 1))
            if not (isinstance(n, int) and n == 0):
                pe.wait_ge(xsl_done, n)
            nc.tensor.transpose(psT[:, 0, 0:P], xs[:, pair % AHEAD, j % 2, :], ident[:, :]).then_inc(xsT, 1)

        def pe_expert(pe, g, j):
            return pe.value_load(expert[0:1, cut(g * NT + j, 1)], min_val=0, max_val=E - 1)

        def pe_up(pe, g, j, e, head):
            n = g * NT + j
            pe.wait_ge(xsl_done, n + 1)
            if not (head and j < 2):
                pe.wait_ge(relu_done, n - 1)
            ah, al, w = xsh[:, j % 2, :], xsl[:, j % 2, :], bass.ds(e * F, F)
            pe_three(psG[:, j % 2, :], ah, al, WgH[:, w], WgL[:, w]).then_inc(gate_ready, 1)
            if not (head and j < 1):
                pe.wait_ge(hid_done, n)
            pe_three(psU[:, 0, :], ah, al, WuH[:, w], WuL[:, w]).then_inc(up_ready, 1)

        def pe_hidT(pe, g, j, head):
            n = g * NT + j
            pe.wait_ge(hid_done, n + 1)
            if not (head and j < 2):
                pe.wait_ge(hl_done, n - 1)
            for f in range(FS):
                i = nc.tensor.transpose(psH[:, j % 2, f * P:f * P + P], h[:, j % 2, f * P:f * P + P], ident[:, :])
            i.then_inc(hidT, 1)

        def pe_down(pe, g, j, e, head):
            n = g * NT + j
            pe.wait_ge(hl_done, n + 1)
            if not (head and j < 1):
                pe.wait_ge(y_summed, n)
            for f in range(FS):
                k, w = slice(f * P, f * P + P), e * (2 * F) + f * 2 * D
                if f == FS - 1:
                    nc.tensor.matmul(psY[:, 0, 0:D], hl[:, j % 2, k], Wd[:, bass.ds(w, D)], start=False, stop=False)
                i = nc.tensor.matmul(psY[:, 0, 0:2 * D], hh[:, j % 2, k], Wd[:, bass.ds(w, 2 * D)],
                                     start=f == 0, stop=f == FS - 1)
                if f < FS - 1:
                    nc.tensor.matmul(psY[:, 0, 0:D], hl[:, j % 2, k], Wd[:, bass.ds(w, D)], start=False, stop=False)
            i.then_inc(down_ready, 1)

        def act_xsh(act, g, j):
            act.wait_ge(xsT, g * NT + j + 1)
            nc.scalar.activation(xsh[:, j % 2, :], psT[:, 0, 0:P], ACT.Copy).then_inc(xsh_done, 1)

        def act_relu(act, g, j, head):
            n = g * NT + j
            act.wait_ge(gate_ready, n + 1)
            if not (head and j < 2):
                act.wait_ge(hid_done, n - 1)
            nc.scalar.activation(rg[:, j % 2, :], psG[:, j % 2, :], ACT.Relu).then_inc(relu_done, 1)

        def act_hh(act, g, j, head):
            n = g * NT + j
            act.wait_ge(hidT, n + 1)
            if not (head and j < 2):
                act.wait_ge(down_ready, n - 1)
            nc.scalar.activation(hh[:, j % 2, :], psH[:, j % 2, :], ACT.Copy).then_inc(hh_done, 1)

        def act_y(act, g, j, head):
            pair = j // 2
            act.wait_ge(down_ready, g * NT + j + 1)
            if j % 2 == 0 and not (head and j < 4):
                act.wait_ge(y_stored[pair % 2], 16 * (g * (PAIRS // 2) + pair // 2))
            nc.scalar.activation(ysb[:, pair % 2, j % 2, :], psY[:, 0, 0:D], ACT.Copy).then_inc(y_copied, 1)

        def dve_ysum(dve, g, j):
            pair = j // 2
            dve.wait_ge(y_copied, g * NT + j + 1)
            nc.vector.tensor_tensor(ysb[:, pair % 2, j % 2, :], psY[:, 0, D:2 * D], ysb[:, pair % 2, j % 2, :],
                                    ALU.add).then_inc(y_summed, 1)

        def dve_xsl(dve, g, j):
            dve.wait_ge(xsh_done, g * NT + j + 1)
            nc.vector.tensor_tensor(xsl[:, j % 2, :], psT[:, 0, 0:P], xsh[:, j % 2, :].bitcast(F32),
                                    ALU.subtract).then_inc(xsl_done, 1)

        def dve_hid(dve, g, j, head):
            n = g * NT + j
            dve.wait_ge(relu_done, n + 1)
            dve.wait_ge(up_ready, n + 1)
            if not (head and j < 2):
                dve.wait_ge(hidT, n - 1)
            nc.vector.tensor_tensor(h[:, j % 2, :], rg[:, j % 2, :], psU[:, 0, :], ALU.mult).then_inc(hid_done, 1)

        def dve_hl(dve, g, j):
            dve.wait_ge(hh_done, g * NT + j + 1)
            nc.vector.tensor_tensor(hl[:, j % 2, :], psH[:, j % 2, :], hh[:, j % 2, :].bitcast(F32),
                                    ALU.subtract).then_inc(hl_done, 1)

        def sp_load(sp, g, pair, head):
            q = g * PAIRS + pair
            here = (g & 1) * PAIRS + pair
            rows = xsort.rearrange("(t p) d -> p t d", p=P)[:, cut(2 * here, 2), :]
            if pair == 0:
                sp.wait_ge(scattered, (g + 1) * 16 * IN_FLIGHT)
            if not (head and pair < AHEAD):
                sp.wait_ge(xsT, 2 * q - 2 * AHEAD + 2)
            sp.sem_inc(io_go, 1)
            sp.dma_start(xs[:, pair % AHEAD, :, :], rows).then_inc(xs_in[pair % AHEAD], 16)

        def sp_store(sp, g, pair):
            q = g * PAIRS + pair
            here = (g & 1) * PAIRS + pair
            rows = ysort.rearrange("(t p) d -> p t d", p=P)[:, cut(2 * here, 2), :]
            if pair == 0 and not (isinstance(g, int) and g < 2):
                sp.wait_ge(gidx_done, g)
            sp.wait_ge(y_summed, 2 * q + 2)
            sp.sem_inc(io_go, 1)
            sp.dma_start(rows, ysb[:, pair % 2, :, :])\
                .then_inc(y_stored[pair % 2], 16)

        def dve_norm(dve, g, c, start):
            if c == 0 and not start:
                dve.wait_ge(scattered, g * 16 * IN_FLIGHT)
            for t in range(4 * c, 4 * c + 4):
                k = cut(g * GT + t, 1)
                i = nc.vector.tensor_scalar(xn[:, t:t + 1, :], X[:, k, :], stats[:, k, 0:1], rstd[:, k],
                                            ALU.subtract, ALU.mult)
            i.then_inc(norm_done, 1)

        def chunk_bank(c, start):
            return (psG[:, 0, :], psG[:, 1, :], psH[:, 0, :], psH[:, 1, :])[c] if start else psR[:, 0, :]

        def chunk_parts(c, start):
            return (hh[:, c % 2, :], hl[:, c % 2, :]) if start else (xTh[:, :], xTl[:, :])

        def chunk_logits(c, start):
            return c * 4 * E if start else 0

        def pe_normT(pe, g, c, start):
            if c == 0 and not start:
                pe.wait_ge(slots_done, g)
                pe.wait_ge(experts_done, g)
            if c > 0 and not start:
                pe.wait_ge(logits_done, QC * g + c)
            pe.wait_ge(norm_done, QC * g + c + 1)
            for t in range(4):
                i = nc.tensor.transpose(chunk_bank(c, start)[:, t * P:t * P + P], xn[:, 4 * c + t, :], ident[:, :])
            i.then_inc(normT, 1)

        def act_xTh(act, g, c, start=False):
            act.wait_ge(normT, QC * g + c + 1)
            if start and c >= 2:
                act.wait_ge(logits_ready, c - 1)
            nc.scalar.activation(chunk_parts(c, start)[0], chunk_bank(c, start), ACT.Copy).then_inc(xTh_done, 1)

        def dve_xTl(dve, g, c, start=False):
            high, low = chunk_parts(c, start)
            dve.wait_ge(xTh_done, QC * g + c + 1)
            nc.vector.tensor_tensor(low, chunk_bank(c, start), high.bitcast(F32), ALU.subtract).then_inc(xTl_done, 1)

        def pe_logits(pe, g, c, start=False):
            high, low = chunk_parts(c, start)
            pe.wait_ge(xTl_done, QC * g + c + 1)
            for t in range(4):
                k, at = slice(t * P, t * P + P), chunk_logits(c, start) + t * E
                i = pe_three(psR[:, 0, at:at + E], high[:, k], low[:, k], WrH[:, :], WrL[:, :])
            i.then_inc(logits_ready, 1)

        def dve_logits(dve, g, c, start=False):
            at = chunk_logits(c, start)
            dve.wait_ge(logits_ready, QC if start else QC * g + c + 1)
            nc.vector.tensor_copy(lg[:, 4 * c:4 * c + 4, :].rearrange("p t e -> p (t e)"),
                                  psR[:, 0, at:at + 4 * E]).then_inc(logits_done, 1)

        def act_exp(act, g):
            act.wait_ge(shifted, g + 1)
            nc.scalar.activation(ex[:, :, :], lg[:, :, :], ACT.Exp).then_inc(exp_done, 1)

        def along(row):
            return over(red[:, row, :], 2, (P, GT, E))

        def token_major(t):
            return t.rearrange("p (e t) -> p t e", t=GT)

        def flat(t):
            return t[:, :, :].rearrange("p t e -> p (t e)")

        def dve_route(dve, g, step):
            count, upto = [LINKS_BEFORE[step]], LINKS_BEFORE[step + 1]

            def link(ins):
                count[0] += 1
                ins.then_inc(chain, 1)
                dve.wait_ge(chain, g * LINKS + count[0])

            if step == 0:
                dve.wait_ge(logits_done, QC * g + QC)
                link(nc.vector.tensor_reduce(red[:, 0, :], lg[:, :, :], AX.X, ALU.max))
                nc.vector.tensor_tensor(lg[:, :, :], lg[:, :, :], along(0), ALU.subtract).then_inc(shifted, 1)
            elif step == 1:
                dve.wait_ge(exp_done, g + 1)
                link(nc.vector.tensor_reduce(red[:, 1, :], ex[:, :, :], AX.X, ALU.add))
                link(nc.vector.reciprocal(red[:, 2, :], red[:, 1, :]))
                link(nc.vector.tensor_tensor(lg[:, :, :], ex[:, :, :], along(2), ALU.mult))
            elif 2 <= step < 7:
                other, mine = over(lg[:, :, :], 2, (P, GT, E, E)), over(lg[:, :, :], 3, (P, GT, E, E))
                higher = beats[:, :, :].rearrange("p (t e) j -> p t e j", e=E)
                equal = ties[:, :, :].rearrange("p (t e) j -> p t e j", e=E)
                if step == 2:
                    nc.vector.tensor_tensor(higher, other, mine, ALU.is_gt)
                elif step == 3:
                    link(nc.vector.tensor_tensor(equal, other, mine, ALU.is_equal))
                elif step == 4:
                    link(nc.vector.tensor_tensor(equal, equal, over(later[:, :, :], 1, (P, GT, E, E)), ALU.mult))
                elif step == 5:
                    link(nc.vector.tensor_tensor(beats[:, :, :], beats[:, :, :], ties[:, :, :], ALU.add))
                else:
                    link(nc.vector.tensor_reduce(flat(rank), beats[:, :, :], AX.X, ALU.add))
                    nc.vector.tensor_scalar(token_major(mask[:, :]), rank[:, :, :], 1.5, None, ALU.is_lt).then_inc(mask_done, 1)
                    count[0] += 1
                    dve.wait_ge(mask_done, g + 1)
                    dve.sem_inc(chain, 1)
            elif step == 7:
                for r, (pick, place) in enumerate(((pick1, 0.0), (pick2, 1.0))):
                    link(nc.vector.scalar_tensor_tensor(out=flat(pick), in0=flat(rank), scalar=place, in1=flat(lg),
                                                        op0=ALU.is_equal, op1=ALU.mult))
                    link(nc.vector.tensor_reduce(red[:, 3 + r, :], pick[:, :, :], AX.X, ALU.add))
                link(nc.vector.tensor_tensor(red[:, 5, :], red[:, 3, :], red[:, 4, :], ALU.add))
                link(nc.vector.tensor_scalar(red[:, 6, :], red[:, 5, :], FP32_EPS, None, ALU.add))
                link(nc.vector.reciprocal(red[:, 7, :], red[:, 6, :]))
                for r in (0, 1):
                    nc.vector.scalar_tensor_tensor(out=comb_all[:, cut(g * 2 * GT + r * GT, GT)], in0=red[:, 3 + r, :],
                                                   scalar=0.5, in1=red[:, 7, :], op0=ALU.mult, op1=ALU.mult)
            elif step == 8:
                dve.wait_ge(ranks_ready, g + 1)
                link(nc.vector.tensor_tensor_scan(out=upto_tile[:, :], data0=persist["restart"][:, :], data1=psR[:, 0, E * GT:2 * E * GT],
                                                  initial=0.0, op0=ALU.mult, op1=ALU.add))
                nc.vector.tensor_tensor(tiles_before[:, :], upto_tile[:, :], psR[:, 0, E * GT:2 * E * GT], ALU.subtract)
                link(nc.vector.tensor_scalar(ends[:, 0, :], upto_tile[:, GT - 1::GT], P / 2 - 0.5, 1.0 / P,
                                             ALU.add, ALU.mult))
                link(nc.vector.tensor_scalar(ends[:, 1, :], ends[:, 0, :], MAGIC, -MAGIC, ALU.add, ALU.add))
                link(nc.vector.tensor_tensor_scan(out=ends[:, 2, :], data0=persist["one8"][:, :], data1=ends[:, 1, :],
                                                  initial=0.0, op0=ALU.mult, op1=ALU.add))
            elif step == 9:
                link(nc.vector.tensor_tensor(ends[:, 3, :], ends[:, 2, :], ends[:, 1, :], ALU.subtract))
                link(nc.vector.tensor_scalar(ends[:, 4, :], ends[:, 3, :], float(P), gbase[:, 0:1], ALU.mult, ALU.add))
                link(nc.vector.tensor_tensor(slot[:, :, :], token_major(psR[:, 0, 0:E * GT]),
                                             over(ends[:, 4, :], 1, (P, GT, E)), ALU.add))
                link(nc.vector.tensor_tensor(slot[:, :, :], slot[:, :, :], token_major(tiles_before[:, :]), ALU.add))
                for r, (pick, place) in enumerate(((pick1, 0.0), (pick2, 1.0))):
                    i = nc.vector.scalar_tensor_tensor(out=flat(pick), in0=flat(rank), scalar=place, in1=flat(slot),
                                                       op0=ALU.is_equal, op1=ALU.mult)
                link(i)
                for r, pick in enumerate((pick1, pick2)):
                    i = nc.vector.tensor_reduce(posf[:, r * GT:r * GT + GT], pick[:, :, :], AX.X, ALU.add)
                link(i)
            elif step == 10:
                nc.vector.tensor_copy(sidx[:, :], posf[:, :]).then_inc(slots_done, 1)
                nc.vector.tensor_scalar(pos_all[:, cut(g * 2 * GT, 2 * GT)], posf[:, :], 1.0, None, ALU.mult)
                link(nc.vector.tensor_scalar(gbase[:, :], gbase[:, :], -1.0, float(NT * P), ALU.mult, ALU.add))
            else:
                link(nc.vector.tensor_tensor(past[:, :, :], jt[:, :, :], over(ends[0:1, 2, :], 1, (1, NT, E)), ALU.is_ge))
                link(nc.vector.tensor_reduce(pastn[:, :], past[:, :, :], AX.X, ALU.add))
                nc.vector.tensor_scalar(expert[:, cut(g * NT, NT)], pastn[:, :], float(E - 1), None,
                                        ALU.min).then_inc(experts_done, 1)
            assert count[0] == upto, (step, count[0], upto)

        def pe_ranks(pe, g):
            pe.wait_ge(mask_done, g + 1)
            nc.tensor.matmul(psR[:, 0, 0:E * GT], before[:, :], mask[:, :], start=True, stop=True)
            nc.tensor.matmul(psR[:, 0, E * GT:2 * E * GT], ones_r[:, :], mask[:, :], start=True, stop=True)\
                .then_inc(ranks_ready, 1)

        def pool_scatter(pool, g, start):
            pool.wait_ge(slots_done, g + 1)
            if not start:
                pool.wait_ge(scattered, g * 16 * IN_FLIGHT)
                pool.wait_ge(xsT, (g - 1) * NT + 1)
            pool.sem_inc(scatter_go, 1)
            for r in (0, 1):
                for t in range(GT):
                    k = r * GT + t
                    pool.indirect_dma_start(xsort, bass.IndirectOffsetOnAxis(ap=sidx[:, k:k + 1], axis=0),
                                            xn[:, t, :], None).then_inc(scattered, 16)

        def dve_gidx(dve, g):
            nc.vector.tensor_scalar(gidx[:, :], pos_all[:, cut(g * 2 * GT, 2 * GT)], 1.0, None,
                                    ALU.mult).then_inc(gidx_done, 1)

        def pool_gather(pool, g):
            pool.wait_ge(gidx_done, g + 1)
            for b in (0, 1):
                pool.wait_ge(y_stored[b], 16 * (PAIRS // 2) * (g + 1))
            pool.sem_inc(gather_go, 1)
            for t in range(GT):
                for r in (0, 1):
                    k = r * GT + t
                    pool.indirect_dma_start(yg[:, r, t, :], None, ysort,
                                            bass.IndirectOffsetOnAxis(ap=gidx[:, k:k + 1], axis=0))\
                        .then_inc(gathered[t // 4], 16)

        def dve_combine(dve, g, t):
            n, k, c = g * GT + t, cut(g * GT + t, 1), g * 2 * GT + t
            if t % 4 == 0:
                dve.wait_ge(gathered[t // 4], 16 * 8 * (g + 1))
            if t > 0:
                dve.wait_ge(x_done, n)
            nc.vector.scalar_tensor_tensor(out=xw[:, t % 2, :], in0=yg[:, 0, t, :], scalar=comb_all[:, cut(c, 1)],
                                           in1=X[:, k, :].rearrange("p t d -> p (t d)"),
                                           op0=ALU.mult, op1=ALU.add).then_inc(half_added, 1)
            if t > 0 and not finish:
                nc.vector.bn_stats(bst[:, t - 1, :], X[:, cut(n - 1, 1), :].rearrange("p t d -> p (t d)"))
            dve.wait_ge(half_added, n + 1)
            nc.vector.scalar_tensor_tensor(out=X[:, k, :].rearrange("p t d -> p (t d)"), in0=yg[:, 1, t, :],
                                           scalar=comb_all[:, cut(c + GT, 1)], in1=xw[:, t % 2, :],
                                           op0=ALU.mult, op1=ALU.add).then_inc(x_done, 1)

        def dve_stats(dve, g):
            dve.wait_ge(x_done, g * GT + GT)
            nc.vector.tensor_scalar(xw[:, 0:1, :], X[:, cut(g * GT + GT - 1, 1), :], 1.0, None, ALU.mult).then_inc(bst_done, 1)
            dve.wait_ge(bst_done, 2 * g + 1)
            nc.vector.bn_stats(bst[:, GT - 1, :], xw[:, 0, :]).then_inc(bst_done, 1)
            dve.wait_ge(bst_done, 2 * g + 2)
            nc.vector.tensor_copy(settled[:, :], bst[:, 0, 0:2])
            for t in range(GT):
                i = nc.vector.bn_aggr(mv[:, t, :], bst[:, t, :])
            i.then_inc(mv_done, 1)
            dve.wait_ge(mv_done, g + 1)
            nc.vector.tensor_scalar(stats[:, cut(g * GT, GT), :], mv[:, :, :], 1.0, None, ALU.mult)

        AT_CHUNK, AT_SOFTMAX, AT_RANKS = 2, 2 + 2 * QC, 2 + 2 * QC + 7
        AT_COMBINE = NT - GT - 2

        def pe_group(pe, g, first, last):
            e = {}
            if not first:
                e[-2], e[-1] = (pe_expert(pe, g - 1, j) for j in (NT - 2, NT - 1))
            for j in range(NT):
                if not (last and j == NT - 1):
                    if j < NT - 1:
                        pe_xsT(pe, g, j + 1)
                    else:
                        pe_xsT(pe, g + 1, 0)
                if j == 0:
                    pe.wait_ge(experts_done, g + 1)
                    e[0] = pe_expert(pe, g, 0)
                pe_up(pe, g, j, e[j], first)
                if j < NT - 1:
                    e[j + 1] = pe_expert(pe, g, j + 1)
                if j >= 1:
                    pe_hidT(pe, g, j - 1, first)
                elif not first:
                    pe_hidT(pe, g - 1, NT - 1, False)
                if j >= 2:
                    pe_down(pe, g, j - 2, e[j - 2], first)
                elif not first:
                    pe_down(pe, g - 1, NT - 2 + j, e[j - 2], False)
                if not last:
                    c = j - AT_CHUNK
                    if 0 <= c < 2 * QC:
                        (pe_normT(pe, g + 1, c // 2, False) if c % 2 == 0 else pe_logits(pe, g + 1, c // 2))
                    if j == AT_RANKS:
                        pe_ranks(pe, g + 1)

        def act_group(act, g, first, last):
            for j in range(NT):
                if j < NT - 1:
                    act_xsh(act, g, j + 1)
                elif not last:
                    act_xsh(act, g + 1, 0)
                act_relu(act, g, j, first)
                if j >= 1:
                    act_hh(act, g, j - 1, first)
                elif not first:
                    act_hh(act, g - 1, NT - 1, False)
                if j >= 2:
                    act_y(act, g, j - 2, first)
                elif not first:
                    act_y(act, g - 1, NT - 2 + j, False)
                if not last:
                    c = j - AT_CHUNK
                    if 0 <= c < 2 * QC and c % 2 == 0:
                        act_xTh(act, g + 1, c // 2)
                    if j == AT_SOFTMAX:
                        act_exp(act, g + 1)

        def dve_group(dve, g, first, last):
            for j in range(NT):
                if j < NT - 1:
                    dve_xsl(dve, g, j + 1)
                elif not last:
                    dve_xsl(dve, g + 1, 0)
                dve_hid(dve, g, j, first)
                if j >= 1:
                    dve_hl(dve, g, j - 1)
                elif not first:
                    dve_hl(dve, g - 1, NT - 1)
                if j >= 2:
                    dve_ysum(dve, g, j - 2)
                elif not first:
                    dve_ysum(dve, g - 1, NT - 2 + j)
                if not last:
                    c = j - AT_CHUNK
                    if j < QC:
                        dve_norm(dve, g + 1, j, False)
                    if 0 <= c < 2 * QC:
                        (dve_xTl(dve, g + 1, c // 2) if c % 2 == 0 else dve_logits(dve, g + 1, c // 2))
                    if AT_SOFTMAX <= j < AT_SOFTMAX + STEPS:
                        dve_route(dve, g + 1, j - AT_SOFTMAX)
                if not first:
                    if j == 0:
                        dve_gidx(dve, g - 1)
                    if 0 <= j - AT_COMBINE < GT:
                        dve_combine(dve, g - 1, j - AT_COMBINE)
                    if j == NT - 1 and not finish:
                        dve_stats(dve, g - 1)

        def pool_group(pool, g, first, last):
            if not first:
                pool_gather(pool, g - 1)
            if not last:
                pool_scatter(pool, g + 1, False)

        def sp_group(sp, g, first, last):
            for pair in range(PAIRS):
                if pair < PAIRS - AHEAD + 1:
                    sp_load(sp, g, pair + AHEAD - 1, first)
                elif not last:
                    sp_load(sp, g + 1, pair + AHEAD - 1 - PAIRS, False)
                if pair >= 1:
                    sp_store(sp, g, pair - 1)
                elif not first:
                    sp_store(sp, g - 1, PAIRS - 1)
            if finish and not first:
                sp_out(sp, g - 1)

        def sp_out(sp, g):
            sp.wait_ge(x_done, GT * (g + 1))
            sp.dma_start(persist["out"][:, cut(g * GT, GT), :], X[:, cut(g * GT, GT), :]).then_inc(out_done, 16)

        def over_groups(eng, body):
            body(eng, 0, True, False)
            with eng.Fori(1, GROUPS - 1) as g:
                body(eng, g, False, False)
            body(eng, GROUPS - 1, False, True)

        end = GROUPS - 1
        block = ctx.enter_context(nc.Block(tag + "block"))

        @block.sync
        def _(sp):
            sp_weights(sp)
            for pair in range(AHEAD - 1):
                sp_load(sp, 0, pair, True)
            sp.wait_ge(persist["cleared"][1], 16 * persist["FILLS"])
            over_groups(sp, sp_group)
            sp_store(sp, end, PAIRS - 1)
            for b in (0, 1):
                sp.wait_ge(y_stored[b], 16 * (PAIRS // 2) * GROUPS)
            if finish:
                for t in range(0, GT, 4):
                    n, first_t = end * GT + t + 4, end * GT + t
                    sp.wait_ge(x_done, n)
                    sp.dma_start(persist["out"][:, cut(first_t, 4), :], X[:, cut(first_t, 4), :]).then_inc(out_done, 16)
                sp.wait_ge(out_done, 16 * (GROUPS - 1 + GT // 4))

        @block.tensor
        def _(pe):
            for c in range(QC):
                pe_normT(pe, 0, c, True)
            for c in range(QC):
                pe_logits(pe, 0, c, True)
            pe_ranks(pe, 0)
            pe_xsT(pe, 0, 0)
            pe.wait_ge(w_low, WC)
            over_groups(pe, pe_group)
            pe_hidT(pe, end, NT - 1, False)
            for j in (NT - 2, NT - 1):
                pe_down(pe, end, j, pe_expert(pe, end, j), False)

        @block.scalar
        def _(act):
            for c in range(QC):
                act_xTh(act, 0, c, True)
            act_exp(act, 0)
            act_weights(act)
            act_xsh(act, 0, 0)
            over_groups(act, act_group)
            act_hh(act, end, NT - 1, False)
            for j in (NT - 2, NT - 1):
                act_y(act, end, j, False)

        @block.vector
        def _(dve):
            nc.vector.memset(gbase[:, :], 0.0)
            dve_norm(dve, 0, 0, True)
            for c in range(QC):
                if c < QC - 1:
                    dve_norm(dve, 0, c + 1, True)
                dve_xTl(dve, 0, c, True)
            for c in range(QC):
                dve_logits(dve, 0, c, True)
            for step in range(STEPS):
                dve_route(dve, 0, step)
            dve_weights(dve)
            dve_xsl(dve, 0, 0)
            over_groups(dve, dve_group)
            dve_hl(dve, end, NT - 1)
            for j in (NT - 2, NT - 1):
                dve_ysum(dve, end, j)
            dve_gidx(dve, end)
            for t in range(GT):
                dve_combine(dve, end, t)
            if not finish:
                dve_stats(dve, end)

        @block.gpsimd
        def _(pool):
            pool.wait_ge(persist["cleared"][0], 16 * persist["FILLS"])
            pool_scatter(pool, 0, True)
            if not finish:
                for rows in (xsort, ysort):
                    clear_rows(pool, persist, rows, 1, persist["cleared"][2])
            pool.wait_ge(persist["cleared"][2], 2 * 16 * persist["FILLS"])
            over_groups(pool, pool_group)
            pool_gather(pool, end)


def clear_rows(eng, persist, rows, half, signal):
    NT, ZC, D = persist["NT"], persist["ZC"], rows.shape[-1]
    part = rows[half * NT * P:(half + 1) * NT * P, :].rearrange("(p r) d -> p (r d)", p=P)
    for k in range(persist["FILLS"]):
        eng.dma_start(part[:, k * ZC:k * ZC + ZC], persist["zero"][:, :]).then_inc(signal, 16)


def moe_constants(nc, tag, persist, ins, T, D, E, F, first):
    X, stats = persist["X"], persist["stats"]
    TILES = T // P
    with ExitStack() as ctx:
        wr = ctx.enter_context(nc.sbuf_tensor(tag + "wr", [P, E], F32))
        bst = ctx.enter_context(nc.sbuf_tensor(tag + "bst0", [P, TILES, 6], F32))
        in_x = [ctx.enter_context(nc.semaphore(tag + f"in_x{k}")) for k in range(4)]
        in_wr = ctx.enter_context(nc.semaphore(tag + "in_wr"))
        high = ctx.enter_context(nc.semaphore(tag + "high"))
        bst_ready = ctx.enter_context(nc.semaphore(tag + "bst_ready"))
        made = ctx.enter_context(nc.semaphore(tag + "made"))
        tri = ctx.enter_context(nc.sbuf_tensor(tag + "tri", [P, P], F32))
        ones0 = ctx.enter_context(nc.sbuf_tensor(tag + "ones0", [P, P], F32))
        NT, GT = persist["NT"], persist["GT"]
        zeroed = ctx.enter_context(nc.semaphore(tag + "zeroed"))
        Q = TILES // 4
        block = ctx.enter_context(nc.Block(tag + "setup"))

        @block.sync
        def _(sp):
            sp.dma_start(wr[:, :], ins["WrT"]).then_inc(in_wr, 16)
            for k in range(4 if first else 0):
                sp.dma_start(X[:, k * Q:k * Q + Q, :], persist["x"][:, k * Q:k * Q + Q, :]).then_inc(in_x[k], 16)

        @block.gpsimd
        def _(pool):
            ident, later, jti = persist["ident"], persist["later"], persist["jti"]
            nc.gpsimd.iota(jti[:, :, :], pattern=[[1, NT], [0, E]], base=0, channel_multiplier=0).then_inc(made, 1)
            nc.gpsimd.memset(ident[:, :], 0.0)
            nc.gpsimd.memset(tri[:, :], 1.0)
            nc.gpsimd.memset(persist["one8"][:, :], 1.0)
            nc.gpsimd.memset(later[:, :, :], 1.0).then_inc(made, 1)
            pool.wait_ge(made, 2)
            nc.gpsimd.affine_select(out=ident[:, :], in_=ident[:, :], compare_op=ALU.not_equal, fill=1.0,
                                    base=0, pattern=[[-1, P]], channel_multiplier=1)
            nc.gpsimd.affine_select(out=tri[:, :], in_=tri[:, :], compare_op=ALU.is_gt, fill=0.0,
                                    base=0, pattern=[[1, P]], channel_multiplier=-1)
            nc.gpsimd.affine_select(out=later[:, :, :],
                                    in_=later[:, :, :],
                                    compare_op=ALU.is_gt, fill=0.0, base=0,
                                    pattern=[[1, E], [-1, E]], channel_multiplier=0).then_inc(made, 1)

        @block.scalar
        def _(act):
            if first:
                act.wait_ge(zeroed, 1)
                clear_rows(act, persist, persist["xsort"], 0, persist["cleared"][0])
                clear_rows(act, persist, persist["ysort"], 0, persist["cleared"][1])
            act.wait_ge(in_wr, 16)
            nc.scalar.activation(persist["WrH"][:, :], wr[:, :], ACT.Copy).then_inc(high, 1)
            act.wait_ge(made, 3)
            nc.scalar.activation(persist["before"][:, :], tri[:, :], ACT.Copy)

        @block.vector
        def _(dve):
            if first:
                nc.vector.memset(persist["zero"][:, :].bitcast(U32), 0).then_inc(zeroed, 1)
            nc.vector.memset(ones0[:, :], 1.0).then_inc(zeroed, 1)
            dve.wait_ge(zeroed, 2 if first else 1)
            nc.vector.tensor_copy(persist["ones_r"][:, :], ones0[:, :])
            nc.vector.tensor_copy(persist["restart"][:, :], ones0[:, 0:E * GT]).then_inc(zeroed, 1)
            dve.wait_ge(zeroed, 3 if first else 2)
            nc.vector.memset(persist["restart"][:, 0::GT], 0.0)
            dve.wait_ge(made, 1)
            nc.vector.tensor_copy(persist["jt"][:, :, :], persist["jti"][:, :, :])
            for k in range(4 if first else 0):
                dve.wait_ge(in_x[k], 16)
                for t in range(k * Q, k * Q + Q):
                    i = nc.vector.bn_stats(bst[:, t, :], X[:, t, :])
                i.then_inc(bst_ready, 1)
                dve.wait_ge(bst_ready, k + 1)
                for t in range(k * Q, k * Q + Q):
                    nc.vector.bn_aggr(stats[:, t, :], bst[:, t, :])
            dve.wait_ge(high, 1)
            nc.vector.tensor_tensor(persist["WrL"][:, :], wr[:, :], persist["WrH"][:, :].bitcast(F32), ALU.subtract)


def norm_phase(nc, tag, persist, T, inner):
    stats, rstd = persist["stats"], persist["rstd"]
    TILES = T // P
    with ExitStack() as ctx:
        v = ctx.enter_context(nc.sbuf_tensor(tag + "v", [P, TILES], F32))
        r = ctx.enter_context(nc.sbuf_tensor(tag + "r", [P, TILES], F32))
        q = ctx.enter_context(nc.sbuf_tensor(tag + "q", [P, TILES], F32))
        link = ctx.enter_context(nc.semaphore(tag + "link"))
        block = ctx.enter_context(nc.Block(tag + "norm"))
        LINKS = 6

        @block.scalar
        def _(act):
            for n in range(2 if inner else 1):
                act.wait_ge(link, n * LINKS + 1)
                nc.scalar.activation(r[:, :], v[:, :], ACT.Sqrt).then_inc(link, 1)

        @block.vector
        def _(dve):
            def root(n, out):
                dve.wait_ge(link, n * LINKS + 2)
                nc.vector.reciprocal(q[:, :], r[:, :]).then_inc(link, 1)
                dve.wait_ge(link, n * LINKS + 3)
                nc.vector.tensor_tensor(r[:, :], q[:, :], q[:, :], ALU.mult).then_inc(link, 1)
                dve.wait_ge(link, n * LINKS + 4)
                nc.vector.scalar_tensor_tensor(out=v[:, :], in0=v[:, :], scalar=-0.5, in1=r[:, :],
                                               op0=ALU.mult, op1=ALU.mult).then_inc(link, 1)
                dve.wait_ge(link, n * LINKS + 5)
                nc.vector.scalar_tensor_tensor(out=out, in0=v[:, :], scalar=1.5, in1=q[:, :],
                                               op0=ALU.add, op1=ALU.mult).then_inc(link, 1)
                dve.wait_ge(link, n * LINKS + 6)

            nc.vector.tensor_scalar(v[:, :], stats[:, :, 1], LN_EPS, None, ALU.add).then_inc(link, 1)
            root(0, rstd[:, :])
            if inner:
                squared = ctx.enter_context(nc.semaphore(tag + "squared"))
                nc.vector.tensor_tensor(q[:, :], rstd[:, :], rstd[:, :], ALU.mult).then_inc(squared, 1)
                dve.wait_ge(squared, 1)
                nc.vector.tensor_tensor(r[:, :], q[:, :], stats[:, :, 1], ALU.mult).then_inc(squared, 1)
                dve.wait_ge(squared, 2)
                nc.vector.tensor_scalar(v[:, :], r[:, :], FP32_EPS, None, ALU.add).then_inc(link, 1)
                root(1, persist["rmsin"][:, :])


def attention_constants(nc, persist, ins):
    A = persist["attn"]
    D = ins["mixA"].shape[0]
    with ExitStack() as ctx:
        raw = ctx.enter_context(nc.sbuf_tensor("aw_raw", [P, 4 * P], F32))
        woT = ctx.enter_context(nc.sbuf_tensor("aw_woT", [P, A["DH"]], F32))
        kone = ctx.enter_context(nc.sbuf_tensor("aw_kone", [P, A["K"].shape[-1]], F32))
        ps = ctx.enter_context(nc.psum_tensor("aw_ps", [P, 512], F32))
        loaded = ctx.enter_context(nc.semaphore("aw_loaded"))
        raw_in = ctx.enter_context(nc.semaphore("aw_raw_in"))
        cleared = ctx.enter_context(nc.semaphore("aw_cleared"))
        high = ctx.enter_context(nc.semaphore("aw_high"))
        folded = ctx.enter_context(nc.semaphore("aw_folded"))
        folding_in = ctx.enter_context(nc.semaphore("aw_folding_in"))
        lam_in = ctx.enter_context(nc.semaphore("aw_lam_in"))
        DH = A["DH"]
        block = ctx.enter_context(nc.Block("aw"))

        @block.sync
        def _(sp):
            sp.dma_start(raw[:, :], ins["wproj"]).then_inc(raw_in, 16)
            sp.dma_start(woT[:, :], ins["woT"]).then_inc(folding_in, 16)
            sp.dma_start(A["mixA"][:, :], ins["mixA"]).then_inc(folding_in, 16)
            sp.dma_start(A["lam"][:, :], ins["lambdas"]).then_inc(lam_in, 16)
            for n in ("w_out", "slam", "lm", "lmT", "expand"):
                sp.dma_start(A[n][:, :], ins[n]).then_inc(loaded, 16)
            sp.wait_ge(loaded, 16 * 13)

        @block.scalar
        def _(act):
            for n in ("mixB", "wv", "w1", "w2", "b2", "w_in", "compress", "publish"):
                act.dma_start(A[n][:, :], ins[n]).then_inc(loaded, 16)
            act.wait_ge(raw_in, 16)
            nc.scalar.activation(A["wpH"][:, :], raw[:, :], ACT.Copy).then_inc(high, 1)

        @block.gpsimd
        def _(pool):
            nc.gpsimd.memset(A["mpad"][:, :, :], 0.0)
            nc.gpsimd.memset(A["V1"][:, :, :, :], 1.0)
            nc.gpsimd.memset(A["half"][:, :], -0.5)
            nc.gpsimd.memset(A["ones"][:, :], 1.0)

        @block.vector
        def _(dve):
            nc.vector.memset(A["Wc"][:, :], 0.0)
            nc.vector.memset(kone[:, :], 1.0)
            nc.vector.memset(A["sgnQ"][:, :], 0.0)
            nc.vector.memset(A["sgnK"][:, :], 0.0).then_inc(cleared, 1)
            dve.wait_ge(cleared, 1)
            nc.vector.memset(A["sgnQ"][DH:2 * DH, :], -1.0)
            nc.vector.memset(A["sgnK"][2 * DH:3 * DH, :], -1.0)
            for m in (0, 1):
                c = m * (D + 1) + D
                nc.vector.memset(A["Wc"][64 * m + DH:64 * m + DH + 1, c:c + 1], 1.0)
            for q in (0, 1):
                for m in (0, 1):
                    nc.vector.tensor_copy(A["K"][96:97, q, m, :], kone[96:97, :])
            dve.wait_ge(high, 1)
            nc.vector.tensor_tensor(A["wpL"][:, :], raw[:, :], A["wpH"][:, :].bitcast(F32), ALU.subtract)
            dve.wait_ge(lam_in, 16)
            nc.vector.tensor_scalar(A["oml"][:, :], A["lam"][:, :], -1.0, 1.0, ALU.mult, ALU.add)
            dve.wait_ge(folded, 1)
            for m in (0, 1):
                nc.vector.tensor_copy(A["Wc"][64 * m:64 * m + DH, m * (D + 1):m * (D + 1) + D], ps[64 * m:64 * m + DH, 0:D])

        @block.tensor
        def _(pe):
            pe.wait_ge(folding_in, 16 * 2)
            for m in (0, 1):
                i = nc.tensor.matmul(ps[64 * m:64 * m + DH, 0:D], woT[:, :], A["mixA"][:, :], start=True, stop=True)
            i.then_inc(folded, 1)


def attention_phase(nc, persist, T, BATCH):
    A = persist["attn"]
    X, stats, rstd, ident = persist["X"], persist["stats"], persist["rstd"], persist["ident"]
    rmsin = persist["rmsin"]
    D, DH = 128, A["DH"]
    R = 3 * DH
    SEQ = T // BATCH
    TT = SEQ // P
    H = 512
    SC = float(DH) ** -0.5
    ARC = float(D) ** -0.5
    NL = A["lm"].shape[0]
    with ExitStack() as ctx:
        def sb(name, shape, dt=F32):
            return ctx.enter_context(nc.sbuf_tensor("at_" + name, shape, dt))

        def sem(name):
            return ctx.enter_context(nc.semaphore("at_" + name))

        Y = sb("Y", [P, TT, D])
        ysum = sb("ysum", [P, 2])
        ybus = sb("ybus", [P, 1])
        xn = sb("xn", [P, TT, D])
        xnT = sb("xnT", [P, SEQ])
        xnTh = sb("xnTh", [P, SEQ], F32R)
        xnTl = sb("xnTl", [P, SEQ], F32R)
        projh = sb("projh", [P, 2, H], F32R)
        rsum = sb("rsum", [P, 2])
        ema_in = sb("ema_in", [P, SEQ])
        ssmT = sb("ssmT", [P, SEQ])
        base = sb("base", [P, 2, TT, D])
        Ex = sb("Ex", [P, 2, 2 * H])
        CT = sb("CT", [P, 2, SEQ])
        O = sb("O", [P, TT, D])
        sq = sb("sq", [P, TT, D])
        col = sb("col", [P, 16])
        p3 = sb("p3", [P, 8])
        pl = sb("pl", [P, 2, 2])
        silb = sb("silb", [64, P])
        arow = sb("arow", [1, NL])
        arcn = sb("arcn", [1, 4])
        acol = sb("acol", [NL, 1])
        rec = sb("rec", [P, 2])
        coef = sb("coef", [P, TT, 2])
        ss = sb("ss", [P, TT])
        ms = sb("ms", [P, TT])
        rr = sb("rr", [P, TT])
        busc = sb("busc", [P, 4])
        yscale = sb("yscale", [P, 3, TT])
        pmax = sb("pmax", [P, 2 * TT, 2])
        pubb = sb("pubb", [P, P])
        bst = sb("bst", [P, TT, 6])
        mv = sb("mv", [P, TT, 2])
        psE = ctx.enter_context(nc.psum_tensor("at_psE", [P, 2, 2 * H], F32))
        psS = ctx.enter_context(nc.psum_tensor("at_psS", [P, 2, H], F32))
        psC = ctx.enter_context(nc.psum_tensor("at_psC", [P, H], F32))
        psM = ctx.enter_context(nc.psum_tensor("at_psM", [P, H], F32))

        yscale_done = sem("yscale_done")
        y_done, xn_done = sem("y_done"), sem("xn_done")
        act_go, pool_go = sem("act_go"), sem("pool_go")
        xT_ready, xT_done, xTh_done = sem("xT_ready"), sem("xT_done"), sem("xTh_done")
        xTl_done = sem("xTl_done")
        proj_ready, projh_done, proj_done = sem("proj_ready"), sem("projh_done"), sem("proj_done")
        v_ready, v_done = sem("v_ready"), sem("v_done")
        r1_ready, r1_exp, r1_done = sem("r1_ready"), sem("r1_exp"), sem("r1_done")
        r1_copied = sem("r1_copied")
        arc_max, arc_exp = sem("arc_max"), sem("arc_exp")
        r2_ready, r2_shift, r2_exp, r2_done = sem("r2_ready"), sem("r2_shift"), sem("r2_exp"), sem("r2_done")
        r3_ready, r3_done = sem("r3_ready"), sem("r3_done")
        rchain = sem("rchain")
        ema_scaled, ema_done = sem("ema_scaled"), sem("ema_done")
        p1_ready, p1_done = sem("p1_ready"), sem("p1_done")
        gmax_done = sem("gmax_done")
        row_ready, row_done = sem("row_ready"), sem("row_done")
        st_ready, ex_done, pv_done = sem("st_ready"), sem("ex_done"), sem("pv_done")
        ct_done = sem("ct_done")
        mix_ready = sem("mix_ready")
        base_ready, base_done = sem("base_ready"), sem("base_done")
        xr_done = sem("xr_done")
        mchain = sem("mchain")
        o_done, sq_done = sem("o_done"), sem("sq_done")
        ms_done, rr_done, o2_done = sem("ms_done"), sem("rr_done"), sem("o2_done")
        bus_ready, bus_done = sem("bus_ready"), sem("bus_done")
        xa_done, bst_done, mv_done = sem("xa_done"), sem("bst_done"), sem("mv_done")

        UNITS = 16
        KP = SEQ // P // 2
        CR = 64 + DH + 1
        RCH, MCH = 10, 3

        def group(g):
            return g % 2, g // 2

        def half(h):
            return slice(h * H, h * H + H)

        def tile_cols(t):
            return slice(t * P, t * P + P)

        def xtiles(b):
            return slice(b * TT, b * TT + TT) if isinstance(b, int) else bass.ds(b * TT, TT)

        def xtile(b, t):
            return slice(b * TT + t, b * TT + t + 1) if isinstance(b, int) else bass.ds(b * TT + t, 1)

        def pe_xT(pe, b, q, h, start):
            pe.wait_ge(xn_done, 2 * b + h + 1)
            if h == 0 and not start:
                pe.wait_ge(row_done, 4 * b)
                pe.wait_ge(p1_done, 2 * UNITS * b)
            for t in range(4):
                i = nc.tensor.transpose(psS[:, h, tile_cols(t)], xn[:, 4 * h + t, :], ident[:, :])
            i.then_inc(xT_ready, 1)

        def pe_proj(pe, b, k):
            w, h = k // 2, k % 2
            if k == 0:
                pe.wait_ge(xTl_done, 2 * b + 2)
            if k >= 2:
                pe.wait_ge(proj_done, 8 * b + k - 1)
            lo, hi = A["wpL"][:, w * P:w * P + P], A["wpH"][:, w * P:w * P + P]
            out = psS[:, h, :]
            nc.tensor.matmul(out, hi, xnTh[:, half(h)], start=True, stop=False)
            nc.tensor.matmul(out, lo, xnTh[:, half(h)], start=False, stop=False)
            nc.tensor.matmul(out, hi, xnTl[:, half(h)], start=False, stop=True).then_inc(proj_ready, 1)

        def pe_v_r1(pe, b, q):
            pe.wait_ge(proj_done, 8 * b + 8)
            for t in range(TT):
                i = nc.tensor.matmul(psS[:, 0, t * DH:t * DH + DH], xnT[:, tile_cols(t)], A["wv"][:, :],
                                     start=True, stop=True)
            i.then_inc(v_ready, 1)
            for h in (0, 1):
                nc.tensor.matmul(psS[0:64, 1, 0:1], A["w1"][:, :], rsum[:, h:h + 1], start=(h == 0), stop=(h == 1))
            for t in range(TT):
                nc.tensor.matmul(psS[:, 1, 32:33], Y[:, t, :], A["ones"][:, 0:1], start=(t == 0), stop=(t == TT - 1))
            nc.tensor.matmul(psS[0:1, 1, 64:64 + NL], xnT[:, SEQ - 1:SEQ], A["lmT"][:, :],
                             start=True, stop=True).then_inc(r1_ready, 1)

        def pe_r2(pe, b):
            pe.wait_ge(r1_done, b + 1)
            nc.tensor.matmul(psS[:, 1, 0:3], silb[:, :], A["w2"][:, :], start=True, stop=True)
            nc.tensor.matmul(psS[0:NL, 1, 8:9], arow[:, :], A["ones"][0:1, 0:1], start=True, stop=True).then_inc(r2_ready, 1)

        def pe_base(pe, b, h, after_bus):
            if h == 0:
                pe.wait_ge(r3_done, b + 1)
                if after_bus:
                    pe.wait_ge(xa_done, 2 * b - 2)
            else:
                pe.wait_ge(base_done, 2 * b + 1)
            for t in range(4):
                k = tile_cols(4 * h + t)
                nc.tensor.matmul(psM[:, tile_cols(t)], ssmT[:, k], A["mixA"][:, :], start=True, stop=False)
                i = nc.tensor.matmul(psM[:, tile_cols(t)], xnT[:, k], A["mixB"][:, :], start=False, stop=True)
            i.then_inc(base_ready, 1)

        def act_base(act, b, q, h):
            act.wait_ge(base_ready, 2 * b + h + 1)
            nc.scalar.activation(base[:, q, 4 * h:4 * h + 4, :].rearrange("p t d -> p (t d)"), psM[:, :],
                                 ACT.Copy).then_inc(base_done, 1)

        def pe_r3(pe, b):
            pe.wait_ge(r2_done, b + 1)
            nc.tensor.matmul(psS[:, 1, 16:17], A["lm"][:, :], acol[:, :], start=True, stop=True).then_inc(r3_ready, 1)

        def pe_p1(pe, b, q, v):
            m, t = v // TT, v % TT
            if v == 0:
                pe.wait_ge(v_done, b + 1)
                pe.wait_ge(r3_done, b + 1)
            for h in (0, 1):
                if v > 0:
                    pe.wait_ge(p1_done, 2 * (UNITS * b + v) + h - 1)
                nc.tensor.matmul(psS[:, h, :], A["Q"][0:R, q, m, tile_cols(t)], A["K"][0:R, q, m, half(h)],
                                 start=True, stop=True).then_inc(p1_ready, 1)

        def row_bank(g):
            return (psM[:, :], psS[:, 0, :], psM[:, :], psS[:, 1, :])[g]

        def pe_row(pe, b, g):
            m, h = g // 2, g % 2
            pe.wait_ge(gmax_done, 4 * b + g + 1)
            if g == 0:
                pe.wait_ge(base_done, 2 * b + 2)
            elif g == 2:
                pe.wait_ge(row_done, 4 * b + 1)
            else:
                pe.wait_ge(p1_done, 2 * UNITS * b + 2 * UNITS)
            for t in range(4):
                i = nc.tensor.transpose(row_bank(g)[0:R + 1, tile_cols(t)], A["mpad"][:, TT * m + 4 * h + t, :], ident[:, :])
            i.then_inc(row_ready, 1)

        def act_xT(act, b, q, h, start):
            act.wait_ge(xT_ready, 2 * b + h + 1)
            if h == 0 and not start:
                act.wait_ge(r1_ready, b)
                act.wait_ge(base_ready, 2 * b)
            nc.scalar.activation(xnT[:, half(h)], psS[:, h, :], ACT.Copy, scale=A["w_in"][:, 0:1],
                                 accum_out=rsum[:, h:h + 1]).then_inc(xT_done, 1)
            if h == 0 and not start:
                act.wait_ge(proj_ready, 8 * b)
            nc.scalar.activation(xnTh[:, half(h)], psS[:, h, :], ACT.Copy, scale=A["w_in"][:, 0:1]).then_inc(xTh_done, 1)

        def act_proj(act, b, k, start):
            act.wait_ge(proj_ready, 8 * b + k + 1)
            if not (start and k < 2):
                act.wait_ge(proj_done, 8 * b + k - 1)
            nc.scalar.activation(projh[0:R, k % 2, :], psS[0:R, k % 2, :], ACT.Copy).then_inc(projh_done, 1)

        def act_r1(act, b):
            act.wait_ge(r1_copied, b + 1)
            nc.scalar.activation(col[0:64, 0:1], col[0:64, 4:5], ACT.Exp, scale=-1.0 / SEQ).then_inc(r1_exp, 1)
            act.wait_ge(arc_max, b + 1)
            nc.scalar.activation(arow[:, :], arow[:, :], ACT.Exp, bias=arcn[:, 0:1], scale=ARC,
                                 accum_out=arcn[:, 1:2]).then_inc(arc_exp, 1)

        def act_r2(act, b):
            act.wait_ge(r2_shift, b + 1)
            nc.scalar.activation(p3[:, 0:3], p3[:, 0:3], ACT.Exp, accum_out=p3[:, 3:4]).then_inc(r2_exp, 1)

        def act_row(act, b, q, g):
            m, h = g // 2, g % 2
            act.wait_ge(row_ready, 4 * b + g + 1)
            nc.scalar.activation(A["Q"][R:R + 1, q, m, half(h)], row_bank(g)[R:R + 1, :], ACT.Copy).then_inc(row_done, 1)

        def dve_y(dve, b, start):
            if not start:
                dve.wait_ge(xn_done, 2 * b)
            nc.vector.tensor_scalar(yscale[:, 0, :], rstd[:, xtiles(b)], 1.0, None, ALU.mult)
            nc.vector.scalar_tensor_tensor(out=yscale[:, 1, :], in0=stats[:, xtiles(b), 0], scalar=-1.0,
                                           in1=rstd[:, xtiles(b)], op0=ALU.mult, op1=ALU.mult)
            nc.vector.tensor_scalar(yscale[:, 2, :], rmsin[:, xtiles(b)], 1.0, None, ALU.mult).then_inc(yscale_done, 1)

        def act_y(act, b, start):
            act.wait_ge(yscale_done, b + 1)
            if not start:
                act.wait_ge(r1_ready, b)
                act.wait_ge(xr_done, b)
            act.sem_inc(act_go, 1)
            for t in range(TT):
                i = nc.scalar.activation(Y[:, t:t + 1, :], X[:, xtile(b, t), :], ACT.Identity,
                                         scale=yscale[:, 0, t:t + 1], bias=yscale[:, 1, t:t + 1])
            i.then_inc(y_done, 1)

        def act_xn(act, b):
            act.wait_ge(y_done, b + 1)
            for t in range(TT):
                i = nc.scalar.activation(xn[:, t, :], Y[:, t, :], ACT.Copy, scale=yscale[:, 2, t:t + 1])
                if t % 4 == 3:
                    i.then_inc(xn_done, 1)

        def pool_xr(pool, b):
            pool.wait_ge(y_done, b + 1)
            pool.sem_inc(pool_go, 1)
            nc.gpsimd.tensor_tensor(X[:, xtiles(b), :], X[:, xtiles(b), :], Y[:, :, :], ALU.add).then_inc(xr_done, 1)

        def dve_xTl(dve, b, h):
            dve.wait_ge(xTh_done, 2 * b + h + 1)
            nc.vector.tensor_tensor(xnTl[:, half(h)], xnT[:, half(h)], xnTh[:, half(h)].bitcast(F32),
                                    ALU.subtract).then_inc(xTl_done, 1)

        def dve_proj(dve, b, q, k):
            w, h = k // 2, k % 2
            m, side = w // 2, ("Q", "K")[w % 2]
            dve.wait_ge(projh_done, 8 * b + k + 1)
            nc.vector.scalar_tensor_tensor(out=A[side][0:R, q, m, half(h)], in0=projh[0:R, k % 2, :].bitcast(F32),
                                           scalar=A["sgn" + side][0:R, :], in1=psS[0:R, h, :],
                                           op0=ALU.mult, op1=ALU.add).then_inc(proj_done, 1)

        def dve_v(dve, b, q):
            dve.wait_ge(v_ready, b + 1)
            nc.vector.tensor_copy(A["V1"][:, q, :, 0:DH],
                                  psS[:, 0, 0:TT * DH].rearrange("p (t c) -> p t c", c=DH)).then_inc(v_done, 1)

        def dve_ema(dve, b, start):
            dve.wait_ge(xT_done, 2 * b + 2)
            if not start:
                dve.wait_ge(base_ready, 2 * b)
            nc.vector.tensor_scalar(ema_in[:, :], xnT[:, :], A["oml"][:, :], None, ALU.mult).then_inc(ema_scaled, 1)
            dve.wait_ge(ema_scaled, b + 1)
            nc.vector.tensor_tensor_scan(out=ssmT[:, :], data0=A["lam"][:, 0:1].broadcast_to((P, SEQ)),
                                         data1=ema_in[:, :], initial=0.0, op0=ALU.mult, op1=ALU.add).then_inc(ema_done, 1)

        def dve_r1(dve, b, q):
            n = [RCH * b]

            def link(ins):
                n[0] = n[0] + 1
                ins.then_inc(rchain, 1)
                dve.wait_ge(rchain, n[0])

            dve.wait_ge(r1_ready, b + 1)
            nc.vector.tensor_copy(ysum[:, q:q + 1], psS[:, 1, 32:33])
            nc.vector.tensor_copy(col[0:64, 4:5], psS[0:64, 1, 0:1])
            nc.vector.tensor_copy(arow[:, :], psS[0:1, 1, 64:64 + NL]).then_inc(r1_copied, 1)
            dve.wait_ge(r1_copied, b + 1)
            link(nc.vector.tensor_reduce(arcn[:, 2:3], arow[:, :], AX.X, ALU.max))
            nc.vector.tensor_scalar(arcn[:, 0:1], arcn[:, 2:3], -ARC, None, ALU.mult).then_inc(arc_max, 1)
            dve.wait_ge(r1_exp, b + 1)
            link(nc.vector.tensor_scalar(col[0:64, 1:2], col[0:64, 0:1], 1.0, None, ALU.add))
            link(nc.vector.reciprocal(col[0:64, 2:3], col[0:64, 1:2]))
            link(nc.vector.scalar_tensor_tensor(out=col[0:64, 3:4], in0=col[0:64, 4:5], scalar=1.0 / SEQ,
                                                in1=col[0:64, 2:3], op0=ALU.mult, op1=ALU.mult))
            nc.vector.tensor_scalar(silb[:, :], A["ones"][0:64, :], col[0:64, 3:4], None, ALU.mult)
            dve.wait_ge(arc_exp, b + 1)
            link(nc.vector.reciprocal(arcn[:, 3:4], arcn[:, 1:2]))
            nc.vector.tensor_scalar(arow[:, :], arow[:, :], arcn[:, 3:4], None, ALU.mult).then_inc(r1_done, 1)

        def dve_r2(dve, b, q):
            n = [RCH * b + 5]

            def link(ins):
                n[0] = n[0] + 1
                ins.then_inc(rchain, 1)
                dve.wait_ge(rchain, n[0])

            dve.wait_ge(r2_ready, b + 1)
            nc.vector.tensor_copy(acol[:, :], psS[0:NL, 1, 8:9])
            link(nc.vector.tensor_tensor(p3[:, 0:3], psS[:, 1, 0:3], A["b2"][:, :], ALU.add))
            link(nc.vector.tensor_reduce(p3[:, 4:5], p3[:, 0:3], AX.X, ALU.max))
            nc.vector.tensor_scalar(p3[:, 0:3], p3[:, 0:3], p3[:, 4:5], None, ALU.subtract).then_inc(r2_shift, 1)
            dve.wait_ge(r2_exp, b + 1)
            link(nc.vector.reciprocal(p3[:, 5:6], p3[:, 3:4]))
            link(nc.vector.tensor_scalar(p3[:, 0:3], p3[:, 0:3], p3[:, 5:6], None, ALU.mult))
            link(nc.vector.tensor_tensor(pl[:, q, 0:1], p3[:, 1:2], p3[:, 2:3], ALU.add))
            nc.vector.scalar_tensor_tensor(out=pl[:, q, 1:2], in0=pl[:, q, 0:1], scalar=-1.0, in1=A["slam"][:, :],
                                           op0=ALU.mult, op1=ALU.mult).then_inc(r2_done, 1)

        def dve_r3(dve, b, q):
            dve.wait_ge(r3_ready, b + 1)
            dve.wait_ge(ema_done, b + 1)
            nc.vector.scalar_tensor_tensor(out=ssmT[:, SEQ - 1:SEQ], in0=psS[:, 1, 16:17], scalar=p3[:, 2:3],
                                           in1=ssmT[:, SEQ - 1:SEQ], op0=ALU.mult, op1=ALU.add).then_inc(r3_done, 1)

        def dve_p1(dve, b, v):
            n = 2 * (UNITS * b + v)
            for h in (0, 1):
                dve.wait_ge(p1_ready, n + h + 1)
                nc.vector.tensor_reduce(pmax[:, v, h:h + 1], psS[:, h, :], AX.X, ALU.max).then_inc(p1_done, 1)
            if v % 4 == 3:
                dve.wait_ge(p1_done, n + 2)
                nc.vector.tensor_reduce(A["mpad"][:, v - 3:v + 1, R:R + 1].rearrange("p v o -> p (v o)"),
                                        pmax[:, v - 3:v + 1, :], AX.X, ALU.max, negate=True).then_inc(gmax_done, 1)

        def pe_st(pe, b, q, u, start):
            m, h = group(u // KP)
            if u in (0, KP):
                pe.wait_ge(row_done, 4 * b + (1 if u == 0 else 4))
            if not (start and u < 2):
                pe.wait_ge(ex_done, UNITS * b + u - 1)
            for j in (0, 1):
                i = nc.tensor.matmul(psE[:, u % 2, j * H:j * H + H], A["K"][0:R + 1, q, m, tile_cols(2 * (u % KP) + j)],
                                     A["Q"][0:R + 1, q, m, half(h)], start=True, stop=True)
            i.then_inc(st_ready, 1)

        def act_ex(act, b, u, start):
            act.wait_ge(st_ready, UNITS * b + u + 1)
            if not (start and u < 2):
                act.wait_ge(pv_done, UNITS * b + u - 1)
            nc.scalar.activation(Ex[:, u % 2, :], psE[:, u % 2, :], ACT.Exp, scale=SC).then_inc(ex_done, 1)

        def pe_pv(pe, b, q, u, start):
            g, kp = u // KP, u % KP
            m, h = group(g)
            pe.wait_ge(ex_done, UNITS * b + u + 1)
            if kp == 0 and not (start and g < 2):
                pe.wait_ge(ct_done, 4 * b + g - 1)
            for j in (0, 1):
                i = nc.tensor.matmul(psC[64 * m:64 * m + DH + 1, :], A["V1"][:, q, 2 * kp + j, :], Ex[:, u % 2, j * H:j * H + H],
                                     start=(kp == 0 and j == 0), stop=(kp == KP - 1 and j == 1))
            i.then_inc(pv_done, 1)

        def dve_ct(dve, b, q, g):
            m, h = group(g)
            dve.wait_ge(pv_done, UNITS * b + KP * (g + 1))
            nc.vector.tensor_copy(CT[64 * m:64 * m + DH + 1, q, half(h)],
                                  psC[64 * m:64 * m + DH + 1, :]).then_inc(ct_done, 1)

        def pe_mix(pe, b, q, t, tail=False):
            if t == 0:
                pe.wait_ge(ct_done, 4 * b + 4)
                if not tail:
                    pe.wait_ge(row_done, 4 * b + 7)
            else:
                pe.wait_ge(o_done, TT * b + t)
            nc.tensor.matmul(psM[:, 0:2 * (D + 1)], CT[0:CR, q, tile_cols(t)], A["Wc"][0:CR, :],
                             start=True, stop=True).then_inc(mix_ready, 1)

        def act_sq(act, b, t):
            act.wait_ge(o_done, TT * b + t + 1)
            nc.scalar.activation(sq[:, t, :], O[:, t, :], ACT.Square, accum_out=ss[:, t:t + 1]).then_inc(sq_done, 1)

        def dve_mix(dve, b, q, t):
            n = (b * TT + t) * MCH
            dve.wait_ge(mix_ready, TT * b + t + 1)
            if t == 0:
                dve.wait_ge(base_done, 2 * b + 2)
                nc.vector.tensor_copy(ybus[:, :], ysum[:, q:q + 1])
            nc.vector.reciprocal(rec[:, :], psM[:, D:2 * D + 2:D + 1]).then_inc(mchain, 1)
            dve.wait_ge(mchain, n + 1)
            nc.vector.tensor_tensor(coef[:, t, :], rec[:, :], pl[:, q, :], ALU.mult).then_inc(mchain, 1)
            dve.wait_ge(mchain, n + 2)
            nc.vector.scalar_tensor_tensor(out=O[:, t, :], in0=psM[:, 0:D], scalar=coef[:, t, 0:1],
                                           in1=base[:, q, t, :], op0=ALU.mult, op1=ALU.add).then_inc(mchain, 1)
            dve.wait_ge(mchain, n + 3)
            nc.vector.scalar_tensor_tensor(out=O[:, t, :], in0=psM[:, D + 1:2 * D + 1], scalar=coef[:, t, 1:2],
                                           in1=O[:, t, :], op0=ALU.mult, op1=ALU.add).then_inc(o_done, 1)

        def dve_ms(dve, b):
            dve.wait_ge(sq_done, TT * b + TT)
            nc.vector.tensor_scalar(ms[:, :], ss[:, :], 1.0 / D, FP32_EPS, ALU.mult, ALU.add).then_inc(ms_done, 1)

        def pool_rr(pool, b):
            pool.wait_ge(ms_done, b + 1)
            nc.gpsimd.tensor_tensor(rr[:, :], ms[:, :], A["half"][:, :], ALU.pow).then_inc(rr_done, 1)

        def dve_o2(dve, b):
            dve.wait_ge(rr_done, b + 1)
            for t in range(TT):
                i = nc.vector.scalar_tensor_tensor(out=O[:, t, :], in0=O[:, t, :], scalar=rr[:, t:t + 1],
                                                   in1=A["w_out"][:, :], op0=ALU.mult, op1=ALU.mult)
            i.then_inc(o2_done, 1)

        def pe_bus(pe, b, k):
            if k == 0:
                pe.wait_ge(o2_done, b + 1)
                for t in range(TT):
                    i = nc.tensor.matmul(psM[:, 0:1], O[:, t, :], A["ones"][:, 0:1], start=(t == 0), stop=(t == TT - 1))
            else:
                pe.wait_ge(bus_done, 3 * b + k)
                if k == 1:
                    i = nc.tensor.matmul(psM[:, 0:1], A["compress"][:, :], busc[:, 0:1], start=True, stop=True)
                elif k == 2:
                    i = nc.tensor.matmul(psM[:, 0:1], A["publish"][:, :], busc[:, 1:2], start=True, stop=True)
                else:
                    i = nc.tensor.matmul(psM[:, 0:D], pubb[:, :], A["expand"][:, :], start=True, stop=True)
            i.then_inc(bus_ready, 1)

        def dve_bus(dve, b, k):
            dve.wait_ge(bus_ready, 4 * b + k + 1)
            if k == 0:
                i = nc.vector.tensor_scalar(busc[:, 0:1], psM[:, 0:1], ybus[:, :], 1.0 / SEQ, ALU.add, ALU.mult)
            elif k == 1:
                i = nc.vector.tensor_copy(busc[:, 1:2], psM[:, 0:1])
            else:
                i = nc.vector.tensor_scalar(pubb[:, :], A["ones"][:, :], psM[:, 0:1], 0.1, ALU.mult, ALU.mult)
            i.then_inc(bus_done, 1)

        def pool_x(pool, b):
            pool.wait_ge(xr_done, b + 1)
            pool.wait_ge(bus_ready, 4 * b + 1)
            pool.sem_inc(pool_go, 1)
            nc.gpsimd.tensor_tensor(O[:, :, :], X[:, xtiles(b), :], O[:, :, :], ALU.add).then_inc(xa_done, 1)

        def dve_x(dve, b, piece):
            k = xtiles(b)
            if piece == 1:
                dve.wait_ge(xa_done, 2 * b + 1)
                dve.wait_ge(bus_ready, 4 * b + 4)
                nc.vector.tensor_tensor(O[:, :, :], O[:, :, :], psM[:, 0:D].unsqueeze(1).broadcast_to((P, TT, D)),
                                        ALU.add).then_inc(xa_done, 1)
            elif piece == 2:
                dve.wait_ge(xa_done, 2 * b + 2)
                for t in range(TT):
                    i = nc.vector.bn_stats(bst[:, t, :], O[:, t, :])
                i.then_inc(bst_done, 1)
            else:
                dve.wait_ge(bst_done, b + 1)
                nc.vector.tensor_scalar(X[:, k, :], O[:, :, :], 1.0, None, ALU.mult)
                for t in range(TT):
                    i = nc.vector.bn_aggr(mv[:, t, :], bst[:, t, :])
                i.then_inc(mv_done, 1)
                dve.wait_ge(mv_done, b + 1)
                nc.vector.tensor_scalar(stats[:, k, :], mv[:, :, :], 1.0, None, ALU.mult)

        def pe_turn(pe, b, q, first, last):
            for u in range(UNITS):
                pe_st(pe, b, q, u, first)
                if not last and u >= 9:
                    pe_p1(pe, b + 1, 1 - q, 2 * u - 16)
                if u >= 1:
                    pe_pv(pe, b, q, u - 1, first)
                if not first:
                    if u < TT:
                        pe_mix(pe, b - 1, 1 - q, u)
                    if 10 <= u < 14:
                        pe_bus(pe, b - 1, u - 10)
                if not last:
                    if u in (0, 1):
                        pe_xT(pe, b + 1, 1 - q, u, False)
                    if u in (2, 3, 4, 5):
                        pe_proj(pe, b + 1, 2 * u - 4)
                        pe_proj(pe, b + 1, 2 * u - 3)
                    if u == 6:
                        pe_v_r1(pe, b + 1, 1 - q)
                    if u == 7:
                        pe_r2(pe, b + 1)
                    if u == 8:
                        pe_r3(pe, b + 1)
                    if u in (14, 15):
                        pe_base(pe, b + 1, u - 14, not first)
                    if u == 8:
                        pe_p1(pe, b + 1, 1 - q, 0)
                    if u >= 8:
                        pe_p1(pe, b + 1, 1 - q, 2 * u - 15)
                    if u == 15:
                        pe_row(pe, b + 1, 0)
                        pe_row(pe, b + 1, 1)
            pe_pv(pe, b, q, UNITS - 1, first)
            if not last:
                for g in (2, 3):
                    pe_row(pe, b + 1, g)

        def act_turn(act, b, q, first, last):
            for u in range(UNITS):
                act_ex(act, b, u, first)
                if not last and not no_next(b):
                    if u == 10:
                        act_y(act, b + 2, False)
                    if u == 11:
                        act_xn(act, b + 2)
                if not first and 1 <= u <= TT:
                    act_sq(act, b - 1, u - 1)
                if not last:
                    if u in (0, 1):
                        act_xT(act, b + 1, 1 - q, u, False)
                    if u in (2, 3, 4, 5):
                        act_proj(act, b + 1, 2 * u - 4, False)
                        act_proj(act, b + 1, 2 * u - 3, False)
                    if u == 6:
                        act_r1(act, b + 1)
                    if u == 7:
                        act_r2(act, b + 1)
                    if u in (14, 15):
                        act_base(act, b + 1, 1 - q, u - 14)
                    if u == 15:
                        act_row(act, b + 1, 1 - q, 0)
                        act_row(act, b + 1, 1 - q, 1)
            if not last:
                for g in (2, 3):
                    act_row(act, b + 1, 1 - q, g)

        def no_next(b):
            return isinstance(b, int) and b == BATCH - 2

        def dve_turn(dve, b, q, first, last):
            for u in range(UNITS):
                if u >= KP and u % KP == 1:
                    dve_ct(dve, b, q, u // KP - 1)
                if not first and u < TT:
                    dve_mix(dve, b - 1, 1 - q, u)
                if not last:
                    if u in (0, 1):
                        dve_xTl(dve, b + 1, u)
                    if u in (2, 3, 4, 5):
                        dve_proj(dve, b + 1, 1 - q, 2 * u - 4)
                        dve_proj(dve, b + 1, 1 - q, 2 * u - 3)
                    if u == 5:
                        dve_ema(dve, b + 1, False)
                    if u == 6:
                        dve_v(dve, b + 1, 1 - q)
                        dve_r1(dve, b + 1, 1 - q)
                    if u == 7:
                        dve_r2(dve, b + 1, 1 - q)
                    if u == 8:
                        dve_r3(dve, b + 1, 1 - q)
                if not first:
                    if u == 8:
                        dve_ms(dve, b - 1)
                    if u == 14:
                        dve_x(dve, b - 1, 1)
                if not last and u >= 8:
                    dve_p1(dve, b + 1, 2 * u - 16)
                if not first:
                    if 10 <= u < 13:
                        dve_bus(dve, b - 1, u - 10)
                    if u in (14, 15):
                        dve_x(dve, b - 1, {14: 2, 15: 3}[u])
                if not last and u == 9 and not no_next(b):
                    dve_y(dve, b + 2, False)
                if not last and u >= 8:
                    dve_p1(dve, b + 1, 2 * u - 15)
                if not first and u == 8:
                    dve_o2(dve, b - 1)
            dve_ct(dve, b, q, 3)

        def pool_turn(pool, b, q, first, last):
            if not first:
                pool_rr(pool, b - 1)
                pool_x(pool, b - 1)
            if not last and not no_next(b):
                pool_xr(pool, b + 2)

        def over_batches(eng, turn):
            turn(eng, 0, 0, True, False)
            turn(eng, 1, 1, False, False)
            with eng.Fori(2, BATCH - 2, 2) as b:
                b = b.with_bounds(min_val=2, max_val=BATCH - 4)
                turn(eng, b, 0, False, False)
                turn(eng, b + 1, 1, False, False)
            turn(eng, BATCH - 2, 0, False, False)
            turn(eng, BATCH - 1, 1, False, True)

        end, eq = BATCH - 1, (BATCH - 1) % 2
        block = ctx.enter_context(nc.Block("at_block"))

        @block.tensor
        def _(pe):
            for h in (0, 1):
                pe_xT(pe, 0, 0, h, True)
            for k in range(8):
                pe_proj(pe, 0, k)
            pe_v_r1(pe, 0, 0)
            pe_r2(pe, 0)
            pe_r3(pe, 0)
            for v in range(UNITS):
                pe_p1(pe, 0, 0, v)
            for h in (0, 1):
                pe_base(pe, 0, h, False)
            for g in range(4):
                pe_row(pe, 0, g)
            over_batches(pe, pe_turn)
            for t in range(TT):
                pe_mix(pe, end, eq, t, True)
            for k in range(4):
                pe_bus(pe, end, k)

        @block.scalar
        def _(act):
            act_y(act, 0, True)
            act_xn(act, 0)
            for h in (0, 1):
                act_xT(act, 0, 0, h, True)
            for k in range(8):
                act_proj(act, 0, k, True)
            act_r1(act, 0)
            act_r2(act, 0)
            for h in (0, 1):
                act_base(act, 0, 0, h)
            for g in range(4):
                act_row(act, 0, 0, g)
            act_y(act, 1, False)
            act_xn(act, 1)
            over_batches(act, act_turn)
            for t in range(TT):
                act_sq(act, end, t)

        @block.vector
        def _(dve):
            nc.vector.memset(CT[:, :, :].bitcast(mybir.dt.uint32), 0)
            dve_y(dve, 0, True)
            for h in (0, 1):
                dve_xTl(dve, 0, h)
            for k in range(8):
                dve_proj(dve, 0, 0, k)
            dve_ema(dve, 0, True)
            dve_v(dve, 0, 0)
            dve_r1(dve, 0, 0)
            dve_r2(dve, 0, 0)
            dve_r3(dve, 0, 0)
            for v in range(UNITS):
                dve_p1(dve, 0, v)
            dve_y(dve, 1, False)
            over_batches(dve, dve_turn)
            for t in range(TT):
                dve_mix(dve, end, eq, t)
            dve_ms(dve, end)
            dve_o2(dve, end)
            for k in range(3):
                dve_bus(dve, end, k)
            for piece in (1, 2, 3):
                dve_x(dve, end, piece)

        @block.gpsimd
        def _(pool):
            pool_xr(pool, 0)
            pool_xr(pool, 1)
            over_batches(pool, pool_turn)
            pool_rr(pool, end)
            pool_x(pool, end)


def program(nc, ins, out):
    T, D = ins["x"].shape
    E = ins["WrT"].shape[1]
    F = ins["WgT"].shape[1] // E
    BATCH = ins["batches"]
    DH = ins["wv"].shape[1]
    TILES = T // P
    SEQ = T // BATCH
    with ExitStack() as ctx:
        def sb(name, shape, dt=F32, where=None):
            return (where or ctx).enter_context(nc.sbuf_tensor(name, shape, dt))

        persist = {
            "X": sb("X", [P, TILES, D]),
            "stats": sb("stats", [P, TILES, 2]),
            "rstd": sb("rstd", [P, TILES]),
            "rmsin": sb("rmsin", [P, TILES]),
            "ident": sb("ident", [P, P]),
            "x": ins["x"].rearrange("(t p) d -> p t d", p=P),
            "out": out.rearrange("(t p) d -> p t d", p=P),
        }

        GROUPS = 4
        GT = TILES // GROUPS
        NT = 2 * GT + E - 1
        NT += NT % 2
        NT += 2 * (NT // 2 % 2)
        slots = 2 * NT * P
        persist["GROUPS"], persist["GT"], persist["NT"], persist["ZC"] = GROUPS, GT, NT, 640
        persist["xsort"] = nc.dram_tensor("xsort", (slots, D), F32, kind="Internal").ap()
        persist["ysort"] = nc.dram_tensor("ysort", (slots, D), F32, kind="Internal").ap()
        persist["zero"] = sb("zero", [P, persist["ZC"]])
        persist["cleared"] = [ctx.enter_context(nc.semaphore(f"cleared{k}")) for k in range(3)]
        persist["FILLS"] = NT * D // persist["ZC"]

        def moe(tag, first):
            with ExitStack() as here:
                for n in ("WgH", "WgL", "WuH", "WuL"):
                    persist[n] = sb(tag + n, [P, E * F], F32R, here)
                persist["Wd"] = sb(tag + "Wd", [P, 2 * E * F], F32R, here)
                persist["WrH"], persist["WrL"] = (sb(tag + n, [P, E], F32R, here) for n in ("WrH", "WrL"))
                persist["before"], persist["ones_r"] = (sb(tag + n, [P, P], F32R, here) for n in ("before", "ones_r"))
                persist["later"] = sb(tag + "later", [P, E, E], F32, here)
                persist["one8"] = sb(tag + "one8", [P, E], F32, here)
                persist["restart"] = sb(tag + "restart", [P, E * GT], F32, here)
                persist["jt"] = sb(tag + "jt", [1, NT, E], F32, here)
                persist["jti"] = sb(tag + "jti", [1, NT, E], mybir.dt.int32, here)
                persist["weights"] = [ins[n] for n in ("WgT", "WuT", "WdT")]
                moe_constants(nc, tag, persist, ins, T, D, E, F, first)
                norm_phase(nc, tag, persist, T, False)
                with nc.cleanup_on_exit():
                    ffn_phase(nc, tag, persist, T, D, E, F, not first)

        moe("ffn1_", True)
        with ExitStack() as here:
            A = {"DH": DH}
            for n in ("mixA", "mixB", "wv", "w1", "w2", "b2", "w_in", "w_out", "slam", "lm", "lmT", "compress",
                      "publish", "expand", "lambdas"):
                A["lam" if n == "lambdas" else n] = sb("a_" + n, list(ins[n].shape), F32, here)
            A["wpH"], A["wpL"] = (sb("a_" + n, [P, 4 * P], F32R, here) for n in ("wpH", "wpL"))
            A["mpad"] = sb("a_mpad", [P, 2 * SEQ // P, 3 * DH + 1], F32, here)
            A["V1"] = sb("a_V1", [P, 2, SEQ // P, DH + 1], F32, here)
            A["half"] = sb("a_half", [P, SEQ // P], F32, here)
            A["ones"] = sb("a_ones", [P, P], F32, here)
            A["Wc"] = sb("a_Wc", [P, 2 * (D + 1)], F32, here)
            A["sgnQ"], A["sgnK"], A["oml"] = (sb("a_" + n, [P, 1], F32, here) for n in ("sgnQ", "sgnK", "oml"))
            A["Q"], A["K"] = (sb("a_" + n, [P, 2, 2, SEQ], F32R, here) for n in ("Q", "K"))
            persist["attn"] = A
            attention_constants(nc, persist, ins)
            norm_phase(nc, "at_", persist, T, True)
            attention_phase(nc, persist, T, BATCH)
        moe("ffn2_", False)


def kernel(**inputs):
    import numpy as np
    import concourse.bacc as bacc
    from concourse import mybir as mb
    from concourse.bass_utils import run_bass_kernel_spmd as run

    nc = bacc.Bacc("TRN2", target_bir_lowering=False, num_devices=1)
    g = {k: np.asarray(v) for k, v in inputs.items()}
    E, F, D = g["L0_ffn_Wg"].shape
    B, S, _ = g["L0_attn_x"].shape

    def rows(a):
        return np.broadcast_to(a, (128, a.size))

    arrays = {
        "x": g["L0_attn_x"].reshape(B * S, D),
        "WrT": g["L0_ffn_Wr"].T,
        "WgT": g["L0_ffn_Wg"].transpose(2, 0, 1).reshape(D, E * F),
        "WuT": g["L0_ffn_Wu"].transpose(2, 0, 1).reshape(D, E * F),
        "WdT": g["L0_ffn_Wd"].reshape(E, D, F // 128, 128).transpose(3, 0, 2, 1).reshape(128, E * F // 128 * D),
        "wproj": np.concatenate([np.tile(g["L0_attn_slr_" + n], (1, 4)) for n in ("wq1", "wk1", "wq2", "wk2")], axis=1),
        "woT": g["L0_attn_slr_wo"].T,
        "mixA": g["L0_attn_mix_w"][:D],
        "mixB": g["L0_attn_mix_w"][D:],
        "wv": g["L0_attn_slr_wv"],
        "w1": g["L0_attn_router_w1"],
        "w2": g["L0_attn_router_w2"],
        "b2": rows(g["L0_attn_router_b2"]),
        "w_in": g["L0_attn_w_norm_in"].reshape(D, 1),
        "w_out": rows(g["L0_attn_w_norm_out"]),
        "slam": rows(g["L0_attn_slr_lam"].reshape(1)),
        "lambdas": np.repeat(g["L0_attn_lambdas"], D // g["L0_attn_lambdas"].size).reshape(D, 1),
        "lm": g["L0_attn_landmarks"],
        "lmT": g["L0_attn_landmarks"].T,
        "compress": g["L0_attn_bus_compress"],
        "publish": g["L0_attn_bus_publish"],
        "expand": g["L0_attn_bus_expand"],
    }
    arrays = {k: np.ascontiguousarray(v) for k, v in arrays.items()}
    ins = {k: nc.dram_tensor("in_" + k, v.shape, mb.dt.from_np(v.dtype), kind="ExternalInput").ap() for k, v in arrays.items()}
    ins["batches"] = B
    out = nc.dram_tensor("out", (B * S, D), mb.dt.float32, kind="ExternalOutput").ap()
    program(nc, ins, out)
    r = run(nc, [{"in_" + k: v for k, v in arrays.items()}], core_ids=[0])
    return r.results[0]["out"].reshape(B, S, D)
```
